# Optimizing a Trainium2 kernel written in Bass

```python
import numpy as np
import jax
import jax.numpy as jnp

def _softmax(x, axis=-1):
    return jax.nn.softmax(x, axis=axis)

def _gelu(x):
    return jax.nn.gelu(x, approximate=True)

def _silu(x):
    return jax.nn.silu(x)

def _sigmoid(x):
    return jax.nn.sigmoid(x)

def _layernorm(x, axis=-1, eps=1e-05):
    m = jnp.mean(x, axis=axis, keepdims=True)
    v = jnp.var(x, axis=axis, keepdims=True)
    return (x - m) / jnp.sqrt(v + eps)

def _scatter_add(tgt, idx, src, axis=0):
    return tgt.at[idx].add(src)

def _segment_sum(src, seg, n):
    return jax.ops.segment_sum(src, seg, n)
kernel_name = 'mk_adaln_d1_jaxref_r4_376f7b'

def setup_inputs(seed: int=0):
    np.random.seed(seed)
    _w = jnp.asarray

    def _L0_attn_setup():
        import jax, jax.numpy as jnp
        import numpy as np
        import math
        B, S, D_MODEL = (4, 512, 512)
        N_HEADS, D_HEAD = (16, 128)
        NEG = -100000.0
        key = jax.random.key(seed)
        ks = jax.random.split(key, 9)
        std_qkv = math.sqrt(2.0 / (D_MODEL * D_HEAD + N_HEADS * D_HEAD))
        x = jax.random.normal(ks[0], (B, S, D_MODEL), dtype=jnp.float32)
        Q_w = jax.random.normal(ks[1], (N_HEADS, D_MODEL, D_HEAD), dtype=jnp.float32) * std_qkv
        K_w = jax.random.normal(ks[2], (N_HEADS, D_MODEL, D_HEAD), dtype=jnp.float32) * std_qkv
        V_w = jax.random.normal(ks[3], (N_HEADS, D_MODEL, D_HEAD), dtype=jnp.float32) * std_qkv
        std_o = math.sqrt(2.0 / (N_HEADS * D_HEAD + D_MODEL))
        O_w = jax.random.normal(ks[4], (N_HEADS, D_HEAD, D_MODEL), dtype=jnp.float32) * std_o
        Q_b = jax.random.normal(ks[5], (N_HEADS, D_HEAD), dtype=jnp.float32) * 0.02
        K_b = jax.random.normal(ks[6], (N_HEADS, D_HEAD), dtype=jnp.float32) * 0.02
        V_b = jax.random.normal(ks[7], (N_HEADS, D_HEAD), dtype=jnp.float32) * 0.02
        O_b = jax.random.normal(ks[8], (D_MODEL,), dtype=jnp.float32) * 0.02
        return {'x': x, 'Q_w': Q_w, 'Q_b': Q_b, 'K_w': K_w, 'K_b': K_b, 'V_w': V_w, 'V_b': V_b, 'O_w': O_w, 'O_b': O_b}
    _L0_attn_in = _L0_attn_setup()

    def _L0_ffn_setup():
        import jax, jax.numpy as jnp
        import numpy as np
        B, T, D = (2, 256, 512)
        E, K, H = (64, 4, 128)
        S, HS = (2, H * K)
        CAP = 128
        key = jax.random.key(seed)
        ks = jax.random.split(key, 9)
        scale = 0.02
        return {'x': jax.random.normal(ks[0], (B, T, D), jnp.float32), 'Wr': jax.random.normal(ks[1], (D, E), jnp.float32) * scale, 'router_bias': jnp.zeros((E,), jnp.float32), 'Wg': jax.random.normal(ks[2], (E, D, H), jnp.float32) * scale, 'Wu': jax.random.normal(ks[3], (E, D, H), jnp.float32) * scale, 'Wd': jax.random.normal(ks[4], (E, H, D), jnp.float32) * scale, 'Sg': jax.random.normal(ks[5], (S, D, HS), jnp.float32) * scale, 'Su': jax.random.normal(ks[6], (S, D, HS), jnp.float32) * scale, 'Sd': jax.random.normal(ks[7], (S, HS, D), jnp.float32) * scale}
    _L0_ffn_in = _L0_ffn_setup()
    _L0_c = _w((lambda *s: np.random.randn(*s).astype(np.float32) * 0.05)(1, 512))
    _L0_wmod = _w((lambda *s: np.random.randn(*s).astype(np.float32) * 0.05)(512, 6 * 512) * 512 ** (-0.5))
    _d = {'L0_attn_x': _L0_attn_in['x'], 'L0_attn_Q_w': _L0_attn_in['Q_w'], 'L0_attn_Q_b': _L0_attn_in['Q_b'], 'L0_attn_K_w': _L0_attn_in['K_w'], 'L0_attn_K_b': _L0_attn_in['K_b'], 'L0_attn_V_w': _L0_attn_in['V_w'], 'L0_attn_V_b': _L0_attn_in['V_b'], 'L0_attn_O_w': _L0_attn_in['O_w'], 'L0_attn_O_b': _L0_attn_in['O_b'], 'L0_ffn_Wr': _L0_ffn_in['Wr'], 'L0_ffn_router_bias': _L0_ffn_in['router_bias'], 'L0_ffn_Wg': _L0_ffn_in['Wg'], 'L0_ffn_Wu': _L0_ffn_in['Wu'], 'L0_ffn_Wd': _L0_ffn_in['Wd'], 'L0_ffn_Sg': _L0_ffn_in['Sg'], 'L0_ffn_Su': _L0_ffn_in['Su'], 'L0_ffn_Sd': _L0_ffn_in['Sd'], 'L0_c': _L0_c, 'L0_wmod': _L0_wmod}
    _x0 = _d['L0_attn_x']
    _d['L0_attn_x'] = jax.random.normal(jax.random.fold_in(jax.random.key(seed), 1), (1, 2048, 512), dtype=_x0.dtype)
    del _x0
    return _d

def reference(L0_attn_x, L0_attn_Q_w, L0_attn_Q_b, L0_attn_K_w, L0_attn_K_b, L0_attn_V_w, L0_attn_V_b, L0_attn_O_w, L0_attn_O_b, L0_ffn_Wr, L0_ffn_router_bias, L0_ffn_Wg, L0_ffn_Wu, L0_ffn_Wd, L0_ffn_Sg, L0_ffn_Su, L0_ffn_Sd, L0_c, L0_wmod):

    def _L0_attn_ref(x, Q_w, Q_b, K_w, K_b, V_w, V_b, O_w, O_b):
        import jax, jax.numpy as jnp
        import numpy as np
        import math
        B, S, D_MODEL = (4, 512, 512)
        N_HEADS, D_HEAD = (16, 128)
        NEG = -100000.0
        d_head = Q_w.shape[-1]
        q = jnp.einsum('bpm,hmd->bphd', x, Q_w) + Q_b
        k = jnp.einsum('bpm,hmd->bphd', x, K_w) + K_b
        v = jnp.einsum('bpm,hmd->bphd', x, V_w) + V_b
        logits = jnp.einsum('bqhd,bkhd->bhqk', q, k) / math.sqrt(d_head)
        s = x.shape[1]
        causal_mask = jnp.triu(jnp.ones((s, s), dtype=bool), k=1)
        logits = jnp.where(causal_mask, NEG, logits)
        scores = jax.nn.softmax(logits, axis=-1)
        attn = jnp.einsum('bhqk,bkhd->bqhd', scores, v)
        out = jnp.einsum('bqhd,hdm->bqm', attn, O_w) + O_b
        return out

    def _L0_ffn_ref(x, Wr, router_bias, Wg, Wu, Wd, Sg, Su, Sd):
        import jax, jax.numpy as jnp
        import numpy as np
        B, T, D = (2, 256, 512)
        E, K, H = (64, 4, 128)
        S, HS = (2, H * K)
        CAP = 128
        Bx, Tx, Dx = x.shape
        N = Bx * Tx
        flat = x.reshape(N, Dx)
        logits = flat @ Wr + router_bias
        scores = jax.nn.softmax(logits, axis=-1)
        topk_scores, topk_idx = jax.lax.top_k(scores, K)
        topk_scores = topk_scores / topk_scores.sum(-1, keepdims=True)
        eid = topk_idx.reshape(-1)
        w = topk_scores.reshape(-1)
        tok = jnp.repeat(jnp.arange(N), K)
        oh = jax.nn.one_hot(eid, E, dtype=jnp.int32)
        pos = (jnp.cumsum(oh, axis=0) * oh).sum(-1) - 1
        valid = pos < CAP
        xb = jnp.zeros((E, CAP, Dx), x.dtype).at[eid, pos].set(flat[tok], mode='drop')
        h = jax.nn.silu(jnp.einsum('ecd,edh->ech', xb, Wg)) * jnp.einsum('ecd,edh->ech', xb, Wu)
        yb = jnp.einsum('ech,ehd->ecd', h, Wd)
        y = yb[eid, jnp.minimum(pos, CAP - 1)] * (w * valid)[:, None]
        out = jnp.zeros((N, Dx), x.dtype).at[tok].add(y)
        hs = jax.nn.silu(jnp.einsum('nd,sdh->nsh', flat, Sg)) * jnp.einsum('nd,sdh->nsh', flat, Su)
        out = out + jnp.einsum('nsh,shd->nd', hs, Sd)
        return out.reshape(Bx, Tx, Dx)
    x = L0_attn_x
    mod = (_silu(L0_c) @ L0_wmod).reshape(L0_c.shape[0], 6, 1, -1)
    sa, ca, ga, sb, cb, gb = (mod[:, 0], mod[:, 1], mod[:, 2], mod[:, 3], mod[:, 4], mod[:, 5])
    ga = (2 * (ga >= 0) - 1) * jnp.maximum(jnp.abs(ga), 0.25)
    gb = (2 * (gb >= 0) - 1) * jnp.maximum(jnp.abs(gb), 0.25)
    h = _layernorm(x, axis=-1) * (1 + ca) + sa
    x = x + ga * _L0_attn_ref(h, L0_attn_Q_w, L0_attn_Q_b, L0_attn_K_w, L0_attn_K_b, L0_attn_V_w, L0_attn_V_b, L0_attn_O_w, L0_attn_O_b)
    h = _layernorm(x, axis=-1) * (1 + cb) + sb
    x = x + gb * _L0_ffn_ref(h, L0_ffn_Wr, L0_ffn_router_bias, L0_ffn_Wg, L0_ffn_Wu, L0_ffn_Wd, L0_ffn_Sg, L0_ffn_Su, L0_ffn_Sd)
    return x

_drawn_inputs = setup_inputs


def setup_inputs(seed=0):
    import zlib

    import numpy as np

    out = dict(_drawn_inputs(seed))
    spreads = {'L0_ffn_router_bias': (0.0, 0.8)}
    factors = {'L0_attn_Q_w': 8.0,
     'L0_attn_Q_b': 8.0,
     'L0_attn_K_w': 8.0,
     'L0_attn_K_b': 8.0,
     'L0_attn_V_w': 8.0,
     'L0_attn_V_b': 8.0,
     'L0_attn_O_w': 8.0,
     'L0_attn_O_b': 8.0,
     'L0_ffn_Wr': 8.0,
     'L0_ffn_Wg': 8.0,
     'L0_ffn_Wu': 8.0,
     'L0_ffn_Wd': 8.0,
     'L0_ffn_Sg': 3.32,
     'L0_ffn_Su': 3.257,
     'L0_ffn_Sd': 3.252,
     'L0_c': 2.893,
     'L0_wmod': 2.788}
    for name, (base, spread) in spreads.items():
        noise = np.random.default_rng([zlib.crc32(name.encode()), seed]).standard_normal(out[name].shape)
        drawn = base * np.exp(spread * noise) if base else spread * noise
        out[name] = jnp.asarray(drawn.astype(out[name].dtype))
    for name, factor in factors.items():
        out[name] = (out[name] * factor).astype(out[name].dtype)
    return out
```

```python
from contextlib import ExitStack

import numpy as np
import concourse.bass as bass
from concourse import mybir

F32 = mybir.dt.float32
F32R = mybir.dt.float32r
BF16 = mybir.dt.bfloat16
I32 = mybir.dt.int32
U32 = mybir.dt.uint32
ALU = mybir.AluOpType
ACT = mybir.ActivationFunctionType
AX_X = mybir.AxisListType.X
P = 128


class SbufMap:

    def __init__(self, nc, at):
        self.nc, self.at = nc, at

    def place(self, name, shape, dtype):
        size = int(np.prod(shape[1:])) * (2 if dtype == BF16 else 4)
        t = self.nc.alloc_sbuf_tensor_at(name, list(shape), dtype, offset=self.at)
        self.at += (size + 31) // 32 * 32
        return t


def adaln_block(nc, x, Q_w, Q_b, K_w, K_b, V_w, V_b, O_w, O_b, Wr, router_bias, Wg, Wu, Wd, Sg, Su, Sd,
                c_in, wmod, out):
    _, S, D = x.shape
    H, _, DH = Q_w.shape
    E, _, HE = Wg.shape
    NS, _, HS = Sg.shape
    TOPK = 4
    CAP = 128
    NT = S // P
    DC = D // P
    QB = S // 512
    TB = 4
    SC = NS * HS // P
    EPS = 1e-5
    SCALE = float(DH) ** -0.5
    MASKED = -1e5 / SCALE
    TRASH = E * CAP
    assert DH == P and HE == P and D == 512 and CAP == P

    n2_dram = nc.dram_tensor("n2_dram", [S, D], F32, kind="Internal").ap()
    table_dram = nc.dram_tensor("table_dram", [TRASH + S * TOPK, 1], I32, kind="Internal").ap()
    yb_dram = nc.dram_tensor("yb_dram", [E * CAP, D], F32, kind="Internal").ap()

    with ExitStack() as ctx:
        def sem(name):
            return ctx.enter_context(nc.semaphore(name))

        def bank(name):
            return ctx.enter_context(nc.psum_tensor(name, [P, 512], F32))

        STRIPS, GENS, PTS = 5, 2, 3
        strip = [bank(f"strip{i}") for i in range(STRIPS)]
        gen = [bank(f"gen{i}") for i in range(GENS)]
        pv = bank("pv")

        base = (nc.sbuf_base + 63) // 64 * 64
        keep = SbufMap(nc, base)
        acc = keep.place("acc", [P, NT, D], F32)
        ident = keep.place("ident", [P, P], F32)
        ident_bf = keep.place("ident_bf", [P, P], BF16)
        mask_bf = keep.place("mask_bf", [P, P], BF16)
        modT = keep.place("modT", [P, 6 * DC], F32)
        scale_a = keep.place("scale_a", [P, DC], F32)
        scale_b = keep.place("scale_b", [P, DC], F32)
        ga_bc = keep.place("ga_bc", [P, D], F32)
        gb_bc = keep.place("gb_bc", [P, D], F32)
        biasT = keep.place("biasT", [P, 3 * H], F32)
        bias_now = keep.place("bias_now", [P, 3], F32)
        stats = keep.place("stats", [P, NT, 6], F32)
        meanvar = keep.place("meanvar", [P, NT, 2], F32)
        rstd = keep.place("rstd", [P, NT], F32)
        veps = keep.place("veps", [P, NT], F32)
        neghalf = keep.place("neghalf", [P, NT], F32)
        cmax = keep.place("cmax", [P, TB, QB], F32)
        nbias = keep.place("nbias", [P, TB], F32)
        rsum = keep.place("rsum", [P, NT], F32)
        rinv = keep.place("rinv", [P, NT], F32)
        c_col = keep.place("c_col", [P, DC], F32)
        c_exp = keep.place("c_exp", [P, DC], F32)
        c_sig = keep.place("c_sig", [P, DC], F32)
        sc_col = keep.place("sc_col", [P, DC], F32)

        a = SbufMap(nc, keep.at)
        hT_hi = a.place("hT_hi", [P, DC, S], F32R)
        hT_lo = a.place("hT_lo", [P, DC, S], F32R)
        w_hi_t = [a.place(f"w{n}_hi", [P, DC, P], F32R) for n in "qkvo"]
        w_lo_t = [a.place(f"w{n}_lo", [P, DC, P], F32R) for n in "qkvo"]
        raw = [a.place(f"w{n}_raw", [P, DC, P], F32) for n in ("q", "k", "vo")]
        raw.append(raw[2])
        at_hi = a.place("at_hi", [P, 512], F32R)
        at_lo = a.place("at_lo", [P, 512], F32R)
        overlaid = a.at
        qT_hi = a.place("qT_hi", [P, 512], F32R)
        qT_lo = a.place("qT_lo", [P, 512], F32R)
        vT_f = a.place("vT_f", [P, 512], F32)
        row_at = [sum((NT - TB + q + 1) * P for q in range(r)) for r in range(TB + 1)]
        probs = a.place("probs", [P, row_at[TB]], F32)
        pT_hi = a.place("pT_hi", [P, PTS, 512], F32R)
        pT_lo = a.place("pT_lo", [P, PTS, 512], F32R)
        kT_hi = a.place("kT_hi", [P, S], F32R)
        kT_lo = a.place("kT_lo", [P, S], F32R)
        v_hi = a.place("v_hi", [P, NT, P], F32R)
        v_lo = a.place("v_lo", [P, NT, P], F32R)
        assert a.at <= nc.sbuf_usable_end, a.at
        pre = SbufMap(nc, overlaid)
        n1 = pre.place("n1", [P, 2, TB, D], F32)
        h_tmp = pre.place("h_tmp", [P, DC, 512], F32)
        wmod_sb = pre.place("wmod_sb", [P, DC, 6 * D], F32)
        sc_bc = pre.place("sc_bc", [P, DC, P], F32)
        gate_sgn, gate_mag = n1[:, 0, 0, :], n1[:, 0, 1, :]
        ob_bc = pre.place("ob_bc", [P, D], F32)
        bias_rows = pre.place("bias_rows", [3 * H, P], F32)
        assert pre.at <= a.at - D * 4, pre.at
        gob = SbufMap(nc, a.at - D * 4).place("gob", [P, D], F32)

        f = SbufMap(nc, keep.at)
        sg_sb = f.place("sg_sb", [P, DC, NS * HS], F32)
        su_sb = f.place("su_sb", [P, DC, NS * HS], F32)
        sd_sb = f.place("sd_sb", [P, SC, D], F32)
        wr_sb = f.place("wr_sb", [P, DC, E], F32)
        rb_bc = f.place("rb_bc", [P, E], F32)
        zeros_i = f.place("zeros_i", [P, E], I32)
        EX = 4
        assert f.at <= overlaid
        h2T = f.place("h2T", [P, DC, S], F32)
        wg_sb = f.place("wg_sb", [P, EX, DC, HE], F32)
        wu_sb = f.place("wu_sb", [P, EX, DC, HE], F32)
        wd_sb = f.place("wd_sb", [P, EX, D], F32)
        xb = f.place("xb", [P, EX, D], F32)
        xbT = f.place("xbT", [P, 2, D], F32)
        sil_e = f.place("sil_e", [P, 2, P], F32)
        hE = f.place("hE", [P, 2, P], F32)
        yb = f.place("yb", [P, EX, D], F32)
        sil_s = f.place("sil_s", [P, 2, 512], F32)
        w_top = f.place("w_top", [P, NT, TOPK], F32)
        slot_u = f.place("slot_u", [P, NT, TOPK], U32)
        scat_u = f.place("scat_u", [P, NT, TOPK], U32)
        tok_i = f.place("tok_i", [P, NT], I32)
        trash_i = f.place("trash_i", [P, NT, TOPK], I32)
        iota_i = f.place("iota_i", [P, E], I32)
        table = f.place("table", [P, E], I32)
        tri_bf = f.place("tri_bf", [P, P], BF16)
        ones_bf = f.place("ones_bf", [P, P], BF16)
        slot_now = f.place("slot_now", [P, 2, TOPK], U32)
        tok_now = f.place("tok_now", [P, EX], I32)
        shared_at = f.at
        n2 = f.place("n2", [P, 2, TB, D], F32)
        hs = f.place("hs", [P, SC, 512], F32)
        assert f.at <= nc.sbuf_usable_end, f.at
        r = SbufMap(nc, shared_at)
        scores = r.place("scores", [P, NT, E], F32)
        onehot = [r.place(f"onehot{k}", [P, NT, E], BF16) for k in range(TOPK)]
        picked = r.place("picked", [P, NT, E], BF16)
        pos = r.place("pos", [P, NT, E], F32)
        prod = r.place("prod", [P, NT, E], F32)
        r_stat = [r.place(f"r_stat{n}", [P, NT], F32) for n in range(4)]
        vals = r.place("vals", [P, NT, 8], F32)
        idx = r.place("idx", [P, NT, 8], U32)
        idx_f = r.place("idx_f", [P, NT, TOPK], F32)
        pos_k = r.place("pos_k", [P, NT, TOPK], F32)
        valid = r.place("valid", [P, NT, TOPK], F32)
        r_tmp = [r.place(f"r_tmp{n}", [P, NT, TOPK], F32) for n in range(3)]
        iota_f = r.place("iota_f", [P, E], F32)
        assert r.at <= nc.sbuf_usable_end, r.at
        g_ = SbufMap(nc, shared_at)
        gath = g_.place("gath", [P, 2, TOPK, D], F32)
        assert g_.at <= shared_at + 2 * TB * D * 4, g_.at

        c_landed, mod1_landed, mod2_landed = sem("c_landed"), sem("mod1_landed"), sem("mod2_landed")
        x_landed = [sem(f"x_landed{b}") for b in range(QB)]
        rows_landed, ob_landed = sem("rows_landed"), sem("ob_landed")
        raw_landed = [sem(f"raw_landed_{n}") for n in "qkvo"]
        consts = sem("consts")
        c_step = sem("c_step")
        c_act = sem("c_act")
        mod_mm, mod_out = sem("mod_mm"), sem("mod_out")
        dve_step = sem("dve_step")
        pool_step = sem("pool_step")
        pool_waited = sem("pool_waited")
        ln_stats, ln_rstd, ln_norm = sem("ln_stats"), sem("ln_rstd"), sem("ln_norm")
        ln_turned, ln_mod, ln_split = sem("ln_turned"), sem("ln_mod"), sem("ln_split")
        resid = sem("resid")
        w_hi, w_split, wo_scaled = sem("w_hi"), sem("w_split"), sem("wo_scaled")
        bias_ready = sem("bias_ready")
        gen_done, gen_hi, gen_out = sem("gen_done"), sem("gen_hi"), sem("gen_out")
        strip_done, strip_out = sem("strip_done"), sem("strip_out")
        row_logits, row_probs = sem("row_logits"), sem("row_probs")
        pt_hi, pv_done = sem("pt_hi"), sem("pv_done")
        attn_hi, attn_split = sem("attn_hi"), sem("attn_split")
        rinv_ready = sem("rinv_ready")
        sw_landed, wr_landed, rb_landed = sem("sw_landed"), sem("wr_landed"), sem("rb_landed")
        sd_scaled = sem("sd_scaled")
        n2_stored = [sem(f"n2_stored{i}") for i in range(2)]
        zero_stored = sem("zero_stored")
        logits_mm, r_shift, r_exp, picked_ready, pos_mm, routed = (
            sem("logits_mm"), sem("r_shift"), sem("r_exp"), sem("picked_ready"), sem("pos_mm"), sem("routed"))
        scattered, table_landed = sem("scattered"), sem("table_landed")
        gu_done, silu_done, hs_ready = sem("gu_done"), sem("silu_done"), sem("hs_ready")
        down_done, down_out = sem("down_done"), sem("down_out")
        e_landed = [sem(f"e_landed{i}") for i in range(EX)]
        xb_landed = [sem(f"xb_landed{i}") for i in range(EX)]
        tok_ready = sem("tok_ready")
        xb_turned, xbT_ready = sem("xb_turned"), sem("xbT_ready")
        e_gu, e_silu, e_h = sem("e_gu"), sem("e_silu"), sem("e_h")
        e_down, yb_ready = sem("e_down"), sem("yb_ready")
        yb_stored = [sem(f"yb_stored{i}") for i in range(EX)]
        slot_ready = sem("slot_ready")
        g_landed = [sem(f"g_landed{i}") for i in range(2)]
        gath_free, combined = sem("gath_free"), sem("combined")
        out_stored = sem("out_stored")

        order = [("q", 0, 0), ("k", 0, 0), ("v", 0, 0)] + [("o", QB - 1, t) for t in range(TB)] + [("t", 0, 0)]
        for j in range(1, QB):
            order += [("q", j, 0), ("k", j, 0), ("v", j, 0)]
            if j >= 2:
                order += [("o", j - 2, t) for t in range(TB)]
            order += [("t", j, 0)]
        order += [("o", QB - 2, t) for t in range(TB)]
        G = {u: n for n, u in enumerate(order)}
        NG = len(order)
        HI = {u: n for n, u in enumerate([u for u in order if u[0] in "qkt"])}
        NHI = len(HI)

        def units(j):
            return TB * (j + 1)

        def strips_before(j):
            return sum(2 * units(i) for i in range(j))

        def turned_before(j):
            return sum(units(i) for i in range(j))

        NSTRIP, NTURN = strips_before(QB), turned_before(QB)
        assert NG % GENS == 0 and NSTRIP % STRIPS == 0

        def score_units(j):
            return [(t, ch, 512 if ch < j else (t + 1) * P) for t in range(TB) for ch in range(j + 1)]

        def first_col(j, kk):
            return max(0, kk - TB * j) * P

        block = ctx.enter_context(nc.Block())

        @block.sync
        def _(sp):
            sp.dma_start(c_col[:], c_in.rearrange("o (c p) -> p (o c)", p=P),
                         allow_slow_non_contiguous=True).then_inc(c_landed, 16)
            wm = wmod.rearrange("(c p) n -> p c n", p=P)
            xt = x.rearrange("o (t p) d -> p (o t) d", p=P)
            w_dram = [w.rearrange("h (c p) d -> h p c d", p=P) for w in (Q_w, K_w, V_w)]
            w_dram.append(O_w.rearrange("h p (c d) -> h p c d", d=P))

            def load_x(b):
                sp.dma_start(acc[:, TB * b:TB * b + TB, :], xt[:, TB * b:TB * b + TB, :]).then_inc(x_landed[b], 16)

            load_x(0)
            sp.dma_start(wmod_sb[:, :, 0:2 * D], wm[:, :, 0:2 * D]).then_inc(mod1_landed, 16)
            for b in range(1, QB):
                load_x(b)
            for n, bias in enumerate((Q_b, K_b, V_b)):
                sp.dma_start(bias_rows[H * n:H * n + H, :], bias).then_inc(rows_landed, 16)
            sp.dma_start(ob_bc[:], O_b.partition_broadcast(P)).then_inc(ob_landed, 16)
            for n in range(3):
                sp.dma_start(raw[n][:], w_dram[n][0]).then_inc(raw_landed[n], 16)
            sp.dma_start(wmod_sb[:, :, 2 * D:6 * D], wm[:, :, 2 * D:6 * D]).then_inc(mod2_landed, 16)
            sp.wait_ge(w_split, 3)
            sp.dma_start(raw[3][:], w_dram[3][0]).then_inc(raw_landed[3], 16)
            with sp.Fori(0, H - 1) as h:
                for n in range(4):
                    sp.wait_ge(w_split, h * 4 + (1, 2, 4, 7)[n])
                    sp.dma_start(raw[n][:], w_dram[n][bass.ds(h + 1, 1)].rearrange("o p c d -> (o p) c d")
                                 ).then_inc(raw_landed[n], 16)
            sp.wait_ge(gen_done, NG * (H - 1) + G["v", QB - 1, 0] + 1)
            sp.dma_start(wr_sb[:], Wr.rearrange("(c p) e -> p c e", p=P)).then_inc(wr_landed, 16)
            sp.dma_start(rb_bc[:], router_bias.partition_broadcast(P)).then_inc(rb_landed, 16)
            for dst, src in ((sg_sb, Sg), (su_sb, Su)):
                for s in range(NS):
                    sp.dma_start(dst[:, :, HS * s:HS * s + HS], src[s].rearrange("(c p) h -> p c h", p=P)
                                 ).then_inc(sw_landed, 16)
            for s in range(NS):
                sp.dma_start(sd_sb[:, SC // NS * s:SC // NS * (s + 1), :], Sd[s].rearrange("(c p) d -> p c d", p=P)
                             ).then_inc(sw_landed, 16)
            sp.wait_ge(consts, 5)
            sp.dma_start(table_dram[0:TRASH, :].rearrange("(p e) o -> p (e o)", p=P), zeros_i[:]
                         ).then_inc(zero_stored, 16)
            n2v = n2_dram.rearrange("(b t p) d -> b p t d", p=P, t=TB)
            for b in range(QB):
                sp.wait_ge(ln_norm, NT + TB * b + TB)
                sp.dma_start(n2v[b], n2[:, b % 2]).then_inc(n2_stored[b % 2], 16)
            sp.wait_ge(scattered, 16 * NT * TOPK)
            sp.dma_start(table[:], table_dram[0:TRASH, :].rearrange("(s e) o -> s (e o)", e=E)
                         ).then_inc(table_landed, 16)
            ybv = yb_dram.rearrange("(e s) d -> e s d", s=CAP)
            with sp.Fori(0, E // EX) as g:
                for i in range(EX):
                    sp.wait_ge(yb_ready, g * EX + (EX + i + 1))
                    sp.dma_start(ybv[bass.ds(g * EX + i, 1)].rearrange("o s d -> (o s) d"), yb[:, i, :]
                                 ).then_inc(yb_stored[i], 16)
            ov = out.rearrange("o (t p) d -> (o t) p d", p=P)
            with sp.Fori(0, NT) as t:
                sp.wait_ge(combined, t + 1)
                sp.dma_start(ov[bass.ds(t, 1)].rearrange("o p d -> (o p) d"), acc[:, bass.ds(t, 1), :]
                             .rearrange("p o d -> p (o d)")).then_inc(out_stored, 16)
            sp.wait_ge(out_stored, 16 * NT)

        @block.gpsimd
        def _(pool):
            steps = [0]

            def link(ins):
                steps[0] += 1
                ins.then_inc(pool_step, 1)
                pool.wait_ge(pool_step, steps[0])

            def wait_alone(semaphore, value):
                pool.wait_ge(semaphore, value)
                pool.sem_inc(pool_waited, 1)

            link(nc.gpsimd.memset(ident[:], 0.0))
            nc.gpsimd.affine_select(out=ident[:], in_=ident[:], compare_op=ALU.not_equal, fill=1.0, base=0,
                                    pattern=[[-1, P]], channel_multiplier=1).then_inc(consts, 1)
            link(nc.gpsimd.memset(ident_bf[:], 0.0))
            nc.gpsimd.affine_select(out=ident_bf[:], in_=ident_bf[:], compare_op=ALU.not_equal, fill=1.0, base=0,
                                    pattern=[[-1, P]], channel_multiplier=1).then_inc(consts, 1)
            link(nc.gpsimd.memset(mask_bf[:], 0.0))
            nc.gpsimd.affine_select(out=mask_bf[:], in_=mask_bf[:], compare_op=ALU.is_ge, fill=MASKED, base=0,
                                    pattern=[[-1, P]], channel_multiplier=1).then_inc(consts, 1)
            nc.gpsimd.memset(neghalf[:], -0.5).then_inc(consts, 1)

            def ln_scales(base, b):
                pool.wait_ge(ln_stats, base + TB * b + TB)
                tiles = slice(TB * b, TB * b + TB)
                link(nc.gpsimd.tensor_scalar(veps[:, tiles], meanvar[:, tiles, 1], EPS, None, ALU.add))
                nc.gpsimd.tensor_tensor(rstd[:, tiles], veps[:, tiles], neghalf[:, tiles], ALU.pow
                                        ).then_inc(ln_rstd, 1)

            pool.wait_ge(consts, 4)
            for b in range(QB):
                ln_scales(0, b)
            for b in range(QB):
                for ch in range(DC):
                    pool.wait_ge(ln_mod, DC * b + ch + 1)
                    cols = slice(512 * b, 512 * b + 512)
                    nc.gpsimd.tensor_tensor(hT_lo[:, ch, cols], h_tmp[:, ch, :], hT_hi[:, ch, cols].bitcast(F32),
                                            ALU.subtract).then_inc(ln_split, 1)

            def split_lo(n, h):
                pool.wait_ge(w_hi, h * 4 + (n + 1))
                nc.gpsimd.tensor_tensor(w_lo_t[n][:], raw[n][:], w_hi_t[n][:].bitcast(F32), ALU.subtract
                                        ).then_inc(w_split, 1)

            def take_bias(h):
                src = biasT[:].rearrange("p (n h) -> p n h", n=3)[:, :, bass.ds(h, 1)].rearrange("p n o -> p (n o)")
                nc.gpsimd.tensor_copy(bias_now[:], src).then_inc(bias_ready, 1)

            def scale_wo(h):
                pool.wait_ge(raw_landed[3], h * 16 + 16)
                nc.gpsimd.tensor_tensor(raw[3][:].rearrange("p c d -> p (c d)"), raw[3][:].rearrange("p c d -> p (c d)"),
                                        ga_bc[:], ALU.mult).then_inc(wo_scaled, 1)

            for n in range(3):
                split_lo(n, 0)
            pool.wait_ge(mod_out, 2)
            nc.gpsimd.tensor_copy(bias_now[:], biasT[:].rearrange("p (n h) -> p n h", n=3)[:, :, 0]
                                  ).then_inc(bias_ready, 1)
            pool.wait_ge(mod_out, 3)
            pool.wait_ge(ob_landed, 16)
            pool.wait_ge(ln_norm, NT)
            link(nc.gpsimd.tensor_tensor(gob[:], ga_bc[:], ob_bc[:], ALU.mult))
            for t in list(range(NT - TB, NT)) + list(range(NT - TB)):
                nc.gpsimd.tensor_tensor(acc[:, t, :], acc[:, t, :], gob[:], ALU.add).then_inc(resid, 1)

            with pool.Fori(0, H - 1) as h:
                scale_wo(h)
                split_lo(3, h)
                split_lo(0, h + 1)
                split_lo(1, h + 1)
                split_lo(2, h + 1)
                take_bias(h + 1)
            scale_wo(H - 1)
            split_lo(3, H - 1)

            pool.wait_ge(gen_done, NG * (H - 1) + G["v", QB - 1, 0] + 1)
            nc.gpsimd.memset(zeros_i[:], 0).then_inc(consts, 1)
            pool.wait_ge(sw_landed, 16 * 3 * NS)
            for ch in range(SC):
                nc.gpsimd.tensor_tensor(sd_sb[:, ch, :], sd_sb[:, ch, :], gb_bc[:], ALU.mult).then_inc(sd_scaled, 1)
            pool.wait_ge(gen_out, GENS + NG * H + TB)
            link(nc.gpsimd.memset(tri_bf[:], 0.0))
            nc.gpsimd.affine_select(out=tri_bf[:], in_=tri_bf[:], compare_op=ALU.is_ge, fill=1.0, base=0,
                                    pattern=[[-1, P]], channel_multiplier=1).then_inc(consts, 1)
            nc.gpsimd.memset(ones_bf[:], 1.0).then_inc(consts, 1)
            nc.gpsimd.iota(iota_i[:], [[1, E]], base=0, channel_multiplier=0).then_inc(consts, 1)
            nc.gpsimd.iota(tok_i[:], [[P, NT]], base=0, channel_multiplier=1).then_inc(consts, 1)
            nc.gpsimd.iota(trash_i[:], [[P * TOPK, NT], [1, TOPK]], base=TRASH, channel_multiplier=TOPK
                           ).then_inc(consts, 1)
            for b in range(QB):
                ln_scales(NT, b)

            pool.wait_ge(routed, 1)
            pool.wait_ge(zero_stored, 16)
            pool.wait_ge(consts, 10)
            for t in range(NT):
                for k in range(TOPK):
                    nc.gpsimd.indirect_dma_start(
                        out=table_dram, out_offset=bass.IndirectOffsetOnAxis(ap=scat_u[:, t, k:k + 1], axis=0),
                        in_=tok_i[:, t:t + 1], in_offset=None).then_inc(scattered, 16)
            pool.wait_ge(table_landed, 16)
            pool.wait_ge(n2_stored[0], 32)
            pool.wait_ge(n2_stored[1], 32)
            with pool.Fori(0, E // EX) as g:
                for i in range(EX):
                    wait_alone(xb_turned, g * EX + (i + 1))
                    nc.gpsimd.tensor_copy(tok_now[:, i:i + 1], table[:, bass.ds(g * EX + i, 1)]).then_inc(tok_ready, 1)
                    wait_alone(tok_ready, g * EX + (i + 1))
                    nc.gpsimd.indirect_dma_start(
                        out=xb[:, i, :], out_offset=None, in_=n2_dram,
                        in_offset=bass.IndirectOffsetOnAxis(ap=tok_now[:, i:i + 1], axis=0)).then_inc(xb_landed[i], 16)
            for i in range(EX):
                pool.wait_ge(yb_stored[i], 16 * (E // EX + 1))
            with pool.Fori(0, NT // 2) as g:
                for i in range(2):
                    wait_alone(gath_free, g * 2 + (i + 1))
                    nc.gpsimd.tensor_copy(slot_now[:, i, :], slot_u[:, bass.ds(g * 2 + i, 1), :]
                                          .rearrange("p o k -> p (o k)")).then_inc(slot_ready, 1)
                    wait_alone(slot_ready, g * 2 + (i + 1))
                    for k in range(TOPK):
                        nc.gpsimd.indirect_dma_start(
                            out=gath[:, i, k, :], out_offset=None, in_=yb_dram,
                            in_offset=bass.IndirectOffsetOnAxis(ap=slot_now[:, i, k:k + 1], axis=0)
                        ).then_inc(g_landed[i], 16)

        @block.scalar
        def _(act):
            act.wait_ge(c_landed, 16)
            nc.scalar.activation(c_exp[:], c_col[:], ACT.Exp, scale=-1.0).then_inc(c_act, 1)

            act.wait_ge(mod_out, 1)
            for b in range(QB):
                for ch in range(DC):
                    act.wait_ge(ln_turned, DC * b + ch + 1)
                    if b >= 1:
                        act.wait_ge(ln_split, DC * (b - 1) + ch + 1)
                    nc.scalar.activation(hT_hi[:, ch, 512 * b:512 * b + 512], strip[ch][:], ACT.Identity,
                                         bias=modT[:, ch:ch + 1], scale=scale_a[:, ch:ch + 1])
                    nc.scalar.activation(h_tmp[:, ch, :], strip[ch][:], ACT.Identity,
                                         bias=modT[:, ch:ch + 1], scale=scale_a[:, ch:ch + 1]).then_inc(ln_mod, 1)

            def split_hi(n):
                nc.scalar.activation(w_hi_t[n][:], raw[n][:], ACT.Copy).then_inc(w_hi, 1)

            for n in range(3):
                act.wait_ge(raw_landed[n], 16)
                split_hi(n)

            def gen_hi_of(kind, j, h):
                u = G[kind, j, 0]
                act.wait_ge(gen_done, h * NG + (u + 1))
                src = gen[u % GENS]
                if kind == "q":
                    act.wait_ge(bias_ready, h + 1)
                    ins = nc.scalar.activation(qT_hi[:], src[:], ACT.Identity, bias=bias_now[:, 0:1])
                elif kind == "k":
                    ins = nc.scalar.activation(kT_hi[:, 512 * j:512 * j + 512], src[:], ACT.Identity,
                                               bias=bias_now[:, 1:2])
                else:
                    ins = nc.scalar.activation(v_hi[:, TB * j:TB * j + TB, :],
                                               src[:].rearrange("p (t d) -> p t d", t=TB), ACT.Copy)
                ins.then_inc(gen_hi, 1)

            def exp_rows(j, h):
                for t in range(TB):
                    act.wait_ge(row_logits, h * NT + (TB * j + t + 1))
                    w = (TB * j + t + 1) * P
                    row = probs[:, row_at[t]:row_at[t] + w]
                    nc.scalar.activation(row, row, ACT.Exp, bias=nbias[:, t:t + 1],
                                         accum_out=rsum[:, TB * j + t:TB * j + t + 1]).then_inc(row_probs, 1)

            def turned_hi(j, h):
                for kk in range(units(j)):
                    u = strips_before(j) + units(j) + kk
                    act.wait_ge(strip_done, h * NSTRIP + (u + 1))
                    if kk >= PTS:
                        act.wait_ge(pv_done, h * NTURN + (turned_before(j) + kk - PTS + 1))
                    c0 = first_col(j, kk)
                    nc.scalar.activation(pT_hi[:, kk % PTS, c0:512], strip[u % STRIPS][:, c0:512], ACT.Copy
                                         ).then_inc(pt_hi, 1)
                act.wait_ge(pv_done, h * NTURN + turned_before(j + 1))
                nc.scalar.activation(at_hi[:], pv[:], ACT.Copy).then_inc(attn_hi, 1)

            def head(h, last):
                gen_hi_of("q", 0, h)
                gen_hi_of("k", 0, h)
                act.wait_ge(wo_scaled, h + 1)
                act.wait_ge(gen_done, h * NG + (G["o", QB - 1, TB - 1] + 1))
                split_hi(3)
                gen_hi_of("t", 0, h)
                exp_rows(0, h)
                for j in range(1, QB):
                    gen_hi_of("q", j, h)
                    gen_hi_of("k", j, h)
                    turned_hi(j - 1, h)
                    gen_hi_of("t", j, h)
                    exp_rows(j, h)
                if not last:
                    act.wait_ge(gen_out, h * NG + (GENS + G["v", QB - 1, 0] + 1))
                    for n in range(3):
                        act.wait_ge(raw_landed[n], h * 16 + 32)
                        split_hi(n)
                turned_hi(QB - 1, h)

            act.wait_ge(attn_split, 1)
            with act.Fori(0, H - 1) as h:
                head(h, False)
            head(H - 1, True)

            for b in range(QB):
                for ch in range(DC):
                    act.wait_ge(ln_turned, NT + DC * b + ch + 1)
                    nc.scalar.activation(h2T[:, ch, 512 * b:512 * b + 512], strip[ch][:], ACT.Identity,
                                         bias=modT[:, 3 * DC + ch:3 * DC + ch + 1], scale=scale_b[:, ch:ch + 1]
                                         ).then_inc(ln_mod, 1)
            act.wait_ge(r_shift, 1)
            nc.scalar.activation(scores[:], prod[:], ACT.Exp).then_inc(r_exp, 1)

            def shared_silu(n, b):
                for ch in range(SC):
                    act.wait_ge(gu_done, b * SC + (n + ch + 1))
                    nc.scalar.activation(sil_s[:, ch % 2, :], strip[2 * (ch % 2)][:], ACT.Silu).then_inc(silu_done, 1)

            def load_expert(i, g):
                for dst, src in ((wg_sb, Wg), (wu_sb, Wu)):
                    sv = src.rearrange("e (c p) h -> e p c h", p=P)
                    act.dma_start(dst[:, i, :, :], sv[bass.ds(g * EX + i, 1)].rearrange("o p c h -> (o p) c h")
                                  ).then_inc(e_landed[i], 16)
                act.dma_start(wd_sb[:, i, :], Wd[bass.ds(g * EX + i, 1)].rearrange("o p d -> (o p) d")
                              ).then_inc(e_landed[i], 16)

            act.wait_ge(logits_mm, 2)
            for i in range(EX):
                for dst, src in ((wg_sb, Wg), (wu_sb, Wu)):
                    act.dma_start(dst[:, i, :, :], src[i].rearrange("(c p) h -> p c h", p=P)).then_inc(e_landed[i], 16)
                act.dma_start(wd_sb[:, i, :], Wd[i]).then_inc(e_landed[i], 16)
            for b in range(2):
                shared_silu(b * SC, 0)

            def expert_T(i, g):
                act.wait_ge(xb_turned, g * EX + (EX + i + 1))
                for ch in range(DC):
                    ins = nc.scalar.activation(xbT[:, i % 2, P * ch:P * ch + P], gen[i % 2][:, P * ch:P * ch + P],
                                               ACT.Identity, bias=modT[:, 3 * DC + ch:3 * DC + ch + 1],
                                               scale=scale_b[:, ch:ch + 1])
                ins.then_inc(xbT_ready, 1)

            def expert_silu(i, g):
                act.wait_ge(e_gu, g * EX + (i + 1))
                nc.scalar.activation(sil_e[:, i % 2, :], strip[2 * (i % 2)][:, 0:P], ACT.Silu).then_inc(e_silu, 1)

            def experts(g, last):
                expert_T(0, g)
                for i in range(EX):
                    if i + 1 < EX:
                        expert_T(i + 1, g)
                    expert_silu(i, g)
                if not last:
                    for i in range(EX):
                        act.wait_ge(e_down, g * EX + (i + 1))
                        load_expert(i, g + 1)

            with act.Fori(0, E // EX - 1) as g:
                experts(g, False)
            experts(E // EX - 1, True)
            for b in range(2):
                shared_silu((2 + b) * SC, 0)

        @block.vector
        def _(dve):
            steps = [0]

            def link(ins):
                steps[0] += 1
                ins.then_inc(dve_step, 1)
                dve.wait_ge(dve_step, steps[0])

            for t in (at_hi, at_lo):
                nc.vector.memset(t[:].bitcast(F32), 0.0).then_inc(c_step, 1)
            for t in (w_hi_t[3], w_lo_t[3]):
                nc.vector.memset(t[:].bitcast(F32), 0.0).then_inc(c_step, 1)
            nc.vector.memset(rinv[:], 0.0).then_inc(rinv_ready, 1)

            dve.wait_ge(c_act, 1)
            link(nc.vector.tensor_scalar(c_sig[:], c_exp[:], 1.0, None, ALU.add))
            link(nc.vector.reciprocal(c_sig[:], c_sig[:]))
            link(nc.vector.tensor_tensor(sc_col[:], c_col[:], c_sig[:], ALU.mult))
            nc.vector.tensor_copy(sc_bc[:], sc_col[:].unsqueeze(2).to_broadcast([P, DC, P])).then_inc(c_step, 1)

            def ln_stat(base, b):
                for t in range(TB * b, TB * b + TB):
                    ins = nc.vector.bn_stats(stats[:, t, :], acc[:, t, :])
                    if t < TB * b + TB - 1:
                        steps[0] += 1
                        ins.then_inc(dve_step, 1)
                    else:
                        link(ins)
                for t in range(TB * b, TB * b + TB):
                    nc.vector.bn_aggr(meanvar[:, t, :], stats[:, t, :]).then_inc(ln_stats, 1)

            def ln_normalise(base, b, dst):
                dve.wait_ge(ln_rstd, base // TB + b + 1)
                dve.wait_ge(ln_stats, base + TB * b + TB)
                if b >= 2:
                    dve.wait_ge(ln_turned, base + TB * (b - 2) + TB)
                for t in range(TB):
                    i = TB * b + t
                    nc.vector.tensor_scalar(dst[:, b % 2, t, :], acc[:, i, :], meanvar[:, i, 0:1], rstd[:, i:i + 1],
                                            ALU.subtract, ALU.mult).then_inc(ln_norm, 1)

            def modulation(first, src, dst):
                link(nc.vector.tensor_copy(modT[:, first:first + 2 * DC], src))
                nc.vector.tensor_scalar(dst[:], modT[:, first + DC:first + 2 * DC], 1.0, None, ALU.add
                                        ).then_inc(mod_out, 1)

            def gate(src, dst):
                link(nc.vector.tensor_scalar(gate_sgn, src, 0.0, 2.0, ALU.is_ge, ALU.mult))
                link(nc.vector.scalar_tensor_tensor(gate_mag, gate_sgn, -1.0, src, ALU.add, ALU.mult))
                link(nc.vector.tensor_scalar(gate_mag, gate_mag, 0.25, None, ALU.max))
                return nc.vector.scalar_tensor_tensor(dst[:], gate_sgn, -1.0, gate_mag, ALU.add, ALU.mult)

            dve.wait_ge(x_landed[0], 16)
            ln_stat(0, 0)
            dve.wait_ge(mod_mm, 1)
            modulation(0, pv[:, 0:2 * DC], scale_a)
            ln_normalise(0, 0, n1)
            for b in range(1, QB):
                dve.wait_ge(x_landed[b], 16)
                ln_stat(0, b)
                ln_normalise(0, b, n1)
            dve.wait_ge(mod_mm, 2)
            nc.vector.tensor_copy(biasT[:], gen[0][:, 0:3 * H]).then_inc(mod_out, 1)
            dve.wait_ge(mod_mm, 3)
            gate(strip[4][:], ga_bc).then_inc(mod_out, 1)
            dve.wait_ge(mod_mm, 4)
            dve.wait_ge(mod_out, 3)
            gate(gen[1][:], gb_bc).then_inc(mod_out, 1)
            dve.wait_ge(mod_mm, 5)
            modulation(3 * DC, pv[:, 0:2 * DC], scale_b)
            dve.wait_ge(mod_out, 5)
            dve.wait_ge(ln_mod, NT)
            dve.wait_ge(c_step, 5)
            dve.wait_ge(rinv_ready, 1)
            dve.sem_inc(gen_out, GENS)
            dve.sem_inc(strip_out, STRIPS)
            dve.sem_inc(attn_split, 1)

            def gen_out_of(kind, j, t, h):
                u = G[kind, j, t]
                src = gen[u % GENS]
                if kind in "qkt":
                    dve.wait_ge(gen_hi, h * NHI + (HI[kind, j, t] + 1))
                else:
                    dve.wait_ge(gen_done, h * NG + (u + 1))
                if kind == "q":
                    ins = nc.vector.scalar_tensor_tensor(qT_lo[:], src[:], bias_now[:, 0:1], qT_hi[:].bitcast(F32),
                                                         ALU.add, ALU.subtract)
                elif kind == "k":
                    cols = slice(512 * j, 512 * j + 512)
                    ins = nc.vector.scalar_tensor_tensor(kT_lo[:, cols], src[:], bias_now[:, 1:2],
                                                         kT_hi[:, cols].bitcast(F32), ALU.add, ALU.subtract)
                elif kind == "v":
                    ins = nc.vector.tensor_scalar(vT_f[:], src[:], bias_now[:, 2:3], None, ALU.add)
                elif kind == "t":
                    rows = slice(TB * j, TB * j + TB)
                    ins = nc.vector.tensor_tensor(v_lo[:, rows, :], src[:].rearrange("p (t d) -> p t d", t=TB),
                                                  v_hi[:, rows, :].bitcast(F32), ALU.subtract)
                else:
                    i = TB * j + t
                    if t == 0:
                        dve.wait_ge(rinv_ready, h * QB + (1 if j == QB - 1 else j + 2))
                        dve.wait_ge(resid, TB if j == QB - 1 else NT)
                    ins = nc.vector.scalar_tensor_tensor(acc[:, i, :], src[:], rinv[:, i:i + 1], acc[:, i, :],
                                                         ALU.mult, ALU.add)
                ins.then_inc(gen_out, 1)

            def scores_out(j, h):
                for n, (t, ch, w) in enumerate(score_units(j)):
                    u = strips_before(j) + n
                    dve.wait_ge(strip_done, h * NSTRIP + (u + 1))
                    at = row_at[t] + 512 * ch
                    nc.vector.tensor_scalar(probs[:, at:at + w], strip[u % STRIPS][:, 0:w], SCALE, None, ALU.mult,
                                            ALU.max, accum_out=cmax[:, t, ch:ch + 1]).then_inc(strip_out, 1)
                    if ch == j:
                        dve.wait_ge(strip_out, h * NSTRIP + (STRIPS + u + 1))
                        nc.vector.tensor_reduce(nbias[:, t:t + 1], cmax[:, t, 0:j + 1], AX_X, ALU.max, negate=True
                                                ).then_inc(row_logits, 1)

            def turned_lo(j, h):
                for kk in range(units(j)):
                    u = strips_before(j) + units(j) + kk
                    dve.wait_ge(pt_hi, h * NTURN + (turned_before(j) + kk + 1))
                    c0 = first_col(j, kk)
                    nc.vector.tensor_tensor(pT_lo[:, kk % PTS, c0:512], strip[u % STRIPS][:, c0:512],
                                            pT_hi[:, kk % PTS, c0:512].bitcast(F32), ALU.subtract
                                            ).then_inc(strip_out, 1)
                dve.wait_ge(attn_hi, h * QB + (j + 1))
                nc.vector.tensor_tensor(at_lo[:], pv[:], at_hi[:].bitcast(F32), ALU.subtract).then_inc(attn_split, 1)
                nc.vector.reciprocal(rinv[:, TB * j:TB * j + TB], rsum[:, TB * j:TB * j + TB]).then_inc(rinv_ready, 1)

            def head(h):
                for kind in "qkv":
                    gen_out_of(kind, 0, 0, h)
                for t in range(TB):
                    gen_out_of("o", QB - 1, t, h)
                gen_out_of("t", 0, 0, h)
                scores_out(0, h)
                for j in range(1, QB):
                    for kind in "qkv":
                        gen_out_of(kind, j, 0, h)
                    if j >= 2:
                        for t in range(TB):
                            gen_out_of("o", j - 2, t, h)
                    turned_lo(j - 1, h)
                    gen_out_of("t", j, 0, h)
                    scores_out(j, h)
                for t in range(TB):
                    gen_out_of("o", QB - 2, t, h)
                turned_lo(QB - 1, h)

            with dve.Fori(0, H) as h:
                head(h)
            dve.wait_ge(rinv_ready, QB * H + 1)
            for t in range(TB):
                u = NG * H + t
                dve.wait_ge(gen_done, u + 1)
                i = NT - TB + t
                nc.vector.scalar_tensor_tensor(acc[:, i, :], gen[u % GENS][:], rinv[:, i:i + 1], acc[:, i, :],
                                               ALU.mult, ALU.add).then_inc(gen_out, 1)

            dve.wait_ge(gen_out, GENS + NG * H + TB)
            for b in range(QB):
                ln_stat(NT, b)
                if b >= 2:
                    dve.wait_ge(n2_stored[b % 2], 16)
                ln_normalise(NT, b, n2)

            dve.wait_ge(consts, 10)
            dve.wait_ge(rb_landed, 16)
            dve.wait_ge(n2_stored[0], 32)
            dve.wait_ge(n2_stored[1], 32)
            half = NT // 2
            dve.wait_ge(logits_mm, 2)
            for s in range(2):
                link(nc.vector.tensor_tensor(scores[:, half * s:half * s + half, :],
                                             gen[s][:].rearrange("p (t e) -> p t e", e=E),
                                             rb_bc[:].unsqueeze(1).to_broadcast([P, half, E]), ALU.add))
            mx, total, inv, inv4 = r_stat
            link(nc.vector.tensor_reduce(mx[:], scores[:], AX_X, ALU.max))
            nc.vector.tensor_tensor(prod[:], scores[:], mx[:].unsqueeze(2).to_broadcast([P, NT, E]), ALU.subtract
                                    ).then_inc(r_shift, 1)
            link(nc.vector.tensor_copy(iota_f[:], iota_i[:]))
            dve.wait_ge(r_exp, 1)
            link(nc.vector.tensor_reduce(total[:], scores[:], AX_X, ALU.add))
            link(nc.vector.reciprocal(inv[:], total[:]))
            link(nc.vector.tensor_tensor(scores[:], scores[:], inv[:].unsqueeze(2).to_broadcast([P, NT, E]), ALU.mult))
            for t in range(NT):
                ins = nc.vector.max(vals[:, t, :], scores[:, t, :])
                steps[0] += 1
                ins.then_inc(dve_step, 1)
            dve.wait_ge(dve_step, steps[0])
            for t in range(NT):
                ins = nc.vector.max_index(idx[:, t, :], vals[:, t, :], scores[:, t, :])
                steps[0] += 1
                ins.then_inc(dve_step, 1)
            dve.wait_ge(dve_step, steps[0])
            link(nc.vector.tensor_copy(idx_f[:], idx[:, :, 0:TOPK]))
            for k in range(TOPK):
                link(nc.vector.tensor_tensor(onehot[k][:], iota_f[:].unsqueeze(1).to_broadcast([P, NT, E]),
                                             idx_f[:, :, k:k + 1].to_broadcast([P, NT, E]), ALU.is_equal))
            link(nc.vector.tensor_tensor(picked[:], onehot[0][:], onehot[1][:], ALU.add))
            link(nc.vector.tensor_tensor(picked[:], picked[:], onehot[2][:], ALU.add))
            nc.vector.tensor_tensor(picked[:], picked[:], onehot[3][:], ALU.add).then_inc(picked_ready, 1)
            link(nc.vector.tensor_reduce(total[:], vals[:, :, 0:TOPK], AX_X, ALU.add))
            link(nc.vector.reciprocal(inv4[:], total[:]))
            link(nc.vector.tensor_tensor(w_top[:], vals[:, :, 0:TOPK], inv4[:].unsqueeze(2).to_broadcast([P, NT, TOPK]),
                                         ALU.mult))
            dve.wait_ge(pos_mm, 2)
            for s in range(2):
                link(nc.vector.tensor_copy(pos[:, half * s:half * s + half, :],
                                           gen[s][:].rearrange("p (t e) -> p t e", e=E)))
            for k in range(TOPK):
                link(nc.vector.tensor_tensor(prod[:], onehot[k][:], pos[:], ALU.mult))
                link(nc.vector.tensor_reduce(pos_k[:, :, k], prod[:], AX_X, ALU.add))
            t0, t1, t2 = r_tmp
            link(nc.vector.tensor_scalar(valid[:], pos_k[:], float(CAP), None, ALU.is_lt))
            link(nc.vector.tensor_tensor(w_top[:], w_top[:], valid[:], ALU.mult))
            link(nc.vector.tensor_scalar(t0[:], pos_k[:], float(CAP - 1), None, ALU.min))
            link(nc.vector.scalar_tensor_tensor(t1[:], idx_f[:], float(CAP), t0[:], ALU.mult, ALU.add))
            link(nc.vector.tensor_copy(slot_u[:], t1[:]))
            link(nc.vector.scalar_tensor_tensor(t0[:], pos_k[:], float(E), idx_f[:], ALU.mult, ALU.add))
            link(nc.vector.tensor_copy(t1[:], trash_i[:]))
            link(nc.vector.tensor_tensor(t0[:], t0[:], t1[:], ALU.subtract))
            link(nc.vector.tensor_tensor(t2[:], t0[:], valid[:], ALU.mult))
            link(nc.vector.tensor_tensor(t0[:], t2[:], t1[:], ALU.add))
            nc.vector.tensor_copy(scat_u[:], t0[:]).then_inc(routed, 1)
            dve.sem_inc(xb_turned, EX)
            dve.sem_inc(yb_ready, EX)
            dve.sem_inc(gath_free, 2)
            for i in range(EX):
                dve.sem_inc(yb_stored[i], 16)

            def shared(n):
                for ch in range(SC):
                    u = n * SC + ch
                    dve.wait_ge(silu_done, u + 1)
                    nc.vector.tensor_tensor(hs[:, ch, :], strip[2 * (ch % 2) + 1][:], sil_s[:, ch % 2, :], ALU.mult
                                            ).then_inc(hs_ready, 1)
                for t in range(TB):
                    dve.wait_ge(down_done, n * TB + t + 1)
                    src = strip[4] if t % 2 == 0 else pv
                    nc.vector.tensor_tensor(acc[:, n * TB + t, :], src[:], acc[:, n * TB + t, :], ALU.add
                                            ).then_inc(down_out, 1)

            for n in range(2):
                shared(n)

            def experts(g):
                for i in range(EX):
                    dve.wait_ge(e_silu, g * EX + (i + 1))
                    nc.vector.tensor_tensor(hE[:, i % 2, :], strip[2 * (i % 2) + 1][:, 0:P], sil_e[:, i % 2, :], ALU.mult
                                            ).then_inc(e_h, 1)
                    if i >= 1:
                        expert_out(i - 1, g)
                expert_out(EX - 1, g)

            def expert_out(i, g):
                dve.wait_ge(e_down, g * EX + (i + 1))
                dve.wait_ge(yb_stored[i], g * 16 + 16)
                src = strip[4] if i % 2 == 0 else pv
                nc.vector.tensor_tensor(yb[:, i, :], src[:], gb_bc[:], ALU.mult).then_inc(yb_ready, 1)

            with dve.Fori(0, E // EX) as g:
                experts(g)
            for n in range(2, QB):
                shared(n)
            dve.wait_ge(down_out, NT)
            with dve.Fori(0, NT // 2) as g:
                for i in range(2):
                    dve.wait_ge(g_landed[i], g * (16 * TOPK) + 16 * TOPK)
                    for k in range(TOPK):
                        row = acc[:, bass.ds(g * 2 + i, 1), :].rearrange("p o d -> p (o d)")
                        wk = w_top[:, bass.ds(g * 2 + i, 1), k:k + 1].rearrange("p o k -> p (o k)")
                        ins = nc.vector.scalar_tensor_tensor(row, gath[:, i, k, :], wk, row, ALU.mult, ALU.add)
                        if k < TOPK - 1:
                            ins.then_inc(dve_step, 1)
                            dve.wait_ge(dve_step, g * (2 * (TOPK - 1)) + (steps[0] + i * (TOPK - 1) + k + 1))
                    ins.then_inc(combined, 1)
                    dve.wait_ge(combined, g * 2 + (i + 1))
                    dve.sem_inc(gath_free, 1)

        @block.tensor
        def _(pe):
            def matmul3(o, a_hi, a_lo, b_hi, b_lo, start, stop):
                nc.tensor.matmul(o, a_hi, b_hi, start=start, stop=False)
                nc.tensor.matmul(o, a_hi, b_lo, start=False, stop=False)
                return nc.tensor.matmul(o, a_lo, b_hi, start=False, stop=stop)

            def mod_columns(o, first):
                for n in range(2 * DC):
                    for ch in range(DC):
                        at = (first + n) * P
                        last = nc.tensor.matmul(o[:, n:n + 1], wmod_sb[:, ch, at:at + P], sc_col[:, ch:ch + 1],
                                                start=ch == 0, stop=ch == DC - 1)
                last.then_inc(mod_mm, 1)

            def mod_rows(o, first):
                for ch in range(DC):
                    last = nc.tensor.matmul(o[:], sc_bc[:, ch, :], wmod_sb[:, ch, first * P:first * P + D],
                                            start=ch == 0, stop=ch == DC - 1)
                last.then_inc(mod_mm, 1)

            def ln_turn(base, b, src):
                for ch in range(DC):
                    if b >= 1:
                        pe.wait_ge(ln_mod, base + DC * (b - 1) + ch + 1)
                    for t in range(TB):
                        if ch == 0:
                            pe.wait_ge(ln_norm, base + TB * b + t + 1)
                        last = nc.tensor.transpose(strip[ch][:, P * t:P * t + P], src[:, b % 2, t, P * ch:P * ch + P],
                                                   ident[:])
                    last.then_inc(ln_turned, 1)

            pe.wait_ge(consts, 4)
            pe.wait_ge(c_step, 5)
            pe.wait_ge(mod1_landed, 16)
            mod_columns(pv, 0)
            for b in range(QB):
                ln_turn(0, b, n1)
            pe.wait_ge(rows_landed, 48)
            nc.tensor.transpose(gen[0][:, 0:3 * H], bias_rows[:], ident[0:3 * H, 0:3 * H]).then_inc(mod_mm, 1)
            pe.wait_ge(mod2_landed, 16)
            mod_rows(strip[4], 2 * DC)
            mod_rows(gen[1], 5 * DC)
            pe.wait_ge(mod_out, 1)
            mod_columns(pv, 3 * DC)
            pe.wait_ge(ln_split, NT)

            def project(n, kind, j, h):
                u = G[kind, j, 0]
                pe.wait_ge(gen_out, h * NG + (u + 1))
                if j == 0:
                    pe.wait_ge(w_split, h * 4 + (n + 1))
                for ch in range(DC):
                    cols = slice(512 * j, 512 * j + 512)
                    last = matmul3(gen[u % GENS][:], w_hi_t[n][:, ch, :], w_lo_t[n][:, ch, :],
                                   hT_hi[:, ch, cols], hT_lo[:, ch, cols], ch == 0, ch == DC - 1)
                last.then_inc(gen_done, 1)

            def out_project(u, t):
                last = matmul3(gen[u % GENS][:], at_hi[:, P * t:P * t + P], at_lo[:, P * t:P * t + P],
                               w_hi_t[3][:].rearrange("p c d -> p (c d)"), w_lo_t[3][:].rearrange("p c d -> p (c d)"),
                               True, True)
                last.then_inc(gen_done, 1)

            def outs(j, h):
                pe.wait_ge(attn_split, h * QB + (1 if j == QB - 1 else j + 2))
                if j < QB - 1:
                    pe.wait_ge(w_split, h * 4 + 4)
                for t in range(TB):
                    u = G["o", j, t]
                    pe.wait_ge(gen_out, h * NG + (u + 1))
                    out_project(u, t)

            def turn_values(j, h):
                u = G["t", j, 0]
                pe.wait_ge(gen_out, h * NG + (u + 1))
                pe.wait_ge(gen_out, h * NG + (GENS + G["v", j, 0] + 1))
                for t in range(TB):
                    last = nc.tensor.transpose(gen[u % GENS][:, P * t:P * t + P], vT_f[:, P * t:P * t + P], ident[:])
                last.then_inc(gen_done, 1)

            def score(j, h):
                pe.wait_ge(gen_out, h * NG + (GENS + G["k", j, 0] + 1))
                for n, (t, ch, w) in enumerate(score_units(j)):
                    u = strips_before(j) + n
                    pe.wait_ge(strip_out, h * NSTRIP + (u + 1))
                    o = strip[u % STRIPS]
                    rows, cols = slice(P * t, P * t + P), slice(512 * ch, 512 * ch + w)
                    last = matmul3(o[:, 0:w], qT_hi[:, rows], qT_lo[:, rows], kT_hi[:, cols], kT_lo[:, cols],
                                   True, True)
                    if ch == j:
                        last = nc.tensor.matmul(o[:, w - P:w], ident_bf[:], mask_bf[:], start=False, stop=True,
                                                skip_group_check=True)
                    last.then_inc(strip_done, 1)

            def turn_and_sum(j, h):
                n = units(j)
                pe.wait_ge(row_probs, h * NT + TB * (j + 1))
                ahead = PTS - 1

                def turn(kk):
                    u = strips_before(j) + n + kk
                    pe.wait_ge(strip_out, h * NSTRIP + (u + 1))
                    for t in range(first_col(j, kk) // P, TB):
                        at = row_at[t] + P * kk
                        last = nc.tensor.transpose(strip[u % STRIPS][:, P * t:P * t + P], probs[:, at:at + P], ident[:])
                    last.then_inc(strip_done, 1)

                def sum_values(kk):
                    u = strips_before(j) + n + kk
                    pe.wait_ge(strip_out, h * NSTRIP + (STRIPS + u + 1))
                    if kk == 0 or kk == TB * j:
                        pe.wait_ge(gen_out, h * NG + (GENS + G["t", kk // TB, 0] + 1))
                    c0 = first_col(j, kk)
                    last = matmul3(pv[:, c0:512], v_hi[:, kk, :], v_lo[:, kk, :], pT_hi[:, kk % PTS, c0:512],
                                   pT_lo[:, kk % PTS, c0:512], kk == 0, kk == n - 1)
                    last.then_inc(pv_done, 1)

                for kk in range(n + ahead):
                    if kk < n:
                        turn(kk)
                    if kk >= ahead:
                        sum_values(kk - ahead)

            with pe.Fori(0, H) as h:
                for n, kind in enumerate("qkv"):
                    project(n, kind, 0, h)
                outs(QB - 1, h)
                turn_values(0, h)
                score(0, h)
                for j in range(1, QB):
                    for n, kind in enumerate("qkv"):
                        project(n, kind, j, h)
                    if j >= 2:
                        outs(j - 2, h)
                    turn_and_sum(j - 1, h)
                    turn_values(j, h)
                    score(j, h)
                outs(QB - 2, h)
                turn_and_sum(QB - 1, h)
            pe.wait_ge(attn_split, QB * H + 1)
            for t in range(TB):
                u = NG * H + t
                pe.wait_ge(gen_out, u + 1)
                out_project(u, t)

            for b in range(QB):
                ln_turn(NT, b, n2)
            pe.wait_ge(gen_out, GENS + NG * H + TB)
            pe.wait_ge(wr_landed, 16)
            pe.wait_ge(ln_mod, 2 * NT)
            half = NT // 2
            for s in range(2):
                for t in range(half):
                    for ch in range(DC):
                        at = P * (half * s + t)
                        last = nc.tensor.matmul(gen[s][:, E * t:E * t + E], h2T[:, ch, at:at + P], wr_sb[:, ch, :],
                                                start=ch == 0, stop=ch == DC - 1)
                last.then_inc(logits_mm, 1)

            def shared(n):
                for ch in range(SC):
                    u = n * SC + ch
                    if u >= 2:
                        pe.wait_ge(hs_ready, u - 1)
                    for o, w in ((strip[2 * (ch % 2)], sg_sb), (strip[2 * (ch % 2) + 1], su_sb)):
                        for c in range(DC):
                            last = nc.tensor.matmul(o[:], w[:, c, P * ch:P * ch + P], h2T[:, c, 512 * n:512 * n + 512],
                                                    start=c == 0, stop=c == DC - 1)
                    last.then_inc(gu_done, 1)
                pe.wait_ge(hs_ready, n * SC + SC)
                for t in range(TB):
                    v = n * TB + t
                    if v >= 2:
                        pe.wait_ge(down_out, v - 1)
                    o = strip[4] if t % 2 == 0 else pv
                    for ch in range(SC):
                        last = nc.tensor.matmul(o[:], hs[:, ch, P * t:P * t + P], sd_sb[:, ch, :],
                                                start=ch == 0, stop=ch == SC - 1)
                    last.then_inc(down_done, 1)

            pe.wait_ge(sw_landed, 16 * 3 * NS)
            pe.wait_ge(sd_scaled, SC)
            pe.wait_ge(picked_ready, 1)
            for s in range(2):
                mine = slice(half * s, half * s + half)
                last = nc.tensor.matmul(gen[s][:], tri_bf[:], picked[:, mine, :].rearrange("p t e -> p (t e)"),
                                        start=True, stop=True)
                for j in range(half * s + half - 1):
                    first = max(j + 1, half * s)
                    n = half * s + half - first
                    last = nc.tensor.matmul(gen[s][:, E * (first - half * s):512]
                                            .rearrange("p (t e) -> p t e", e=E), ones_bf[:],
                                            picked[:, j:j + 1, :].to_broadcast([P, n, E]), start=False,
                                            stop=True, skip_group_check=True)
                last.then_inc(pos_mm, 1)
            for n in range(2):
                shared(n)

            def expert_turn(i, g):
                pe.wait_ge(xb_landed[i], g * 16 + 16)
                for ch in range(DC):
                    last = nc.tensor.transpose(gen[i % 2][:, P * ch:P * ch + P], xb[:, i, P * ch:P * ch + P], ident[:])
                last.then_inc(xb_turned, 1)

            def expert_gate_up(i, g):
                pe.wait_ge(xbT_ready, g * EX + (i + 1))
                pe.wait_ge(e_landed[i], g * 48 + 48)
                for o, w in ((strip[2 * (i % 2)], wg_sb), (strip[2 * (i % 2) + 1], wu_sb)):
                    for c in range(DC):
                        last = nc.tensor.matmul(o[:, 0:P], w[:, i, c, :], xbT[:, i % 2, P * c:P * c + P],
                                                start=c == 0, stop=c == DC - 1)
                last.then_inc(e_gu, 1)

            def expert_down(i, g):
                pe.wait_ge(e_h, g * EX + (i + 1))
                pe.wait_ge(yb_ready, g * EX + (EX + i - 1))
                o = strip[4] if i % 2 == 0 else pv
                nc.tensor.matmul(o[:], hE[:, i % 2, :], wd_sb[:, i, :], start=True, stop=True).then_inc(e_down, 1)

            pe.wait_ge(down_out, 2 * TB)
            pe.wait_ge(pos_mm, 2)
            pe.wait_ge(routed, 1)
            with pe.Fori(0, E // EX) as g:
                expert_turn(0, g)
                for i in range(EX):
                    if i + 1 < EX:
                        expert_turn(i + 1, g)
                    expert_gate_up(i, g)
                    if i >= 1:
                        expert_down(i - 1, g)
                expert_down(EX - 1, g)
            pe.wait_ge(yb_ready, EX + E)
            for n in range(2, QB):
                shared(n)


_INS = ["L0_attn_x", "L0_attn_Q_w", "L0_attn_Q_b", "L0_attn_K_w", "L0_attn_K_b", "L0_attn_V_w", "L0_attn_V_b",
        "L0_attn_O_w", "L0_attn_O_b", "L0_ffn_Wr", "L0_ffn_router_bias", "L0_ffn_Wg", "L0_ffn_Wu", "L0_ffn_Wd",
        "L0_ffn_Sg", "L0_ffn_Su", "L0_ffn_Sd", "L0_c", "L0_wmod"]


def kernel(**inputs):
    import concourse.bacc as bacc
    from concourse.bass_utils import run_bass_kernel_spmd

    nc = bacc.Bacc("TRN2", target_bir_lowering=False, num_devices=1)
    arrays, args = {}, []
    for name in _INS:
        arr = np.ascontiguousarray(inputs[name])
        arrays[f"in_{name}"] = arr
        args.append(nc.dram_tensor(f"in_{name}", arr.shape, mybir.dt.from_np(arr.dtype), kind="ExternalInput").ap())
    shape = inputs["L0_attn_x"].shape
    args.append(nc.dram_tensor("out_y", shape, F32, kind="ExternalOutput").ap())
    adaln_block(nc, *args)
    r = run_bass_kernel_spmd(nc, [arrays], core_ids=[0])
    return r.results[0]["out_y"]
```

```python
from contextlib import ExitStack

import numpy as np
import concourse.bass as bass
from concourse import mybir

F32 = mybir.dt.float32
F32R = mybir.dt.float32r
BF16 = mybir.dt.bfloat16
I32 = mybir.dt.int32
U32 = mybir.dt.uint32
ALU = mybir.AluOpType
ACT = mybir.ActivationFunctionType
AX_X = mybir.AxisListType.X
P = 128


class SbufMap:

    def __init__(self, nc, at):
        self.nc, self.at = nc, at

    def place(self, name, shape, dtype):
        size = int(np.prod(shape[1:])) * (2 if dtype == BF16 else 4)
        t = self.nc.alloc_sbuf_tensor_at(name, list(shape), dtype, offset=self.at)
        self.at += (size + 31) // 32 * 32
        return t


def adaln_block(nc, x, Q_w, Q_b, K_w, K_b, V_w, V_b, O_w, O_b, Wr, router_bias, Wg, Wu, Wd, Sg, Su, Sd,
                c_in, wmod, out):
    _, S, D = x.shape
    H, _, DH = Q_w.shape
    E, _, HE = Wg.shape
    NS, _, HS = Sg.shape
    TOPK = 4
    CAP = 128
    NT = S // P
    DC = D // P
    QB = S // 512
    TB = 4
    SC = NS * HS // P
    EPS = 1e-5
    SCALE = float(DH) ** -0.5
    MASKED = -1e5 / SCALE
    TRASH = E * CAP
    assert DH == P and HE == P and D == 512 and CAP == P

    n2_dram = nc.dram_tensor("n2_dram", [S, D], F32, kind="Internal").ap()
    table_dram = nc.dram_tensor("table_dram", [TRASH + S * TOPK, 1], I32, kind="Internal").ap()
    yb_dram = nc.dram_tensor("yb_dram", [E * CAP, D], F32, kind="Internal").ap()

    with ExitStack() as ctx:
        def sem(name):
            return ctx.enter_context(nc.semaphore(name))

        def bank(name):
            return ctx.enter_context(nc.psum_tensor(name, [P, 512], F32))

        STRIPS, GENS, PTS = 5, 2, 3
        AHEAD = PTS - 1
        strip = [bank(f"strip{i}") for i in range(STRIPS)]
        gen = [bank(f"gen{i}") for i in range(GENS)]
        pv = bank("pv")

        base = (nc.sbuf_base + 63) // 64 * 64
        keep = SbufMap(nc, base)
        acc = keep.place("acc", [P, NT, D], F32)
        ident = keep.place("ident", [P, P], F32)
        ident_bf = keep.place("ident_bf", [P, P], BF16)
        mask_bf = keep.place("mask_bf", [P, P], BF16)
        modT = keep.place("modT", [P, 6 * DC], F32)
        scale_a = keep.place("scale_a", [P, DC], F32)
        scale_b = keep.place("scale_b", [P, DC], F32)
        ga_bc = keep.place("ga_bc", [P, D], F32)
        gb_bc = keep.place("gb_bc", [P, D], F32)
        biasT = keep.place("biasT", [P, 3 * H], F32)
        bias_now = keep.place("bias_now", [P, 3], F32)
        stats = keep.place("stats", [P, NT, 6], F32)
        meanvar = keep.place("meanvar", [P, NT, 2], F32)
        rstd = keep.place("rstd", [P, NT], F32)
        veps = keep.place("veps", [P, NT], F32)
        neghalf = keep.place("neghalf", [P, NT], F32)
        cmax = keep.place("cmax", [P, TB, QB], F32)
        nbias = keep.place("nbias", [P, TB], F32)
        rsum = keep.place("rsum", [P, NT], F32)
        rinv = keep.place("rinv", [P, NT], F32)
        c_col = keep.place("c_col", [P, DC], F32)
        c_exp = keep.place("c_exp", [P, DC], F32)
        c_sig = keep.place("c_sig", [P, DC], F32)
        sc_col = keep.place("sc_col", [P, DC], F32)

        a = SbufMap(nc, keep.at)
        hT_hi = a.place("hT_hi", [P, DC, S], F32R)
        hT_lo = a.place("hT_lo", [P, DC, S], F32R)
        w_hi_t = [a.place(f"w{n}_hi", [P, DC, P], F32R) for n in "qkvo"]
        w_lo_t = [a.place(f"w{n}_lo", [P, DC, P], F32R) for n in "qkvo"]
        raw = [a.place(f"w{n}_raw", [P, DC, P], F32) for n in ("q", "k", "vo")]
        raw.append(raw[2])
        at_hi = a.place("at_hi", [P, 512], F32R)
        at_lo = a.place("at_lo", [P, 512], F32R)
        overlaid = a.at
        qT_hi = a.place("qT_hi", [P, 512], F32R)
        qT_lo = a.place("qT_lo", [P, 512], F32R)
        vT_f = a.place("vT_f", [P, 512], F32)
        row_at = [sum((NT - TB + q + 1) * P for q in range(r)) for r in range(TB + 1)]
        probs = a.place("probs", [P, row_at[TB]], F32)
        pT_hi = a.place("pT_hi", [P, PTS, 512], F32R)
        pT_lo = a.place("pT_lo", [P, PTS, 512], F32R)
        kT_hi = a.place("kT_hi", [P, S], F32R)
        kT_lo = a.place("kT_lo", [P, S], F32R)
        v_hi = a.place("v_hi", [P, NT, P], F32R)
        v_lo = a.place("v_lo", [P, NT, P], F32R)
        assert a.at <= nc.sbuf_usable_end, a.at
        pre = SbufMap(nc, overlaid)
        n1 = pre.place("n1", [P, 2, TB, D], F32)
        h_tmp = pre.place("h_tmp", [P, DC, 512], F32)
        wmod_sb = pre.place("wmod_sb", [P, DC, 6 * D], F32)
        sc_bc = pre.place("sc_bc", [P, DC, P], F32)
        gate_sgn, gate_mag = n1[:, 0, 0, :], n1[:, 0, 1, :]
        ob_bc = pre.place("ob_bc", [P, D], F32)
        bias_rows = pre.place("bias_rows", [3 * H, P], F32)
        assert pre.at <= a.at - D * 4, pre.at
        gob = SbufMap(nc, a.at - D * 4).place("gob", [P, D], F32)

        f = SbufMap(nc, keep.at)
        sg_sb = f.place("sg_sb", [P, DC, NS * HS], F32)
        su_sb = f.place("su_sb", [P, DC, NS * HS], F32)
        sd_sb = f.place("sd_sb", [P, SC, D], F32)
        wr_sb = f.place("wr_sb", [P, DC, E], F32)
        rb_bc = f.place("rb_bc", [P, E], F32)
        zeros_i = f.place("zeros_i", [P, E], I32)
        EX = 4
        assert f.at <= overlaid
        h2T = f.place("h2T", [P, DC, S], F32)
        wg_sb = f.place("wg_sb", [P, EX, DC, HE], F32)
        wu_sb = f.place("wu_sb", [P, EX, DC, HE], F32)
        wd_sb = f.place("wd_sb", [P, EX, D], F32)
        xb = f.place("xb", [P, EX, D], F32)
        xbT = f.place("xbT", [P, 2, D], F32)
        sil_e = f.place("sil_e", [P, 2, P], F32)
        hE = f.place("hE", [P, 2, P], F32)
        yb = f.place("yb", [P, EX, D], F32)
        sil_s = f.place("sil_s", [P, 2, 512], F32)
        w_top = f.place("w_top", [P, NT, TOPK], F32)
        slot_u = f.place("slot_u", [P, NT, TOPK], U32)
        scat_u = f.place("scat_u", [P, NT, TOPK], U32)
        tok_i = f.place("tok_i", [P, NT], I32)
        trash_i = f.place("trash_i", [P, NT, TOPK], I32)
        iota_i = f.place("iota_i", [P, E], I32)
        table = f.place("table", [P, E], I32)
        tri_bf = f.place("tri_bf", [P, P], BF16)
        ones_bf = f.place("ones_bf", [P, P], BF16)
        slot_now = f.place("slot_now", [P, 2, TOPK], U32)
        tok_now = f.place("tok_now", [P, EX], I32)
        shared_at = f.at
        n2 = f.place("n2", [P, 2, TB, D], F32)
        hs = f.place("hs", [P, SC, 512], F32)
        assert f.at <= nc.sbuf_usable_end, f.at
        r = SbufMap(nc, shared_at)
        scores = r.place("scores", [P, NT, E], F32)
        onehot = [r.place(f"onehot{k}", [P, NT, E], BF16) for k in range(TOPK)]
        picked = r.place("picked", [P, NT, E], BF16)
        pos = r.place("pos", [P, NT, E], F32)
        prod = r.place("prod", [P, NT, E], F32)
        r_stat = [r.place(f"r_stat{n}", [P, NT], F32) for n in range(4)]
        vals = r.place("vals", [P, NT, 8], F32)
        idx = r.place("idx", [P, NT, 8], U32)
        idx_f = r.place("idx_f", [P, NT, TOPK], F32)
        pos_k = r.place("pos_k", [P, NT, TOPK], F32)
        valid = r.place("valid", [P, NT, TOPK], F32)
        r_tmp = [r.place(f"r_tmp{n}", [P, NT, TOPK], F32) for n in range(3)]
        iota_f = r.place("iota_f", [P, E], F32)
        assert r.at <= nc.sbuf_usable_end, r.at
        g_ = SbufMap(nc, shared_at)
        gath = g_.place("gath", [P, 2, TOPK, D], F32)
        assert g_.at <= shared_at + 2 * TB * D * 4, g_.at

        c_landed, mod1_landed, mod2_landed = sem("c_landed"), sem("mod1_landed"), sem("mod2_landed")
        x_landed = [sem(f"x_landed{b}") for b in range(QB)]
        rows_landed, ob_landed = sem("rows_landed"), sem("ob_landed")
        raw_landed = [sem(f"raw_landed_{n}") for n in "qkvo"]
        consts = sem("consts")
        c_step = sem("c_step")
        c_act = sem("c_act")
        mod_mm, mod_out = sem("mod_mm"), sem("mod_out")
        dve_step = sem("dve_step")
        pool_step = sem("pool_step")
        pool_waited = sem("pool_waited")
        ln_stats, ln_rstd, ln_norm = sem("ln_stats"), sem("ln_rstd"), sem("ln_norm")
        ln_turned, ln_mod, ln_split = sem("ln_turned"), sem("ln_mod"), sem("ln_split")
        resid = sem("resid")
        w_hi, w_split, wo_scaled = sem("w_hi"), sem("w_split"), sem("wo_scaled")
        bias_ready = sem("bias_ready")
        gen_done, gen_hi, gen_out = sem("gen_done"), sem("gen_hi"), sem("gen_out")
        strip_done, strip_out = sem("strip_done"), sem("strip_out")
        row_logits, row_probs = sem("row_logits"), sem("row_probs")
        pt_hi, pv_done = sem("pt_hi"), sem("pv_done")
        attn_hi, attn_split = sem("attn_hi"), sem("attn_split")
        rinv_ready = sem("rinv_ready")
        sw_landed, wr_landed, rb_landed = sem("sw_landed"), sem("wr_landed"), sem("rb_landed")
        sd_scaled = sem("sd_scaled")
        n2_stored = [sem(f"n2_stored{i}") for i in range(2)]
        zero_stored = sem("zero_stored")
        logits_mm, r_shift, r_exp, picked_ready, pos_mm, routed = (
            sem("logits_mm"), sem("r_shift"), sem("r_exp"), sem("picked_ready"), sem("pos_mm"), sem("routed"))
        scattered, table_landed = sem("scattered"), sem("table_landed")
        gu_done, silu_done, hs_ready = sem("gu_done"), sem("silu_done"), sem("hs_ready")
        down_done, down_out = sem("down_done"), sem("down_out")
        e_landed = [sem(f"e_landed{i}") for i in range(EX)]
        xb_landed = [sem(f"xb_landed{i}") for i in range(EX)]
        tok_ready = sem("tok_ready")
        xb_turned, xbT_ready = sem("xb_turned"), sem("xbT_ready")
        e_gu, e_silu, e_h = sem("e_gu"), sem("e_silu"), sem("e_h")
        e_down, yb_ready = sem("e_down"), sem("yb_ready")
        yb_stored = [sem(f"yb_stored{i}") for i in range(EX)]
        slot_ready = sem("slot_ready")
        g_landed = [sem(f"g_landed{i}") for i in range(2)]
        gath_free, combined = sem("gath_free"), sem("combined")
        row_final = sem("row_final")
        out_stored = sem("out_stored")

        order = []
        for j in range(QB):
            order += [("t", j, 0)] + [(kind, (j + 1) % QB, 0) for kind in "qkv"]
            order += [("o", (j - 1) % QB, t) for t in range(TB)]
        NG = len(order)
        G = {u: n for n, u in enumerate(order)}
        HI = {u: n for n, u in enumerate([u for u in order if u[0] in "qkt"])}
        NHI = len(HI)
        G_PRE, HI_PRE = NG - G["q", 0, 0], NHI - HI["q", 0, 0]

        def nth(kind, j, t, h):
            return h * NG + (G_PRE + G[kind, j, t] + 1)

        def nth_hi(kind, j, h):
            return h * NHI + (HI_PRE + HI[kind, j, 0] + 1)

        def bank_of(kind, j, t):
            return gen[G[kind, j, t] % GENS]

        OUTS_END = NG * H + G_PRE

        def units(j):
            return TB * (j + 1)

        def strips_before(j):
            return sum(2 * units(i) for i in range(j))

        def turned_before(j):
            return sum(units(i) for i in range(j))

        NSTRIP, NTURN = strips_before(QB), turned_before(QB)
        assert NG % GENS == 0 and NSTRIP % STRIPS == 0

        def score_units(j):
            return [(t, ch, 512 if ch < j else (t + 1) * P) for t in range(TB) for ch in range(j + 1)]

        def first_col(j, kk):
            return max(0, kk - TB * j) * P

        block = ctx.enter_context(nc.Block())

        @block.sync
        def _(sp):
            sp.dma_start(c_col[:], c_in.rearrange("o (c p) -> p (o c)", p=P),
                         allow_slow_non_contiguous=True).then_inc(c_landed, 16)
            wm = wmod.rearrange("(c p) n -> p c n", p=P)
            xt = x.rearrange("o (t p) d -> p (o t) d", p=P)
            w_dram = [w.rearrange("h (c p) d -> h p c d", p=P) for w in (Q_w, K_w, V_w)]
            w_dram.append(O_w.rearrange("h p (c d) -> h p c d", d=P))

            def load_x(b):
                sp.dma_start(acc[:, TB * b:TB * b + TB, :], xt[:, TB * b:TB * b + TB, :]).then_inc(x_landed[b], 16)

            load_x(0)
            sp.dma_start(wmod_sb[:, :, 0:2 * D], wm[:, :, 0:2 * D]).then_inc(mod1_landed, 16)
            for b in range(1, QB):
                load_x(b)
            for n, bias in enumerate((Q_b, K_b, V_b)):
                sp.dma_start(bias_rows[H * n:H * n + H, :], bias).then_inc(rows_landed, 16)
            sp.dma_start(ob_bc[:], O_b.partition_broadcast(P)).then_inc(ob_landed, 16)
            for n in range(3):
                sp.dma_start(raw[n][:], w_dram[n][0]).then_inc(raw_landed[n], 16)
            sp.dma_start(wmod_sb[:, :, 2 * D:6 * D], wm[:, :, 2 * D:6 * D]).then_inc(mod2_landed, 16)
            sp.wait_ge(w_split, 3)
            sp.dma_start(raw[3][:], w_dram[3][0]).then_inc(raw_landed[3], 16)
            with sp.Fori(0, H - 1) as h:
                for n in range(4):
                    sp.wait_ge(w_split, h * 4 + (1, 2, 4, 7)[n])
                    sp.dma_start(raw[n][:], w_dram[n][bass.ds(h + 1, 1)].rearrange("o p c d -> (o p) c d")
                                 ).then_inc(raw_landed[n], 16)
            sp.wait_ge(gen_done, nth("v", QB - 1, 0, H - 1))
            sp.dma_start(wr_sb[:], Wr.rearrange("(c p) e -> p c e", p=P)).then_inc(wr_landed, 16)
            sp.dma_start(rb_bc[:], router_bias.partition_broadcast(P)).then_inc(rb_landed, 16)
            for dst, src in ((sg_sb, Sg), (su_sb, Su)):
                for s in range(NS):
                    sp.dma_start(dst[:, :, HS * s:HS * s + HS], src[s].rearrange("(c p) h -> p c h", p=P)
                                 ).then_inc(sw_landed, 16)
            for s in range(NS):
                sp.dma_start(sd_sb[:, SC // NS * s:SC // NS * (s + 1), :], Sd[s].rearrange("(c p) d -> p c d", p=P)
                             ).then_inc(sw_landed, 16)
            sp.wait_ge(consts, 5)
            sp.dma_start(table_dram[0:TRASH, :].rearrange("(p e) o -> p (e o)", p=P), zeros_i[:]
                         ).then_inc(zero_stored, 16)
            n2v = n2_dram.rearrange("(b t p) d -> b p t d", p=P, t=TB)
            for b in range(QB):
                sp.wait_ge(ln_norm, NT + TB * b + TB)
                sp.dma_start(n2v[b], n2[:, b % 2]).then_inc(n2_stored[b % 2], 16)
            wg_dram, wu_dram = (w.rearrange("e (c p) h -> e p c h", p=P) for w in (Wg, Wu))

            def load_expert(i, e):
                for dst, src in ((wg_sb, wg_dram), (wu_sb, wu_dram)):
                    sp.dma_start(dst[:, i, :, :], src[bass.ds(e, 1)].rearrange("o p c h -> (o p) c h")
                                 ).then_inc(e_landed[i], 16)
                sp.dma_start(wd_sb[:, i, :], Wd[bass.ds(e, 1)].rearrange("o p d -> (o p) d")).then_inc(e_landed[i], 16)

            for i in range(EX):
                load_expert(i, i)
            sp.wait_ge(scattered, 16 * NT * TOPK)
            sp.dma_start(table[:], table_dram[0:TRASH, :].rearrange("(s e) o -> s (e o)", e=E)
                         ).then_inc(table_landed, 16)
            ybv = yb_dram.rearrange("(e s) d -> e s d", s=CAP)

            def store_yb(i, g):
                sp.wait_ge(yb_ready, g * EX + (EX + i + 1))
                sp.dma_start(ybv[bass.ds(g * EX + i, 1)].rearrange("o s d -> (o s) d"), yb[:, i, :]
                             ).then_inc(yb_stored[i], 16)

            with sp.Fori(0, E // EX - 1) as g:
                for i in range(EX):
                    sp.wait_ge(e_down, g * EX + (i + 1))
                    load_expert(i, g * EX + (EX + i))
                    store_yb(i, g)
            for i in range(EX):
                store_yb(i, E // EX - 1)
            ov = out.rearrange("o (t p) d -> (o t) p d", p=P)
            done = 0
            for first, last in ((NT // 2, NT - TB), (0, NT // 2), (NT - TB, NT)):
                with sp.Fori(first, last) as t:
                    sp.wait_ge(row_final, t + (done - first + 1))
                    sp.dma_start(ov[bass.ds(t, 1)].rearrange("o p d -> (o p) d"), acc[:, bass.ds(t, 1), :]
                                 .rearrange("p o d -> p (o d)")).then_inc(out_stored, 16)
                done += last - first
            sp.wait_ge(out_stored, 16 * NT)

        @block.gpsimd
        def _(pool):
            steps = [0]

            def link(ins):
                steps[0] += 1
                ins.then_inc(pool_step, 1)
                pool.wait_ge(pool_step, steps[0])

            def wait_alone(semaphore, value):
                pool.wait_ge(semaphore, value)
                pool.sem_inc(pool_waited, 1)

            link(nc.gpsimd.memset(ident[:], 0.0))
            nc.gpsimd.affine_select(out=ident[:], in_=ident[:], compare_op=ALU.not_equal, fill=1.0, base=0,
                                    pattern=[[-1, P]], channel_multiplier=1).then_inc(consts, 1)
            link(nc.gpsimd.memset(ident_bf[:], 0.0))
            nc.gpsimd.affine_select(out=ident_bf[:], in_=ident_bf[:], compare_op=ALU.not_equal, fill=1.0, base=0,
                                    pattern=[[-1, P]], channel_multiplier=1).then_inc(consts, 1)
            link(nc.gpsimd.memset(mask_bf[:], 0.0))
            nc.gpsimd.affine_select(out=mask_bf[:], in_=mask_bf[:], compare_op=ALU.is_ge, fill=MASKED, base=0,
                                    pattern=[[-1, P]], channel_multiplier=1).then_inc(consts, 1)
            nc.gpsimd.memset(neghalf[:], -0.5).then_inc(consts, 1)

            def ln_scales(base, b):
                pool.wait_ge(ln_stats, base + TB * b + TB)
                tiles = slice(TB * b, TB * b + TB)
                link(nc.gpsimd.tensor_scalar(veps[:, tiles], meanvar[:, tiles, 1], EPS, None, ALU.add))
                nc.gpsimd.tensor_tensor(rstd[:, tiles], veps[:, tiles], neghalf[:, tiles], ALU.pow
                                        ).then_inc(ln_rstd, 1)

            pool.wait_ge(consts, 4)
            for b in range(QB):
                ln_scales(0, b)
            for b in range(QB):
                for ch in range(DC):
                    pool.wait_ge(ln_mod, DC * b + ch + 1)
                    cols = slice(512 * b, 512 * b + 512)
                    nc.gpsimd.tensor_tensor(hT_lo[:, ch, cols], h_tmp[:, ch, :], hT_hi[:, ch, cols].bitcast(F32),
                                            ALU.subtract).then_inc(ln_split, 1)

            def split_lo(n, h):
                pool.wait_ge(w_hi, h * 4 + (n + 1))
                nc.gpsimd.tensor_tensor(w_lo_t[n][:], raw[n][:], w_hi_t[n][:].bitcast(F32), ALU.subtract
                                        ).then_inc(w_split, 1)

            def take_bias(h):
                src = biasT[:].rearrange("p (n h) -> p n h", n=3)[:, :, bass.ds(h, 1)].rearrange("p n o -> p (n o)")
                nc.gpsimd.tensor_copy(bias_now[:], src).then_inc(bias_ready, 1)

            def scale_wo(h):
                pool.wait_ge(raw_landed[3], h * 16 + 16)
                nc.gpsimd.tensor_tensor(raw[3][:].rearrange("p c d -> p (c d)"), raw[3][:].rearrange("p c d -> p (c d)"),
                                        ga_bc[:], ALU.mult).then_inc(wo_scaled, 1)

            for n in range(3):
                split_lo(n, 0)
            pool.wait_ge(mod_out, 2)
            nc.gpsimd.tensor_copy(bias_now[:], biasT[:].rearrange("p (n h) -> p n h", n=3)[:, :, 0]
                                  ).then_inc(bias_ready, 1)
            pool.wait_ge(mod_out, 3)
            pool.wait_ge(ob_landed, 16)
            pool.wait_ge(ln_norm, NT)
            link(nc.gpsimd.tensor_tensor(gob[:], ga_bc[:], ob_bc[:], ALU.mult))
            for t in list(range(NT - TB, NT)) + list(range(NT - TB)):
                nc.gpsimd.tensor_tensor(acc[:, t, :], acc[:, t, :], gob[:], ALU.add).then_inc(resid, 1)

            with pool.Fori(0, H - 1) as h:
                scale_wo(h)
                split_lo(3, h)
                split_lo(0, h + 1)
                split_lo(1, h + 1)
                split_lo(2, h + 1)
                take_bias(h + 1)
            scale_wo(H - 1)
            split_lo(3, H - 1)

            pool.wait_ge(gen_done, nth("v", QB - 1, 0, H - 1))
            nc.gpsimd.memset(zeros_i[:], 0).then_inc(consts, 1)
            pool.wait_ge(sw_landed, 16 * 3 * NS)
            for ch in range(SC):
                nc.gpsimd.tensor_tensor(sd_sb[:, ch, :], sd_sb[:, ch, :], gb_bc[:], ALU.mult).then_inc(sd_scaled, 1)
            pool.wait_ge(gen_out, GENS + OUTS_END + TB)
            link(nc.gpsimd.memset(tri_bf[:], 0.0))
            nc.gpsimd.affine_select(out=tri_bf[:], in_=tri_bf[:], compare_op=ALU.is_ge, fill=1.0, base=0,
                                    pattern=[[-1, P]], channel_multiplier=1).then_inc(consts, 1)
            nc.gpsimd.memset(ones_bf[:], 1.0).then_inc(consts, 1)
            nc.gpsimd.iota(iota_i[:], [[1, E]], base=0, channel_multiplier=0).then_inc(consts, 1)
            nc.gpsimd.iota(tok_i[:], [[P, NT]], base=0, channel_multiplier=1).then_inc(consts, 1)
            nc.gpsimd.iota(trash_i[:], [[P * TOPK, NT], [1, TOPK]], base=TRASH, channel_multiplier=TOPK
                           ).then_inc(consts, 1)
            for b in range(QB):
                ln_scales(NT, b)

            pool.wait_ge(routed, 1)
            pool.wait_ge(zero_stored, 16)
            pool.wait_ge(consts, 10)
            for t in range(NT):
                for k in range(TOPK):
                    nc.gpsimd.indirect_dma_start(
                        out=table_dram, out_offset=bass.IndirectOffsetOnAxis(ap=scat_u[:, t, k:k + 1], axis=0),
                        in_=tok_i[:, t:t + 1], in_offset=None).then_inc(scattered, 16)
            pool.wait_ge(table_landed, 16)
            pool.wait_ge(n2_stored[0], 32)
            pool.wait_ge(n2_stored[1], 32)
            with pool.Fori(0, E // EX) as g:
                for i in range(EX):
                    wait_alone(xb_turned, g * EX + (i + 1))
                    nc.gpsimd.tensor_copy(tok_now[:, i:i + 1], table[:, bass.ds(g * EX + i, 1)]).then_inc(tok_ready, 1)
                    wait_alone(tok_ready, g * EX + (i + 1))
                    nc.gpsimd.indirect_dma_start(
                        out=xb[:, i, :], out_offset=None, in_=n2_dram,
                        in_offset=bass.IndirectOffsetOnAxis(ap=tok_now[:, i:i + 1], axis=0)).then_inc(xb_landed[i], 16)
            for i in range(EX):
                pool.wait_ge(yb_stored[i], 16 * (E // EX + 1))
            def gather_outputs(i, g, done):
                wait_alone(gath_free, g * 2 + (done + i + 1))
                nc.gpsimd.tensor_copy(slot_now[:, i, :], slot_u[:, bass.ds(g * 2 + i, 1), :]
                                      .rearrange("p o k -> p (o k)")).then_inc(slot_ready, 1)
                wait_alone(slot_ready, g * 2 + (done + i + 1))
                for k in range(TOPK):
                    nc.gpsimd.indirect_dma_start(
                        out=gath[:, i, k, :], out_offset=None, in_=yb_dram,
                        in_offset=bass.IndirectOffsetOnAxis(ap=slot_now[:, i, k:k + 1], axis=0)
                    ).then_inc(g_landed[i], 16)

            for first, last, done in ((NT // 4, NT // 2, -NT // 2), (0, NT // 4, NT // 2)):
                with pool.Fori(first, last) as g:
                    for i in range(2):
                        gather_outputs(i, g, done)

        @block.scalar
        def _(act):
            act.wait_ge(c_landed, 16)
            nc.scalar.activation(c_exp[:], c_col[:], ACT.Exp, scale=-1.0).then_inc(c_act, 1)

            act.wait_ge(mod_out, 1)
            for b in range(QB):
                for ch in range(DC):
                    act.wait_ge(ln_turned, DC * b + ch + 1)
                    if b >= 1:
                        act.wait_ge(ln_split, DC * (b - 1) + ch + 1)
                    nc.scalar.activation(hT_hi[:, ch, 512 * b:512 * b + 512], strip[ch][:], ACT.Identity,
                                         bias=modT[:, ch:ch + 1], scale=scale_a[:, ch:ch + 1])
                    nc.scalar.activation(h_tmp[:, ch, :], strip[ch][:], ACT.Identity,
                                         bias=modT[:, ch:ch + 1], scale=scale_a[:, ch:ch + 1]).then_inc(ln_mod, 1)

            def split_hi(n):
                nc.scalar.activation(w_hi_t[n][:], raw[n][:], ACT.Copy).then_inc(w_hi, 1)

            for n in range(3):
                act.wait_ge(raw_landed[n], 16)
                split_hi(n)

            def gen_hi_of(kind, j, h):
                act.wait_ge(gen_done, nth(kind, j, 0, h))
                src = bank_of(kind, j, 0)
                if kind == "q":
                    act.wait_ge(bias_ready, h + (2 if j == 0 else 1))
                    ins = nc.scalar.activation(qT_hi[:], src[:], ACT.Identity, bias=bias_now[:, 0:1])
                elif kind == "k":
                    ins = nc.scalar.activation(kT_hi[:, 512 * j:512 * j + 512], src[:], ACT.Identity,
                                               bias=bias_now[:, 1:2])
                else:
                    ins = nc.scalar.activation(v_hi[:, TB * j:TB * j + TB, :],
                                               src[:].rearrange("p (t d) -> p t d", t=TB), ACT.Copy)
                ins.then_inc(gen_hi, 1)

            def exp_rows(j, h):
                for t in range(TB):
                    act.wait_ge(row_logits, h * NT + (TB * j + t + 1))
                    w = (TB * j + t + 1) * P
                    row = probs[:, row_at[t]:row_at[t] + w]
                    nc.scalar.activation(row, row, ACT.Exp, bias=nbias[:, t:t + 1],
                                         accum_out=rsum[:, TB * j + t:TB * j + t + 1]).then_inc(row_probs, 1)

            def turned_hi(j, h):
                for kk in range(units(j)):
                    u = strips_before(j) + units(j) + kk
                    act.wait_ge(strip_done, h * NSTRIP + (u + 1))
                    if kk >= PTS:
                        act.wait_ge(pv_done, h * NTURN + (turned_before(j) + kk - PTS + 1))
                    c0 = first_col(j, kk)
                    nc.scalar.activation(pT_hi[:, kk % PTS, c0:512], strip[u % STRIPS][:, c0:512], ACT.Copy
                                         ).then_inc(pt_hi, 1)
                act.wait_ge(pv_done, h * NTURN + turned_before(j + 1))
                nc.scalar.activation(at_hi[:], pv[:], ACT.Copy).then_inc(attn_hi, 1)

            def head(h, last):
                for j in range(QB):
                    gen_hi_of("t", j, h)
                    if j == QB - 1 and not last:
                        act.wait_ge(gen_out, nth("v", QB - 1, 0, h) + GENS)
                        for n in range(3):
                            act.wait_ge(raw_landed[n], h * 16 + 32)
                            split_hi(n)
                    exp_rows(j, h)
                    if j < QB - 1 or not last:
                        gen_hi_of("q", (j + 1) % QB, h)
                        gen_hi_of("k", (j + 1) % QB, h)
                    turned_hi(j, h)
                    if j == 0:
                        act.wait_ge(wo_scaled, h + 1)
                        act.wait_ge(gen_done, nth("o", QB - 1, TB - 1, h))
                        split_hi(3)

            act.wait_ge(attn_split, 1)
            gen_hi_of("q", 0, -1)
            gen_hi_of("k", 0, -1)
            with act.Fori(0, H - 1) as h:
                head(h, False)
            head(H - 1, True)

            for b in range(QB):
                for ch in range(DC):
                    act.wait_ge(ln_turned, NT + DC * b + ch + 1)
                    nc.scalar.activation(h2T[:, ch, 512 * b:512 * b + 512], strip[ch][:], ACT.Identity,
                                         bias=modT[:, 3 * DC + ch:3 * DC + ch + 1], scale=scale_b[:, ch:ch + 1]
                                         ).then_inc(ln_mod, 1)
            act.wait_ge(r_shift, 1)
            nc.scalar.activation(scores[:], prod[:], ACT.Exp).then_inc(r_exp, 1)

            def shared_silu(n, b):
                for ch in range(SC):
                    act.wait_ge(gu_done, b * SC + (n + ch + 1))
                    nc.scalar.activation(sil_s[:, ch % 2, :], strip[2 * (ch % 2)][:], ACT.Silu).then_inc(silu_done, 1)

            for b in range(2):
                shared_silu(b * SC, 0)

            def expert_T(i, g):
                act.wait_ge(xb_turned, g * EX + (EX + i + 1))
                for ch in range(DC):
                    ins = nc.scalar.activation(xbT[:, i % 2, P * ch:P * ch + P], gen[i % 2][:, P * ch:P * ch + P],
                                               ACT.Identity, bias=modT[:, 3 * DC + ch:3 * DC + ch + 1],
                                               scale=scale_b[:, ch:ch + 1])
                ins.then_inc(xbT_ready, 1)

            def expert_silu(i, g):
                act.wait_ge(e_gu, g * EX + (i + 1))
                nc.scalar.activation(sil_e[:, i % 2, :], strip[2 * (i % 2)][:, 0:P], ACT.Silu).then_inc(e_silu, 1)

            def experts(g):
                expert_T(0, g)
                for i in range(EX):
                    if i + 1 < EX:
                        expert_T(i + 1, g)
                    expert_silu(i, g)

            with act.Fori(0, E // EX) as g:
                experts(g)
            for b in range(2):
                shared_silu((2 + b) * SC, 0)

        @block.vector
        def _(dve):
            steps = [0]

            def link(ins):
                steps[0] += 1
                ins.then_inc(dve_step, 1)
                dve.wait_ge(dve_step, steps[0])

            for t in (at_hi, at_lo):
                nc.vector.memset(t[:].bitcast(F32), 0.0).then_inc(c_step, 1)
            for t in (w_hi_t[3], w_lo_t[3]):
                nc.vector.memset(t[:].bitcast(F32), 0.0).then_inc(c_step, 1)
            nc.vector.memset(rinv[:], 0.0).then_inc(rinv_ready, 1)

            dve.wait_ge(c_act, 1)
            link(nc.vector.tensor_scalar(c_sig[:], c_exp[:], 1.0, None, ALU.add))
            link(nc.vector.reciprocal(c_sig[:], c_sig[:]))
            link(nc.vector.tensor_tensor(sc_col[:], c_col[:], c_sig[:], ALU.mult))
            nc.vector.tensor_copy(sc_bc[:], sc_col[:].unsqueeze(2).to_broadcast([P, DC, P])).then_inc(c_step, 1)

            def ln_stat(base, b):
                for t in range(TB * b, TB * b + TB):
                    ins = nc.vector.bn_stats(stats[:, t, :], acc[:, t, :])
                    if t < TB * b + TB - 1:
                        steps[0] += 1
                        ins.then_inc(dve_step, 1)
                    else:
                        link(ins)
                for t in range(TB * b, TB * b + TB):
                    nc.vector.bn_aggr(meanvar[:, t, :], stats[:, t, :]).then_inc(ln_stats, 1)

            def ln_normalise(base, b, dst):
                dve.wait_ge(ln_rstd, base // TB + b + 1)
                dve.wait_ge(ln_stats, base + TB * b + TB)
                if b >= 2:
                    dve.wait_ge(ln_turned, base + TB * (b - 2) + TB)
                for t in range(TB):
                    i = TB * b + t
                    nc.vector.tensor_scalar(dst[:, b % 2, t, :], acc[:, i, :], meanvar[:, i, 0:1], rstd[:, i:i + 1],
                                            ALU.subtract, ALU.mult).then_inc(ln_norm, 1)

            def modulation(first, src, dst):
                link(nc.vector.tensor_copy(modT[:, first:first + 2 * DC], src))
                nc.vector.tensor_scalar(dst[:], modT[:, first + DC:first + 2 * DC], 1.0, None, ALU.add
                                        ).then_inc(mod_out, 1)

            def gate(src, dst):
                link(nc.vector.tensor_scalar(gate_sgn, src, 0.0, 2.0, ALU.is_ge, ALU.mult))
                link(nc.vector.scalar_tensor_tensor(gate_mag, gate_sgn, -1.0, src, ALU.add, ALU.mult))
                link(nc.vector.tensor_scalar(gate_mag, gate_mag, 0.25, None, ALU.max))
                return nc.vector.scalar_tensor_tensor(dst[:], gate_sgn, -1.0, gate_mag, ALU.add, ALU.mult)

            dve.wait_ge(x_landed[0], 16)
            ln_stat(0, 0)
            dve.wait_ge(mod_mm, 1)
            modulation(0, pv[:, 0:2 * DC], scale_a)
            ln_normalise(0, 0, n1)
            for b in range(1, QB):
                dve.wait_ge(x_landed[b], 16)
                ln_stat(0, b)
                ln_normalise(0, b, n1)
            dve.wait_ge(mod_mm, 2)
            nc.vector.tensor_copy(biasT[:], gen[0][:, 0:3 * H]).then_inc(mod_out, 1)
            dve.wait_ge(mod_mm, 3)
            gate(strip[4][:], ga_bc).then_inc(mod_out, 1)
            dve.wait_ge(mod_mm, 4)
            dve.wait_ge(mod_out, 3)
            gate(gen[1][:], gb_bc).then_inc(mod_out, 1)
            dve.wait_ge(mod_mm, 5)
            modulation(3 * DC, pv[:, 0:2 * DC], scale_b)
            dve.wait_ge(mod_out, 5)
            dve.wait_ge(ln_mod, NT)
            dve.wait_ge(c_step, 5)
            dve.wait_ge(rinv_ready, 1)
            dve.sem_inc(gen_out, GENS)
            dve.sem_inc(strip_out, STRIPS)
            dve.sem_inc(attn_split, 1)

            def gen_out_of(kind, j, t, h):
                src = bank_of(kind, j, t)
                if kind in "qkt":
                    dve.wait_ge(gen_hi, nth_hi(kind, j, h))
                else:
                    dve.wait_ge(gen_done, nth(kind, j, t, h))
                if kind == "q":
                    ins = nc.vector.scalar_tensor_tensor(qT_lo[:], src[:], bias_now[:, 0:1], qT_hi[:].bitcast(F32),
                                                         ALU.add, ALU.subtract)
                elif kind == "k":
                    cols = slice(512 * j, 512 * j + 512)
                    ins = nc.vector.scalar_tensor_tensor(kT_lo[:, cols], src[:], bias_now[:, 1:2],
                                                         kT_hi[:, cols].bitcast(F32), ALU.add, ALU.subtract)
                elif kind == "v":
                    ins = nc.vector.tensor_scalar(vT_f[:], src[:], bias_now[:, 2:3], None, ALU.add)
                elif kind == "t":
                    rows = slice(TB * j, TB * j + TB)
                    ins = nc.vector.tensor_tensor(v_lo[:, rows, :], src[:].rearrange("p (t d) -> p t d", t=TB),
                                                  v_hi[:, rows, :].bitcast(F32), ALU.subtract)
                else:
                    i = TB * j + t
                    if t == 0:
                        dve.wait_ge(rinv_ready, h * QB + (1 if j == QB - 1 else j + 2))
                        dve.wait_ge(resid, TB if j == QB - 1 else NT)
                    ins = nc.vector.scalar_tensor_tensor(acc[:, i, :], src[:], rinv[:, i:i + 1], acc[:, i, :],
                                                         ALU.mult, ALU.add)
                ins.then_inc(gen_out, 1)

            def scores_out(j, h):
                for n, (t, ch, w) in enumerate(score_units(j)):
                    u = strips_before(j) + n
                    dve.wait_ge(strip_done, h * NSTRIP + (u + 1))
                    at = row_at[t] + 512 * ch
                    nc.vector.tensor_scalar(probs[:, at:at + w], strip[u % STRIPS][:, 0:w], SCALE, None, ALU.mult,
                                            ALU.max, accum_out=cmax[:, t, ch:ch + 1]).then_inc(strip_out, 1)
                    if ch == j:
                        dve.wait_ge(strip_out, h * NSTRIP + (STRIPS + u + 1))
                        nc.vector.tensor_reduce(nbias[:, t:t + 1], cmax[:, t, 0:j + 1], AX_X, ALU.max, negate=True
                                                ).then_inc(row_logits, 1)

            def turned_lo(j, h):
                for kk in range(units(j)):
                    u = strips_before(j) + units(j) + kk
                    dve.wait_ge(pt_hi, h * NTURN + (turned_before(j) + kk + 1))
                    c0 = first_col(j, kk)
                    nc.vector.tensor_tensor(pT_lo[:, kk % PTS, c0:512], strip[u % STRIPS][:, c0:512],
                                            pT_hi[:, kk % PTS, c0:512].bitcast(F32), ALU.subtract
                                            ).then_inc(strip_out, 1)
                    if 0 <= kk - AHEAD < TB:
                        gen_out_of("o", (j - 1) % QB, kk - AHEAD, h)
                for t in range(units(j) - AHEAD, TB):
                    gen_out_of("o", (j - 1) % QB, t, h)
                dve.wait_ge(attn_hi, h * QB + (j + 1))
                nc.vector.tensor_tensor(at_lo[:], pv[:], at_hi[:].bitcast(F32), ALU.subtract).then_inc(attn_split, 1)
                nc.vector.reciprocal(rinv[:, TB * j:TB * j + TB], rsum[:, TB * j:TB * j + TB]).then_inc(rinv_ready, 1)

            def head(h, last):
                for j in range(QB):
                    gen_out_of("t", j, 0, h)
                    scores_out(j, h)
                    if j < QB - 1 or not last:
                        for kind in "qkv":
                            gen_out_of(kind, (j + 1) % QB, 0, h)
                    else:
                        dve.wait_ge(gen_out, nth("t", j, 0, h) + GENS)
                        dve.sem_inc(gen_done, 3)
                        dve.sem_inc(gen_out, 3)
                    turned_lo(j, h)

            for kind in "qkv":
                gen_out_of(kind, 0, 0, -1)
            dve.wait_ge(gen_out, nth("v", 0, 0, -1) + GENS)
            dve.sem_inc(gen_done, TB)
            dve.sem_inc(gen_out, TB)
            with dve.Fori(0, H - 1) as h:
                head(h, False)
            head(H - 1, True)
            dve.wait_ge(rinv_ready, QB * H + 1)
            for t in range(TB):
                dve.wait_ge(gen_done, OUTS_END + t + 1)
                i = NT - TB + t
                nc.vector.scalar_tensor_tensor(acc[:, i, :], gen[t % GENS][:], rinv[:, i:i + 1], acc[:, i, :],
                                               ALU.mult, ALU.add).then_inc(gen_out, 1)

            dve.wait_ge(gen_out, GENS + OUTS_END + TB)
            for b in range(QB):
                ln_stat(NT, b)
                if b >= 2:
                    dve.wait_ge(n2_stored[b % 2], 16)
                ln_normalise(NT, b, n2)

            dve.wait_ge(consts, 10)
            dve.wait_ge(rb_landed, 16)
            dve.wait_ge(n2_stored[0], 32)
            dve.wait_ge(n2_stored[1], 32)
            half = NT // 2
            dve.wait_ge(logits_mm, 2)
            for s in range(2):
                link(nc.vector.tensor_tensor(scores[:, half * s:half * s + half, :],
                                             gen[s][:].rearrange("p (t e) -> p t e", e=E),
                                             rb_bc[:].unsqueeze(1).to_broadcast([P, half, E]), ALU.add))
            mx, total, inv, inv4 = r_stat
            link(nc.vector.tensor_reduce(mx[:], scores[:], AX_X, ALU.max))
            nc.vector.tensor_tensor(prod[:], scores[:], mx[:].unsqueeze(2).to_broadcast([P, NT, E]), ALU.subtract
                                    ).then_inc(r_shift, 1)
            link(nc.vector.tensor_copy(iota_f[:], iota_i[:]))
            dve.wait_ge(r_exp, 1)
            link(nc.vector.tensor_reduce(total[:], scores[:], AX_X, ALU.add))
            link(nc.vector.reciprocal(inv[:], total[:]))
            link(nc.vector.tensor_tensor(scores[:], scores[:], inv[:].unsqueeze(2).to_broadcast([P, NT, E]), ALU.mult))
            for t in range(NT):
                ins = nc.vector.max(vals[:, t, :], scores[:, t, :])
                steps[0] += 1
                ins.then_inc(dve_step, 1)
            dve.wait_ge(dve_step, steps[0])
            for t in range(NT):
                ins = nc.vector.max_index(idx[:, t, :], vals[:, t, :], scores[:, t, :])
                steps[0] += 1
                ins.then_inc(dve_step, 1)
            dve.wait_ge(dve_step, steps[0])
            link(nc.vector.tensor_copy(idx_f[:], idx[:, :, 0:TOPK]))
            for k in range(TOPK):
                link(nc.vector.tensor_tensor(onehot[k][:], iota_f[:].unsqueeze(1).to_broadcast([P, NT, E]),
                                             idx_f[:, :, k:k + 1].to_broadcast([P, NT, E]), ALU.is_equal))
            link(nc.vector.tensor_tensor(picked[:], onehot[0][:], onehot[1][:], ALU.add))
            link(nc.vector.tensor_tensor(picked[:], picked[:], onehot[2][:], ALU.add))
            nc.vector.tensor_tensor(picked[:], picked[:], onehot[3][:], ALU.add).then_inc(picked_ready, 1)
            link(nc.vector.tensor_reduce(total[:], vals[:, :, 0:TOPK], AX_X, ALU.add))
            link(nc.vector.reciprocal(inv4[:], total[:]))
            link(nc.vector.tensor_tensor(w_top[:], vals[:, :, 0:TOPK], inv4[:].unsqueeze(2).to_broadcast([P, NT, TOPK]),
                                         ALU.mult))
            dve.wait_ge(pos_mm, 2)
            for s in range(2):
                link(nc.vector.tensor_copy(pos[:, half * s:half * s + half, :],
                                           gen[s][:].rearrange("p (t e) -> p t e", e=E)))
            for k in range(TOPK):
                link(nc.vector.tensor_tensor(prod[:], onehot[k][:], pos[:], ALU.mult))
                link(nc.vector.tensor_reduce(pos_k[:, :, k], prod[:], AX_X, ALU.add))
            t0, t1, t2 = r_tmp
            link(nc.vector.tensor_scalar(valid[:], pos_k[:], float(CAP), None, ALU.is_lt))
            link(nc.vector.tensor_tensor(w_top[:], w_top[:], valid[:], ALU.mult))
            link(nc.vector.tensor_scalar(t0[:], pos_k[:], float(CAP - 1), None, ALU.min))
            link(nc.vector.scalar_tensor_tensor(t1[:], idx_f[:], float(CAP), t0[:], ALU.mult, ALU.add))
            link(nc.vector.tensor_copy(slot_u[:], t1[:]))
            link(nc.vector.scalar_tensor_tensor(t0[:], pos_k[:], float(E), idx_f[:], ALU.mult, ALU.add))
            link(nc.vector.tensor_copy(t1[:], trash_i[:]))
            link(nc.vector.tensor_tensor(t0[:], t0[:], t1[:], ALU.subtract))
            link(nc.vector.tensor_tensor(t2[:], t0[:], valid[:], ALU.mult))
            link(nc.vector.tensor_tensor(t0[:], t2[:], t1[:], ALU.add))
            nc.vector.tensor_copy(scat_u[:], t0[:]).then_inc(routed, 1)
            dve.sem_inc(xb_turned, EX)
            dve.sem_inc(yb_ready, EX)
            dve.sem_inc(gath_free, 2)
            for i in range(EX):
                dve.sem_inc(yb_stored[i], 16)

            def shared(n, first_combined=None):
                for ch in range(SC):
                    u = n * SC + ch
                    dve.wait_ge(silu_done, u + 1)
                    nc.vector.tensor_tensor(hs[:, ch, :], strip[2 * (ch % 2) + 1][:], sil_s[:, ch % 2, :], ALU.mult
                                            ).then_inc(hs_ready, 1)
                    if first_combined is not None:
                        combine(first_combined + ch)
                for t in range(TB):
                    i = n * TB + t
                    dve.wait_ge(down_done, i + 1)
                    src = strip[4] if t % 2 == 0 else pv
                    if i >= NT // 2:
                        dve.wait_ge(combined, i - NT // 2 + 1)
                    ins = nc.vector.tensor_tensor(acc[:, i, :], src[:], acc[:, i, :], ALU.add)
                    ins.then_inc(down_out, 1)
                    if i >= NT // 2:
                        dve.wait_ge(down_out, i + 1)
                        dve.sem_inc(row_final, 1)

            def combine(t):
                n = (t + NT // 2) % NT
                dve.wait_ge(g_landed[n % 2], (n // 2 + 1) * 16 * TOPK)
                if t < NT // 2:
                    dve.wait_ge(down_out, t + 1)
                for k in range(TOPK):
                    ins = nc.vector.scalar_tensor_tensor(acc[:, t, :], gath[:, n % 2, k, :], w_top[:, t, k:k + 1],
                                                         acc[:, t, :], ALU.mult, ALU.add)
                    if k < TOPK - 1:
                        link(ins)
                ins.then_inc(combined, 1)
                dve.wait_ge(combined, n + 1)
                dve.sem_inc(gath_free, 1)
                if t < NT // 2:
                    dve.sem_inc(row_final, 1)

            for n in range(2):
                shared(n)

            def experts(g):
                for i in range(EX):
                    dve.wait_ge(e_silu, g * EX + (i + 1))
                    nc.vector.tensor_tensor(hE[:, i % 2, :], strip[2 * (i % 2) + 1][:, 0:P], sil_e[:, i % 2, :], ALU.mult
                                            ).then_inc(e_h, 1)
                    if i >= 1:
                        expert_out(i - 1, g)
                expert_out(EX - 1, g)

            def expert_out(i, g):
                dve.wait_ge(e_down, g * EX + (i + 1))
                dve.wait_ge(yb_stored[i], g * 16 + 16)
                src = strip[4] if i % 2 == 0 else pv
                nc.vector.tensor_tensor(yb[:, i, :], src[:], gb_bc[:], ALU.mult).then_inc(yb_ready, 1)

            with dve.Fori(0, E // EX) as g:
                experts(g)
            for n in range(2, QB):
                shared(n, (NT // 2, 0)[n - 2])

        @block.tensor
        def _(pe):
            def matmul3(o, a_hi, a_lo, b_hi, b_lo, start, stop):
                nc.tensor.matmul(o, a_hi, b_hi, start=start, stop=False)
                nc.tensor.matmul(o, a_hi, b_lo, start=False, stop=False)
                return nc.tensor.matmul(o, a_lo, b_hi, start=False, stop=stop)

            def mod_columns(o, first):
                for n in range(2 * DC):
                    for ch in range(DC):
                        at = (first + n) * P
                        last = nc.tensor.matmul(o[:, n:n + 1], wmod_sb[:, ch, at:at + P], sc_col[:, ch:ch + 1],
                                                start=ch == 0, stop=ch == DC - 1)
                last.then_inc(mod_mm, 1)

            def mod_rows(o, first):
                for ch in range(DC):
                    last = nc.tensor.matmul(o[:], sc_bc[:, ch, :], wmod_sb[:, ch, first * P:first * P + D],
                                            start=ch == 0, stop=ch == DC - 1)
                last.then_inc(mod_mm, 1)

            def ln_turn(base, b, src):
                for ch in range(DC):
                    if b >= 1:
                        pe.wait_ge(ln_mod, base + DC * (b - 1) + ch + 1)
                    for t in range(TB):
                        if ch == 0:
                            pe.wait_ge(ln_norm, base + TB * b + t + 1)
                        last = nc.tensor.transpose(strip[ch][:, P * t:P * t + P], src[:, b % 2, t, P * ch:P * ch + P],
                                                   ident[:])
                    last.then_inc(ln_turned, 1)

            pe.wait_ge(consts, 4)
            pe.wait_ge(c_step, 5)
            pe.wait_ge(mod1_landed, 16)
            mod_columns(pv, 0)
            for b in range(QB):
                ln_turn(0, b, n1)
            pe.wait_ge(rows_landed, 48)
            nc.tensor.transpose(gen[0][:, 0:3 * H], bias_rows[:], ident[0:3 * H, 0:3 * H]).then_inc(mod_mm, 1)
            pe.wait_ge(mod2_landed, 16)
            mod_rows(strip[4], 2 * DC)
            mod_rows(gen[1], 5 * DC)
            pe.wait_ge(mod_out, 1)
            mod_columns(pv, 3 * DC)
            pe.wait_ge(ln_split, NT)

            def project(n, kind, j, h):
                pe.wait_ge(gen_out, nth(kind, j, 0, h))
                o = bank_of(kind, j, 0)
                if j == 0:
                    pe.wait_ge(w_split, h * 4 + (n + 5))
                for ch in range(DC):
                    cols = slice(512 * j, 512 * j + 512)
                    last = matmul3(o[:], w_hi_t[n][:, ch, :], w_lo_t[n][:, ch, :],
                                   hT_hi[:, ch, cols], hT_lo[:, ch, cols], ch == 0, ch == DC - 1)
                last.then_inc(gen_done, 1)

            def out_project(t, o):
                last = matmul3(o[:], at_hi[:, P * t:P * t + P], at_lo[:, P * t:P * t + P],
                               w_hi_t[3][:].rearrange("p c d -> p (c d)"), w_lo_t[3][:].rearrange("p c d -> p (c d)"),
                               True, True)
                last.then_inc(gen_done, 1)

            def outs_of(j, t, h):
                if t == 0:
                    pe.wait_ge(attn_split, h * QB + (1 if j == QB - 1 else j + 2))
                    if j < QB - 1:
                        pe.wait_ge(w_split, h * 4 + 4)
                pe.wait_ge(gen_out, nth("o", j, t, h))
                out_project(t, bank_of("o", j, t))

            def turn_values(j, h):
                pe.wait_ge(gen_out, nth("t", j, 0, h))
                pe.wait_ge(gen_out, nth("v", j, 0, h - 1 if j == 0 else h) + GENS)
                o = bank_of("t", j, 0)
                for t in range(TB):
                    last = nc.tensor.transpose(o[:, P * t:P * t + P], vT_f[:, P * t:P * t + P], ident[:])
                last.then_inc(gen_done, 1)

            def score(j, h):
                pe.wait_ge(gen_out, nth("k", j, 0, h - 1 if j == 0 else h) + GENS)
                for n, (t, ch, w) in enumerate(score_units(j)):
                    u = strips_before(j) + n
                    pe.wait_ge(strip_out, h * NSTRIP + (u + 1))
                    o = strip[u % STRIPS]
                    rows, cols = slice(P * t, P * t + P), slice(512 * ch, 512 * ch + w)
                    last = matmul3(o[:, 0:w], qT_hi[:, rows], qT_lo[:, rows], kT_hi[:, cols], kT_lo[:, cols],
                                   True, True)
                    if ch == j:
                        last = nc.tensor.matmul(o[:, w - P:w], ident_bf[:], mask_bf[:], start=False, stop=True,
                                                skip_group_check=True)
                    last.then_inc(strip_done, 1)

            def turn_and_sum(j, h):
                n = units(j)
                pe.wait_ge(row_probs, h * NT + TB * (j + 1))

                def turn(kk):
                    u = strips_before(j) + n + kk
                    pe.wait_ge(strip_out, h * NSTRIP + (u + 1))
                    for t in range(first_col(j, kk) // P, TB):
                        at = row_at[t] + P * kk
                        last = nc.tensor.transpose(strip[u % STRIPS][:, P * t:P * t + P], probs[:, at:at + P], ident[:])
                    last.then_inc(strip_done, 1)

                def sum_values(kk):
                    u = strips_before(j) + n + kk
                    pe.wait_ge(strip_out, h * NSTRIP + (STRIPS + u + 1))
                    if kk == 0 or kk == TB * j:
                        pe.wait_ge(gen_out, nth("t", kk // TB, 0, h) + GENS)
                    c0 = first_col(j, kk)
                    last = matmul3(pv[:, c0:512], v_hi[:, kk, :], v_lo[:, kk, :], pT_hi[:, kk % PTS, c0:512],
                                   pT_lo[:, kk % PTS, c0:512], kk == 0, kk == n - 1)
                    last.then_inc(pv_done, 1)

                for kk in range(n + AHEAD):
                    if kk < n:
                        turn(kk)
                    if kk >= AHEAD:
                        if kk - AHEAD < TB:
                            outs_of((j - 1) % QB, kk - AHEAD, h)
                        sum_values(kk - AHEAD)

            def head(h, last):
                for j in range(QB):
                    turn_values(j, h)
                    score(j, h)
                    if j < QB - 1 or not last:
                        for n, kind in enumerate("qkv"):
                            project(n, kind, (j + 1) % QB, h)
                    turn_and_sum(j, h)

            for n, kind in enumerate("qkv"):
                project(n, kind, 0, -1)
            with pe.Fori(0, H - 1) as h:
                head(h, False)
            head(H - 1, True)
            pe.wait_ge(attn_split, QB * H + 1)
            for t in range(TB):
                pe.wait_ge(gen_out, OUTS_END + t + 1)
                out_project(t, gen[t % GENS])

            for b in range(QB):
                ln_turn(NT, b, n2)
            pe.wait_ge(gen_out, GENS + OUTS_END + TB)
            pe.wait_ge(wr_landed, 16)
            pe.wait_ge(ln_mod, 2 * NT)
            half = NT // 2
            for s in range(2):
                for t in range(half):
                    for ch in range(DC):
                        at = P * (half * s + t)
                        last = nc.tensor.matmul(gen[s][:, E * t:E * t + E], h2T[:, ch, at:at + P], wr_sb[:, ch, :],
                                                start=ch == 0, stop=ch == DC - 1)
                last.then_inc(logits_mm, 1)

            def shared(n):
                for ch in range(SC):
                    u = n * SC + ch
                    if u >= 2:
                        pe.wait_ge(hs_ready, u - 1)
                    for o, w in ((strip[2 * (ch % 2)], sg_sb), (strip[2 * (ch % 2) + 1], su_sb)):
                        for c in range(DC):
                            last = nc.tensor.matmul(o[:], w[:, c, P * ch:P * ch + P], h2T[:, c, 512 * n:512 * n + 512],
                                                    start=c == 0, stop=c == DC - 1)
                    last.then_inc(gu_done, 1)
                pe.wait_ge(hs_ready, n * SC + SC)
                for t in range(TB):
                    v = n * TB + t
                    if v >= 2:
                        pe.wait_ge(down_out, v - 1)
                    o = strip[4] if t % 2 == 0 else pv
                    for ch in range(SC):
                        last = nc.tensor.matmul(o[:], hs[:, ch, P * t:P * t + P], sd_sb[:, ch, :],
                                                start=ch == 0, stop=ch == SC - 1)
                    last.then_inc(down_done, 1)

            pe.wait_ge(sw_landed, 16 * 3 * NS)
            pe.wait_ge(sd_scaled, SC)
            pe.wait_ge(picked_ready, 1)
            for s in range(2):
                mine = slice(half * s, half * s + half)
                last = nc.tensor.matmul(gen[s][:], tri_bf[:], picked[:, mine, :].rearrange("p t e -> p (t e)"),
                                        start=True, stop=True)
                for j in range(half * s + half - 1):
                    first = max(j + 1, half * s)
                    n = half * s + half - first
                    last = nc.tensor.matmul(gen[s][:, E * (first - half * s):512]
                                            .rearrange("p (t e) -> p t e", e=E), ones_bf[:],
                                            picked[:, j:j + 1, :].to_broadcast([P, n, E]), start=False,
                                            stop=True, skip_group_check=True)
                last.then_inc(pos_mm, 1)
            for n in range(2):
                shared(n)

            def expert_turn(i, g):
                pe.wait_ge(xb_landed[i], g * 16 + 16)
                for ch in range(DC):
                    last = nc.tensor.transpose(gen[i % 2][:, P * ch:P * ch + P], xb[:, i, P * ch:P * ch + P], ident[:])
                last.then_inc(xb_turned, 1)

            def expert_gate_up(i, g):
                pe.wait_ge(xbT_ready, g * EX + (i + 1))
                pe.wait_ge(e_landed[i], g * 48 + 48)
                for o, w in ((strip[2 * (i % 2)], wg_sb), (strip[2 * (i % 2) + 1], wu_sb)):
                    for c in range(DC):
                        last = nc.tensor.matmul(o[:, 0:P], w[:, i, c, :], xbT[:, i % 2, P * c:P * c + P],
                                                start=c == 0, stop=c == DC - 1)
                last.then_inc(e_gu, 1)

            def expert_down(i, g):
                pe.wait_ge(e_h, g * EX + (i + 1))
                pe.wait_ge(yb_ready, g * EX + (EX + i - 1))
                o = strip[4] if i % 2 == 0 else pv
                nc.tensor.matmul(o[:], hE[:, i % 2, :], wd_sb[:, i, :], start=True, stop=True).then_inc(e_down, 1)

            pe.wait_ge(down_out, 2 * TB)
            pe.wait_ge(pos_mm, 2)
            pe.wait_ge(routed, 1)
            with pe.Fori(0, E // EX) as g:
                expert_turn(0, g)
                for i in range(EX):
                    if i + 1 < EX:
                        expert_turn(i + 1, g)
                    expert_gate_up(i, g)
                    if i >= 1:
                        expert_down(i - 1, g)
                expert_down(EX - 1, g)
            pe.wait_ge(yb_ready, EX + E)
            for n in range(2, QB):
                shared(n)


_INS = ["L0_attn_x", "L0_attn_Q_w", "L0_attn_Q_b", "L0_attn_K_w", "L0_attn_K_b", "L0_attn_V_w", "L0_attn_V_b",
        "L0_attn_O_w", "L0_attn_O_b", "L0_ffn_Wr", "L0_ffn_router_bias", "L0_ffn_Wg", "L0_ffn_Wu", "L0_ffn_Wd",
        "L0_ffn_Sg", "L0_ffn_Su", "L0_ffn_Sd", "L0_c", "L0_wmod"]


def kernel(**inputs):
    import concourse.bacc as bacc
    from concourse.bass_utils import run_bass_kernel_spmd

    nc = bacc.Bacc("TRN2", target_bir_lowering=False, num_devices=1)
    arrays, args = {}, []
    for name in _INS:
        arr = np.ascontiguousarray(inputs[name])
        arrays[f"in_{name}"] = arr
        args.append(nc.dram_tensor(f"in_{name}", arr.shape, mybir.dt.from_np(arr.dtype), kind="ExternalInput").ap())
    shape = inputs["L0_attn_x"].shape
    args.append(nc.dram_tensor("out_y", shape, F32, kind="ExternalOutput").ap())
    adaln_block(nc, *args)
    r = run_bass_kernel_spmd(nc, [arrays], core_ids=[0])
    return r.results[0]["out_y"]
```

```python
from contextlib import ExitStack

import numpy as np
import concourse.bass as bass
from concourse import mybir

F32 = mybir.dt.float32
F32R = mybir.dt.float32r
BF16 = mybir.dt.bfloat16
I32 = mybir.dt.int32
U32 = mybir.dt.uint32
ALU = mybir.AluOpType
ACT = mybir.ActivationFunctionType
AX_X = mybir.AxisListType.X
P = 128


class SbufMap:

    def __init__(self, nc, at):
        self.nc, self.at = nc, at

    def place(self, name, shape, dtype):
        size = int(np.prod(shape[1:])) * (2 if dtype == BF16 else 4)
        t = self.nc.alloc_sbuf_tensor_at(name, list(shape), dtype, offset=self.at)
        self.at += (size + 31) // 32 * 32
        return t


def adaln_block(nc, x, Q_w, Q_b, K_w, K_b, V_w, V_b, O_w, O_b, Wr, router_bias, Wg, Wu, Wd, Sg, Su, Sd,
                c_in, wmod, out):
    _, S, D = x.shape
    H, _, DH = Q_w.shape
    E, _, HE = Wg.shape
    NS, _, HS = Sg.shape
    TOPK = 4
    CAP = 128
    NT = S // P
    DC = D // P
    QB = S // 512
    TB = 4
    SC = NS * HS // P
    EPS = 1e-5
    SCALE = float(DH) ** -0.5
    MASKED = -1e5 / SCALE
    TRASH = E * CAP
    assert DH == P and HE == P and D == 512 and CAP == P

    n2_dram = nc.dram_tensor("n2_dram", [S, D], F32, kind="Internal").ap()
    table_dram = nc.dram_tensor("table_dram", [TRASH + S * TOPK, 1], I32, kind="Internal").ap()
    yb_dram = nc.dram_tensor("yb_dram", [E * CAP, D], F32, kind="Internal").ap()

    with ExitStack() as ctx:
        def sem(name):
            return ctx.enter_context(nc.semaphore(name))

        def bank(name):
            return ctx.enter_context(nc.psum_tensor(name, [P, 512], F32))

        STRIPS, GENS, PTS = 5, 2, 3
        AHEAD = PTS - 1
        strip = [bank(f"strip{i}") for i in range(STRIPS)]
        gen = [bank(f"gen{i}") for i in range(GENS)]
        pv = bank("pv")

        base = (nc.sbuf_base + 63) // 64 * 64
        keep = SbufMap(nc, base)
        acc = keep.place("acc", [P, NT, D], F32)
        ident = keep.place("ident", [P, P], F32)
        ident_bf = keep.place("ident_bf", [P, P], BF16)
        mask_bf = keep.place("mask_bf", [P, P], BF16)
        modT = keep.place("modT", [P, 6 * DC], F32)
        scale_a = keep.place("scale_a", [P, DC], F32)
        scale_b = keep.place("scale_b", [P, DC], F32)
        ga_bc = keep.place("ga_bc", [P, D], F32)
        gb_bc = keep.place("gb_bc", [P, D], F32)
        biasT = keep.place("biasT", [P, 3 * H], F32)
        bias_now = keep.place("bias_now", [P, 3], F32)
        stats = keep.place("stats", [P, NT, 6], F32)
        meanvar = keep.place("meanvar", [P, NT, 2], F32)
        rstd = keep.place("rstd", [P, NT], F32)
        veps = keep.place("veps", [P, NT], F32)
        neghalf = keep.place("neghalf", [P, NT], F32)
        cmax = keep.place("cmax", [P, TB, QB], F32)
        nbias = keep.place("nbias", [P, TB], F32)
        rsum = keep.place("rsum", [P, NT], F32)
        rinv = keep.place("rinv", [P, NT], F32)
        c_col = keep.place("c_col", [P, DC], F32)
        c_exp = keep.place("c_exp", [P, DC], F32)
        c_sig = keep.place("c_sig", [P, DC], F32)
        sc_col = keep.place("sc_col", [P, DC], F32)

        a = SbufMap(nc, keep.at)
        hT_hi = a.place("hT_hi", [P, DC, S], F32R)
        hT_lo = a.place("hT_lo", [P, DC, S], F32R)
        w_hi_t = [a.place(f"w{n}_hi", [P, DC, P], F32R) for n in "qkv"]
        w_lo_t = [a.place(f"w{n}_lo", [P, DC, P], F32R) for n in "qkv"]
        raw = [a.place(f"w{n}_raw", [P, DC, P], F32) for n in "qk"]
        early_end = a.at
        raw.append(a.place("wvo_raw", [P, DC, P], F32))
        w_hi_t.append(a.place("wo_hi", [P, DC, P], F32R))
        w_lo_t.append(a.place("wo_lo", [P, DC, P], F32R))
        raw.append(raw[2])
        at_hi = a.place("at_hi", [P, 512], F32R)
        at_lo = a.place("at_lo", [P, 512], F32R)
        overlaid = a.at
        row_at = [sum((NT - TB + q + 1) * P for q in range(r)) for r in range(TB + 1)]
        probs = a.place("probs", [P, row_at[TB]], F32)
        pT_hi = a.place("pT_hi", [P, PTS, 512], F32R)
        pT_lo = a.place("pT_lo", [P, PTS, 512], F32R)
        v_hi = a.place("v_hi", [P, NT, P], F32R)
        v_lo = a.place("v_lo", [P, NT, P], F32R)
        scored = a.at
        kT_hi = a.place("kT_hi", [P, S], F32R)
        kT_lo = a.place("kT_lo", [P, S], F32R)
        qT_hi = a.place("qT_hi", [P, 512], F32R)
        qT_lo = a.place("qT_lo", [P, 512], F32R)
        vT_f = a.place("vT_f", [P, 512], F32)
        assert a.at <= nc.sbuf_usable_end, a.at
        pre = SbufMap(nc, overlaid)
        n1 = pre.place("n1", [P, 2, TB, D], F32)
        h_tmp = pre.place("h_tmp", [P, DC, 512], F32)
        wmod_sb = pre.place("wmod_sb", [P, DC, 3 * D], F32)
        sc_bc = pre.place("sc_bc", [P, DC, P], F32)
        mod_tmp = pre.place("mod_tmp", [P, 2, D], F32)
        bias_rows = pre.place("bias_rows", [3 * H, P], F32)
        assert pre.at <= scored - D * 4, pre.at
        gob = SbufMap(nc, scored - D * 4).place("gob", [P, D], F32)

        f = SbufMap(nc, keep.at)
        h2T_hi = f.place("h2T_hi", [P, DC, S], F32R)
        h2T_lo = f.place("h2T_lo", [P, DC, S], F32R)
        n2 = f.place("n2", [P, 2, TB, D], F32)
        assert f.at <= early_end, (f.at, early_end)
        EX = 4
        GATHS = 4
        io = SbufMap(nc, f.at - 2 * TB * D * 4)
        xb = io.place("xb", [P, EX, D], F32)
        yb = io.place("yb", [P, EX, D], F32)
        assert io.at <= f.at
        f.at = early_end
        h2_tmp = [f.place("h2_tmp0", [P, 512], F32)]
        assert f.at == early_end + DC * P * 4
        s_hi, s_lo = [None, None], [None, None]
        s_hi[1] = f.place("s_hi1", [P, 3, D], F32R)
        s_lo[1] = f.place("s_lo1", [P, 3, D], F32R)
        sil_s = f.place("sil_s", [P, 2, 512], F32)
        hs_hi = f.place("hs_hi", [P, 2, 512], F32R)
        hs_lo = f.place("hs_lo", [P, 2, 512], F32R)
        wr_sb = f.place("wr_sb", [P, DC, E], F32)
        wr_hi = f.place("wr_hi", [P, DC, E], F32R)
        wr_lo = f.place("wr_lo", [P, DC, E], F32R)
        logitsT = f.place("logitsT", [E, 2, 512], F32)
        rb_bc = f.place("rb_bc", [P, E], F32)
        zeros_i = f.place("zeros_i", [P, E], I32)
        w_top = f.place("w_top", [P, NT, TOPK], F32)
        slot_u = f.place("slot_u", [P, NT, TOPK], U32)
        scat_u = f.place("scat_u", [P, NT, TOPK], U32)
        tok_i = f.place("tok_i", [P, NT], I32)
        trash_i = f.place("trash_i", [P, NT, TOPK], I32)
        iota_i = f.place("iota_i", [P, E], I32)
        table = f.place("table", [P, E], I32)
        tri_bf = f.place("tri_bf", [P, P], BF16)
        ones_bf = f.place("ones_bf", [P, P], BF16)
        slot_now = f.place("slot_now", [P, GATHS, TOPK], U32)
        tok_now = f.place("tok_now", [P, EX], I32)
        routed_experts_at = f.at
        wg_sb = f.place("wg_sb", [P, EX, DC, HE], F32)
        wu_sb = f.place("wu_sb", [P, EX, DC, HE], F32)
        wd_sb = f.place("wd_sb", [P, EX, D], F32)
        xbT = f.place("xbT", [P, 2, D], F32)
        sil_e = f.place("sil_e", [P, 2, P], F32)
        hE = f.place("hE", [P, 2, P], F32)
        assert f.at <= scored, (f.at, scored)
        late = SbufMap(nc, scored)
        s_raw = late.place("s_raw", [P, 3, D], F32)
        s_hi[0] = late.place("s_hi0", [P, 3, D], F32R)
        s_lo[0] = late.place("s_lo0", [P, 3, D], F32R)
        h2_tmp.append(late.place("h2_tmp1", [P, 512], F32))
        assert late.at <= a.at, (late.at, a.at)
        r = SbufMap(nc, routed_experts_at)
        scores = r.place("scores", [P, NT, E], F32)
        onehot = [r.place(f"onehot{k}", [P, NT, E], BF16) for k in range(TOPK)]
        picked = r.place("picked", [P, NT, E], BF16)
        pos = r.place("pos", [P, NT, E], F32)
        prod = r.place("prod", [P, NT, E], F32)
        r_stat = [r.place(f"r_stat{n}", [P, NT], F32) for n in range(4)]
        vals = r.place("vals", [P, NT, 8], F32)
        idx = r.place("idx", [P, NT, 8], U32)
        idx_f = r.place("idx_f", [P, NT, TOPK], F32)
        pos_k = r.place("pos_k", [P, NT, TOPK], F32)
        valid = r.place("valid", [P, NT, TOPK], F32)
        r_tmp = [r.place(f"r_tmp{n}", [P, NT, TOPK], F32) for n in range(3)]
        iota_f = r.place("iota_f", [P, E], F32)
        assert r.at <= f.at, (r.at, f.at)
        gath = []
        for at in (routed_experts_at, early_end - 2 * TB * D * 4):
            g_ = SbufMap(nc, at)
            gath += [g_.place(f"gath{len(gath) + i}", [P, TOPK, D], F32) for i in range(2)]

        c_landed = sem("c_landed")
        mod_landed = [sem(f"mod_landed_{n}") for n in ("sa_ca", "ga", "sb_cb", "gb")]
        x_landed = [sem(f"x_landed{b}") for b in range(QB)]
        rows_landed, ob_landed = sem("rows_landed"), sem("ob_landed")
        raw_landed = [sem(f"raw_landed_{n}") for n in "qkvo"]
        consts = sem("consts")
        c_step = sem("c_step")
        c_act = sem("c_act")
        mod_mm, mod_out = sem("mod_mm"), sem("mod_out")
        dve_step = sem("dve_step")
        pool_step = sem("pool_step")
        pool_waited = sem("pool_waited")
        ln_stats, ln_rstd, ln_norm = sem("ln_stats"), sem("ln_rstd"), sem("ln_norm")
        ln_turned, ln_mod, ln_split = sem("ln_turned"), sem("ln_mod"), sem("ln_split")
        gob_ready = sem("gob_ready")
        resid = sem("resid")
        w_hi, w_split, wo_scaled = sem("w_hi"), sem("w_split"), sem("wo_scaled")
        bias_ready = sem("bias_ready")
        gen_done, gen_hi, gen_out = sem("gen_done"), sem("gen_hi"), sem("gen_out")
        strip_done, strip_out = sem("strip_done"), sem("strip_out")
        row_logits, row_probs = sem("row_logits"), sem("row_probs")
        pt_hi, pv_done = sem("pt_hi"), sem("pv_done")
        attn_hi, attn_split = sem("attn_hi"), sem("attn_split")
        rinv_ready = sem("rinv_ready")
        sw_landed, wr_landed, rb_landed = sem("sw_landed"), sem("wr_landed"), sem("rb_landed")
        wr_hi_ready, wr_split = sem("wr_hi_ready"), sem("wr_split")
        sw_scaled, sw_hi, sw_split = sem("sw_scaled"), sem("sw_hi"), sem("sw_split")
        n2_stored = [sem(f"n2_stored{i}") for i in range(2)]
        zero_stored = sem("zero_stored")
        logitsT_mm, logitsT_out = sem("logitsT_mm"), sem("logitsT_out")
        logits_mm, r_shift, r_exp, picked_ready, pos_mm, routed = (
            sem("logits_mm"), sem("r_shift"), sem("r_exp"), sem("picked_ready"), sem("pos_mm"), sem("routed"))
        scattered, table_landed = sem("scattered"), sem("table_landed")
        gate_done, silu_done, up_done = sem("gate_done"), sem("silu_done"), sem("up_done")
        hs_whole, hs_hi_ready, hs_split = sem("hs_whole"), sem("hs_hi_ready"), sem("hs_split")
        down_done, down_out = sem("down_done"), sem("down_out")
        e_landed = [sem(f"e_landed{i}") for i in range(EX)]
        xb_landed = [sem(f"xb_landed{i}") for i in range(EX)]
        tok_ready = sem("tok_ready")
        xb_turned, xbT_ready = sem("xb_turned"), sem("xbT_ready")
        e_gu, e_silu, e_h = sem("e_gu"), sem("e_silu"), sem("e_h")
        e_down, yb_ready = sem("e_down"), sem("yb_ready")
        yb_stored = [sem(f"yb_stored{i}") for i in range(EX)]
        slot_ready = sem("slot_ready")
        g_landed = [sem(f"g_landed{i}") for i in range(GATHS)]
        gath_free, combined = sem("gath_free"), sem("combined")
        out_stored = sem("out_stored")

        order = []
        for j in range(QB):
            order += [("t", j, 0)] + [(kind, (j + 1) % QB, 0) for kind in "qkv"]
            order += [("o", (j - 1) % QB, t) for t in range(TB)]
        NG = len(order)
        G = {u: n for n, u in enumerate(order)}
        HI = {u: n for n, u in enumerate([u for u in order if u[0] in "qkt"])}
        NHI = len(HI)
        G_PRE, HI_PRE = NG - G["q", 0, 0], NHI - HI["q", 0, 0]

        def nth(kind, j, t, h):
            return h * NG + (G_PRE + G[kind, j, t] + 1)

        def nth_hi(kind, j, h):
            return h * NHI + (HI_PRE + HI[kind, j, 0] + 1)

        def bank_of(kind, j, t):
            return gen[G[kind, j, t] % GENS]

        OUTS_END = NG * H + G_PRE
        LN2_STATS = {(1, 7): 0, (3, 13): 2}
        LN2_ROWS = {(2, 5): 0}
        LN2_CHUNKS = {(j, 8 + ch): (j - 2, ch) for j in (2, 3) for ch in range(DC)}

        CHUNK_SCALED, CHUNK_HI, CHUNK_LO = (3, 6), (3, 12), (3, 14)

        def ln2_bank(b, ch):
            return gen[ch % GENS] if b < 2 else strip[ch % 2]

        def ln2_tmp(b, ch):
            return h2_tmp[0 if b == 0 else ch % 2]

        def units(j):
            return TB * (j + 1)

        def strips_before(j):
            return sum(2 * units(i) for i in range(j))

        def turned_before(j):
            return sum(units(i) for i in range(j))

        NSTRIP, NTURN = strips_before(QB), turned_before(QB)
        assert NG % GENS == 0 and NSTRIP % STRIPS == 0

        def score_units(j):
            return [(t, ch, 512 if ch < j else (t + 1) * P) for t in range(TB) for ch in range(j + 1)]

        def first_col(j, kk):
            return max(0, kk - TB * j) * P

        MOE_CHUNKS = (4,)
        BEFORE = [(c, b) for c in range(MOE_CHUNKS[0]) for b in range(QB)]
        AFTER = [(c, b) for c in range(MOE_CHUNKS[-1] + 1, SC) for b in range(QB)]
        EU = E // (len(MOE_CHUNKS) * QB)
        UNIT_AFTER = (MOE_CHUNKS[-1] + 1) * QB
        COMBINE = {step: pair for pair, step in enumerate((1, 2, 3, 4, 6, 7, 8, 9))}
        GATE, UP, DOWN = range(3)
        GATE_UP, DOWNS = [(strip[3], strip[4])], [gen[1], pv]
        DOWNS_BEFORE = DOWNS + [gen[0], strip[2]]
        GATE_UP_AFTER, DOWNS_AFTER = GATE_UP + [(strip[2], gen[0])], DOWNS + strip[0:2]
        e_turn, e_gateup, e_out = gen[0], strip[0:2], strip[2]
        r_logitsT = (strip[2], gen[0])
        assert EU % EX == 0 and EU >= 2 * TB

        ROUTING = {2: [("scores", 0), ("best", 0)], 3: [("scores", 1), ("experts", 0)], 4: [("pick", 0), ("best", 1)],
                   5: [("experts", 1)], 6: [("place", 0), ("rows", 0)], 7: [("pick", 1)],
                   8: [("place", 1), ("rows", 1)]}
        PLACES = {5: 0, 8: 1}

        block = ctx.enter_context(nc.Block())

        @block.sync
        def _(sp):
            sp.dma_start(c_col[:], c_in.rearrange("o (c p) -> p (o c)", p=P),
                         allow_slow_non_contiguous=True).then_inc(c_landed, 16)
            wm = wmod.rearrange("(c p) n -> p c n", p=P)
            xt = x.rearrange("o (t p) d -> p (o t) d", p=P)
            w_dram = [w.rearrange("h (c p) d -> h p c d", p=P) for w in (Q_w, K_w, V_w)]
            w_dram.append(O_w.rearrange("h p (c d) -> h p c d", d=P))

            def load_x(b):
                sp.dma_start(acc[:, TB * b:TB * b + TB, :], xt[:, TB * b:TB * b + TB, :]).then_inc(x_landed[b], 16)

            for n, bias in enumerate((Q_b, K_b, V_b)):
                sp.dma_start(bias_rows[H * n:H * n + H, :], bias).then_inc(rows_landed, 16)
            sp.dma_start(wmod_sb[:, :, 0:2 * D], wm[:, :, 0:2 * D]).then_inc(mod_landed[0], 16)
            load_x(0)
            load_x(1)
            for n in range(3):
                sp.dma_start(raw[n][:], w_dram[n][0]).then_inc(raw_landed[n], 16)
            load_x(2)
            load_x(3)
            sp.dma_start(wmod_sb[:, :, 2 * D:3 * D], wm[:, :, 2 * D:3 * D]).then_inc(mod_landed[1], 16)
            sp.dma_start(gob[:], O_b.partition_broadcast(P)).then_inc(ob_landed, 16)
            sp.wait_ge(mod_mm, 3)
            sp.dma_start(wmod_sb[:, :, 0:2 * D], wm[:, :, 3 * D:5 * D]).then_inc(mod_landed[2], 16)
            sp.wait_ge(mod_mm, 4)
            sp.dma_start(wmod_sb[:, :, 2 * D:3 * D], wm[:, :, 5 * D:6 * D]).then_inc(mod_landed[3], 16)
            sp.wait_ge(w_split, 3)
            sp.dma_start(raw[3][:], w_dram[3][0]).then_inc(raw_landed[3], 16)
            with sp.Fori(0, H - 1) as h:
                for n in range(4):
                    sp.wait_ge(w_split, h * 4 + (1, 2, 4, 7)[n])
                    sp.dma_start(raw[n][:], w_dram[n][bass.ds(h + 1, 1)].rearrange("o p c d -> (o p) c d")
                                 ).then_inc(raw_landed[n], 16)
            n2v = n2_dram.rearrange("(b t p) d -> b p t d", p=P, t=TB)

            def store_n2(b):
                sp.wait_ge(ln_norm, NT + TB * b + TB)
                sp.dma_start(n2v[b], n2[:, b % 2]).then_inc(n2_stored[b % 2], 16)

            store_n2(0)

            def load_chunk(c):
                if c >= 1:
                    sp.wait_ge(sw_split, c)
                s, cols = c // (SC // NS), slice(c % (SC // NS) * P, c % (SC // NS) * P + P)
                for part, w in ((GATE, Sg), (UP, Su)):
                    sp.dma_start(s_raw[:, part, :].rearrange("p (c h) -> p c h", c=DC),
                                 w[s].rearrange("(c p) h -> p c h", p=P)[:, :, cols]).then_inc(sw_landed, 16)
                sp.dma_start(s_raw[:, DOWN, :], Sd[s][cols, :]).then_inc(sw_landed, 16)

            sp.wait_ge(strip_done, NSTRIP * (H - 1) + strips_before(QB - 1) + units(QB - 1))
            load_chunk(0)
            store_n2(1)
            store_n2(2)
            sp.wait_ge(gen_out, GENS + OUTS_END + TB)
            sp.dma_start(wr_sb[:], Wr.rearrange("(c p) e -> p c e", p=P)).then_inc(wr_landed, 16)
            sp.dma_start(rb_bc[:], router_bias.partition_broadcast(P)).then_inc(rb_landed, 16)
            sp.wait_ge(consts, 5)
            sp.dma_start(table_dram[0:TRASH, :].rearrange("(p e) o -> p (e o)", p=P), zeros_i[:]
                         ).then_inc(zero_stored, 16)
            load_chunk(1)
            store_n2(3)
            for c in range(2, MOE_CHUNKS[0]):
                load_chunk(c)
            sp.wait_ge(routed, 2)
            wg_dram, wu_dram = (w.rearrange("e (c p) h -> e p c h", p=P) for w in (Wg, Wu))

            def load_expert(i, e):
                for dst, src in ((wg_sb, wg_dram), (wu_sb, wu_dram)):
                    sp.dma_start(dst[:, i, :, :], src[bass.ds(e, 1)].rearrange("o p c h -> (o p) c h")
                                 ).then_inc(e_landed[i], 16)
                sp.dma_start(wd_sb[:, i, :], Wd[bass.ds(e, 1)].rearrange("o p d -> (o p) d")).then_inc(e_landed[i], 16)

            for i in range(EX):
                load_expert(i, i)
            for c in MOE_CHUNKS:
                load_chunk(c)
            sp.wait_ge(scattered, 16 * NT * TOPK)
            sp.dma_start(table[:], table_dram[0:TRASH, :].rearrange("(s e) o -> s (e o)", e=E)
                         ).then_inc(table_landed, 16)
            load_chunk(MOE_CHUNKS[-1] + 1)
            ybv = yb_dram.rearrange("(e s) d -> e s d", s=CAP)

            def store_yb(i, g):
                sp.wait_ge(yb_ready, g * EX + (EX + i + 1))
                sp.dma_start(ybv[bass.ds(g * EX + i, 1)].rearrange("o s d -> (o s) d"), yb[:, i, :]
                             ).then_inc(yb_stored[i], 16)

            with sp.Fori(0, E // EX - 1) as g:
                for i in range(EX):
                    sp.wait_ge(e_down, g * EX + (i + 1))
                    load_expert(i, g * EX + (EX + i))
                    store_yb(i, g)
            for i in range(EX):
                store_yb(i, E // EX - 1)
            for c in range(MOE_CHUNKS[-1] + 2, SC):
                load_chunk(c)
            ov = out.rearrange("o (t p) d -> (o t) p d", p=P)
            sp.wait_ge(combined, NT)
            with sp.Fori(0, NT) as t:
                sp.wait_ge(down_out, t + (NT * (SC - 1) + 1))
                sp.dma_start(ov[bass.ds(t, 1)].rearrange("o p d -> (o p) d"), acc[:, bass.ds(t, 1), :]
                             .rearrange("p o d -> p (o d)")).then_inc(out_stored, 16)
            sp.wait_ge(out_stored, 16 * NT)

        @block.gpsimd
        def _(pool):
            steps = [0]

            def link(ins):
                steps[0] += 1
                ins.then_inc(pool_step, 1)
                pool.wait_ge(pool_step, steps[0])

            def wait_alone(semaphore, value):
                pool.wait_ge(semaphore, value)
                pool.sem_inc(pool_waited, 1)

            link(nc.gpsimd.memset(ident[:], 0.0))
            nc.gpsimd.affine_select(out=ident[:], in_=ident[:], compare_op=ALU.not_equal, fill=1.0, base=0,
                                    pattern=[[-1, P]], channel_multiplier=1).then_inc(consts, 1)
            link(nc.gpsimd.memset(ident_bf[:], 0.0))
            nc.gpsimd.affine_select(out=ident_bf[:], in_=ident_bf[:], compare_op=ALU.not_equal, fill=1.0, base=0,
                                    pattern=[[-1, P]], channel_multiplier=1).then_inc(consts, 1)
            link(nc.gpsimd.memset(mask_bf[:], 0.0))
            nc.gpsimd.affine_select(out=mask_bf[:], in_=mask_bf[:], compare_op=ALU.is_ge, fill=MASKED, base=0,
                                    pattern=[[-1, P]], channel_multiplier=1).then_inc(consts, 1)
            nc.gpsimd.memset(neghalf[:], -0.5).then_inc(consts, 1)

            def ln_scales(base, b):
                pool.wait_ge(ln_stats, base + TB * b + TB)
                tiles = slice(TB * b, TB * b + TB)
                link(nc.gpsimd.tensor_scalar(veps[:, tiles], meanvar[:, tiles, 1], EPS, None, ALU.add))
                nc.gpsimd.tensor_tensor(rstd[:, tiles], veps[:, tiles], neghalf[:, tiles], ALU.pow
                                        ).then_inc(ln_rstd, 1)

            def ln_lo(b):
                for ch in range(DC):
                    pool.wait_ge(ln_mod, DC * b + ch + 1)
                    cols = slice(512 * b, 512 * b + 512)
                    nc.gpsimd.tensor_tensor(hT_lo[:, ch, cols], h_tmp[:, ch, :], hT_hi[:, ch, cols].bitcast(F32),
                                            ALU.subtract).then_inc(ln_split, 1)

            def split_lo(n, h):
                pool.wait_ge(w_hi, h * 4 + (n + 1))
                nc.gpsimd.tensor_tensor(w_lo_t[n][:], raw[n][:], w_hi_t[n][:].bitcast(F32), ALU.subtract
                                        ).then_inc(w_split, 1)

            def take_bias(h):
                src = biasT[:].rearrange("p (n h) -> p n h", n=3)[:, :, bass.ds(h, 1)].rearrange("p n o -> p (n o)")
                nc.gpsimd.tensor_copy(bias_now[:], src).then_inc(bias_ready, 1)

            def scale_wo(h):
                pool.wait_ge(raw_landed[3], h * 16 + 16)
                w = raw[3][:].rearrange("p c d -> p (c d)")
                nc.gpsimd.tensor_tensor(w, w, ga_bc[:], ALU.mult).then_inc(wo_scaled, 1)

            pool.wait_ge(consts, 4)
            ln_scales(0, 0)
            pool.wait_ge(mod_out, 1)
            nc.gpsimd.tensor_copy(bias_now[:], biasT[:].rearrange("p (n h) -> p n h", n=3)[:, :, 0]
                                  ).then_inc(bias_ready, 1)
            ln_scales(0, 1)
            for n in range(3):
                split_lo(n, 0)
            ln_lo(0)
            ln_scales(0, 2)
            ln_scales(0, 3)
            ln_lo(1)
            ln_lo(2)
            ln_lo(3)
            pool.wait_ge(gob_ready, 1)
            pool.wait_ge(ln_norm, NT)
            for t in list(range(NT - TB, NT)) + list(range(NT - TB)):
                nc.gpsimd.tensor_tensor(acc[:, t, :], acc[:, t, :], gob[:], ALU.add).then_inc(resid, 1)

            with pool.Fori(0, H - 1) as h:
                scale_wo(h)
                split_lo(3, h)
                split_lo(0, h + 1)
                split_lo(1, h + 1)
                split_lo(2, h + 1)
                take_bias(h + 1)
            scale_wo(H - 1)
            split_lo(3, H - 1)

            for b in range(QB):
                ln_scales(NT, b)
            pool.wait_ge(gen_out, GENS + OUTS_END + TB)
            nc.gpsimd.memset(zeros_i[:], 0).then_inc(consts, 1)
            link(nc.gpsimd.memset(tri_bf[:], 0.0))
            nc.gpsimd.affine_select(out=tri_bf[:], in_=tri_bf[:], compare_op=ALU.is_ge, fill=1.0, base=0,
                                    pattern=[[-1, P]], channel_multiplier=1).then_inc(consts, 1)
            nc.gpsimd.memset(ones_bf[:], 1.0).then_inc(consts, 1)
            nc.gpsimd.iota(iota_i[:], [[1, E]], base=0, channel_multiplier=0).then_inc(consts, 1)
            nc.gpsimd.iota(tok_i[:], [[P, NT]], base=0, channel_multiplier=1).then_inc(consts, 1)
            nc.gpsimd.iota(trash_i[:], [[P * TOPK, NT], [1, TOPK]], base=TRASH, channel_multiplier=TOPK
                           ).then_inc(consts, 1)

            pool.wait_ge(zero_stored, 16)
            pool.wait_ge(consts, 10)
            for t in range(NT):
                if t % (NT // 2) == 0:
                    pool.wait_ge(routed, t // (NT // 2) + 1)
                for k in range(TOPK):
                    nc.gpsimd.indirect_dma_start(
                        out=table_dram, out_offset=bass.IndirectOffsetOnAxis(ap=scat_u[:, t, k:k + 1], axis=0),
                        in_=tok_i[:, t:t + 1], in_offset=None).then_inc(scattered, 16)
            pool.wait_ge(table_landed, 16)
            pool.wait_ge(n2_stored[0], 32)
            pool.wait_ge(n2_stored[1], 32)
            with pool.Fori(0, E // EX) as g:
                for i in range(EX):
                    wait_alone(xb_turned, g * EX + (i + 1))
                    nc.gpsimd.tensor_copy(tok_now[:, i:i + 1], table[:, bass.ds(g * EX + i, 1)]).then_inc(tok_ready, 1)
                    wait_alone(tok_ready, g * EX + (i + 1))
                    nc.gpsimd.indirect_dma_start(
                        out=xb[:, i, :], out_offset=None, in_=n2_dram,
                        in_offset=bass.IndirectOffsetOnAxis(ap=tok_now[:, i:i + 1], axis=0)).then_inc(xb_landed[i], 16)
            for i in range(EX):
                pool.wait_ge(yb_stored[i], 16 * (E // EX + 1))
            with pool.Fori(0, NT // GATHS) as g:
                for i in range(GATHS):
                    wait_alone(gath_free, g * GATHS + (i + 1))
                    nc.gpsimd.tensor_copy(slot_now[:, i, :], slot_u[:, bass.ds(g * GATHS + i, 1), :]
                                          .rearrange("p o k -> p (o k)")).then_inc(slot_ready, 1)
                    wait_alone(slot_ready, g * GATHS + (i + 1))
                    for k in range(TOPK):
                        nc.gpsimd.indirect_dma_start(
                            out=gath[i][:, k, :], out_offset=None, in_=yb_dram,
                            in_offset=bass.IndirectOffsetOnAxis(ap=slot_now[:, i, k:k + 1], axis=0)
                        ).then_inc(g_landed[i], 16)

        @block.scalar
        def _(act):
            act.wait_ge(c_landed, 16)
            nc.scalar.activation(c_exp[:], c_col[:], ACT.Exp, scale=-1.0).then_inc(c_act, 1)

            def ln_modulate(b):
                for ch in range(DC):
                    act.wait_ge(ln_turned, DC * b + ch + 1)
                    if b >= 1:
                        act.wait_ge(ln_split, DC * (b - 1) + ch + 1)
                    nc.scalar.activation(hT_hi[:, ch, 512 * b:512 * b + 512], strip[ch][:], ACT.Identity,
                                         bias=modT[:, ch:ch + 1], scale=scale_a[:, ch:ch + 1])
                    nc.scalar.activation(h_tmp[:, ch, :], strip[ch][:], ACT.Identity,
                                         bias=modT[:, ch:ch + 1], scale=scale_a[:, ch:ch + 1]).then_inc(ln_mod, 1)

            def split_hi(n):
                nc.scalar.activation(w_hi_t[n][:], raw[n][:], ACT.Copy).then_inc(w_hi, 1)

            def gen_hi_of(kind, j, h):
                act.wait_ge(gen_done, nth(kind, j, 0, h))
                src = bank_of(kind, j, 0)
                if kind == "q":
                    act.wait_ge(bias_ready, h + (2 if j == 0 else 1))
                    ins = nc.scalar.activation(qT_hi[:], src[:], ACT.Identity, bias=bias_now[:, 0:1])
                elif kind == "k":
                    ins = nc.scalar.activation(kT_hi[:, 512 * j:512 * j + 512], src[:], ACT.Identity,
                                               bias=bias_now[:, 1:2])
                else:
                    ins = nc.scalar.activation(v_hi[:, TB * j:TB * j + TB, :],
                                               src[:].rearrange("p (t d) -> p t d", t=TB), ACT.Copy)
                ins.then_inc(gen_hi, 1)

            def exp_rows(j, h):
                for t in range(TB):
                    act.wait_ge(row_logits, h * NT + (TB * j + t + 1))
                    w = (TB * j + t + 1) * P
                    row = probs[:, row_at[t]:row_at[t] + w]
                    nc.scalar.activation(row, row, ACT.Exp, bias=nbias[:, t:t + 1],
                                         accum_out=rsum[:, TB * j + t:TB * j + t + 1]).then_inc(row_probs, 1)

            def split_chunk_hi(c):
                act.wait_ge(sw_scaled, c + 1)
                if c >= 2:
                    act.wait_ge(down_done, NT * (c - 1))
                nc.scalar.activation(s_hi[c % 2][:], s_raw[:], ACT.Copy).then_inc(sw_hi, 1)

            def turned_hi(j, h, last):
                for kk in range(units(j)):
                    u = strips_before(j) + units(j) + kk
                    act.wait_ge(strip_done, h * NSTRIP + (u + 1))
                    if kk >= PTS:
                        act.wait_ge(pv_done, h * NTURN + (turned_before(j) + kk - PTS + 1))
                    c0 = first_col(j, kk)
                    nc.scalar.activation(pT_hi[:, kk % PTS, c0:512], strip[u % STRIPS][:, c0:512], ACT.Copy
                                         ).then_inc(pt_hi, 1)
                    if last and (j, kk) in LN2_CHUNKS:
                        ln2_mod(*LN2_CHUNKS[j, kk])
                    if last and (j, kk) == CHUNK_HI:
                        split_chunk_hi(0)
                act.wait_ge(pv_done, h * NTURN + turned_before(j + 1))
                nc.scalar.activation(at_hi[:], pv[:], ACT.Copy).then_inc(attn_hi, 1)

            def ln2_mod(b, ch):
                n = NT + DC * b + ch
                act.wait_ge(ln_turned, n + 1)
                if n > NT:
                    act.wait_ge(ln_split, n if b == 0 else n - 1)
                src = ln2_bank(b, ch)
                nc.scalar.activation(h2T_hi[:, ch, 512 * b:512 * b + 512], src[:], ACT.Identity,
                                     bias=modT[:, 3 * DC + ch:3 * DC + ch + 1], scale=scale_b[:, ch:ch + 1])
                nc.scalar.activation(ln2_tmp(b, ch)[:], src[:], ACT.Identity,
                                     bias=modT[:, 3 * DC + ch:3 * DC + ch + 1], scale=scale_b[:, ch:ch + 1]
                                     ).then_inc(ln_mod, 1)

            def head(h, last):
                for j in range(QB):
                    gen_hi_of("t", j, h)
                    if j == QB - 1 and not last:
                        act.wait_ge(gen_out, nth("v", QB - 1, 0, h) + GENS)
                        for n in range(3):
                            act.wait_ge(raw_landed[n], h * 16 + 32)
                            split_hi(n)
                    exp_rows(j, h)
                    if j < QB - 1 or not last:
                        gen_hi_of("q", (j + 1) % QB, h)
                        gen_hi_of("k", (j + 1) % QB, h)
                    turned_hi(j, h, last)
                    if j == 0:
                        act.wait_ge(wo_scaled, h + 1)
                        act.wait_ge(gen_done, nth("o", QB - 1, TB - 1, h))
                        split_hi(3)

            for n in range(3):
                act.wait_ge(raw_landed[n], 16)
                split_hi(n)
            act.wait_ge(mod_out, 2)
            ln_modulate(0)
            ln_modulate(1)
            gen_hi_of("q", 0, -1)
            ln_modulate(2)
            gen_hi_of("k", 0, -1)
            ln_modulate(3)
            act.wait_ge(attn_split, 1)
            with act.Fori(0, H - 1) as h:
                head(h, False)
            head(H - 1, True)

            def shared_silu(n, buf, gate):
                act.wait_ge(gate_done, n + 1)
                nc.scalar.activation(sil_s[:, buf, :], gate[:], ACT.Silu).then_inc(silu_done, 1)

            def shared_hi(n, buf):
                act.wait_ge(hs_whole, n + 1)
                nc.scalar.activation(hs_hi[:, buf, :], sil_s[:, buf, :], ACT.Copy).then_inc(hs_hi_ready, 1)

            def router_beside(step):
                if step == 0:
                    act.wait_ge(wr_landed, 16)
                    nc.scalar.activation(wr_hi[:], wr_sb[:], ACT.Copy).then_inc(wr_hi_ready, 1)
                    for ch in range(DC):
                        ln2_mod(2, ch)
                if step == 1:
                    for ch in range(DC):
                        ln2_mod(3, ch)
                if step in (1, 2):
                    for b in (2 * step - 2, 2 * step - 1):
                        act.wait_ge(logitsT_mm, b + 1)
                        nc.scalar.activation(logitsT[:, b % 2, :], r_logitsT[b % 2][0:E, :], ACT.Copy
                                             ).then_inc(logitsT_out, 1)
                if step in (2, 3):
                    tiles = slice(NT // 2 * (step - 2), NT // 2 * (step - 1))
                    act.wait_ge(r_shift, step - 1)
                    nc.scalar.activation(scores[:, tiles], prod[:, tiles], ACT.Exp).then_inc(r_exp, 1)

            def shared_units(pairs, gate_up, beside):
                for step, (c, b) in enumerate(pairs):
                    n = c * QB + b
                    shared_silu(n, n % 2, gate_up[n % len(gate_up)][0])
                    if b == 1 and c + 1 < SC:
                        split_chunk_hi(c + 1)
                    shared_hi(n, n % 2)
                    beside(step)

            shared_units(BEFORE, GATE_UP, router_beside)

            def expert_T(e, i):
                act.wait_ge(xb_turned, e + (EX + 1))
                for ch in range(DC):
                    ins = nc.scalar.activation(xbT[:, i % 2, P * ch:P * ch + P], e_turn[:, P * ch:P * ch + P],
                                               ACT.Identity, bias=modT[:, 3 * DC + ch:3 * DC + ch + 1],
                                               scale=scale_b[:, ch:ch + 1])
                ins.then_inc(xbT_ready, 1)

            def expert_silu(e, i):
                act.wait_ge(e_gu, e + 1)
                nc.scalar.activation(sil_e[:, i % 2, :], e_gateup[i % 2][:, 0:P], ACT.Silu).then_inc(e_silu, 1)

            act.sem_inc(xbT_ready, 1)
            for m, c in enumerate(MOE_CHUNKS):
                split_chunk_hi(c + 1)
                with act.Fori(0, QB) as b:
                    first = b * EU + m * QB * EU
                    n = b + c * QB
                    expert_T(first, 0)
                    shared_silu(n, 0, GATE_UP[0][0])
                    for i in range(EU):
                        if i + 1 < EU:
                            expert_T(first + (i + 1), i + 1)
                        expert_silu(first + i, i)
                        if i == 1:
                            shared_hi(n, 0)
            shared_units(AFTER, GATE_UP_AFTER, lambda step: None)

        @block.vector
        def _(dve):
            steps = [0]

            def link(ins):
                steps[0] += 1
                ins.then_inc(dve_step, 1)
                dve.wait_ge(dve_step, steps[0])

            for t in (at_hi, at_lo):
                nc.vector.memset(t[:].bitcast(F32), 0.0).then_inc(c_step, 1)
            for t in (w_hi_t[3], w_lo_t[3]):
                nc.vector.memset(t[:].bitcast(F32), 0.0).then_inc(c_step, 1)
            nc.vector.memset(rinv[:], 0.0).then_inc(rinv_ready, 1)

            dve.wait_ge(c_act, 1)
            link(nc.vector.tensor_scalar(c_sig[:], c_exp[:], 1.0, None, ALU.add))
            link(nc.vector.reciprocal(c_sig[:], c_sig[:]))
            link(nc.vector.tensor_tensor(sc_col[:], c_col[:], c_sig[:], ALU.mult))
            nc.vector.tensor_copy(sc_bc[:], sc_col[:].unsqueeze(2).to_broadcast([P, DC, P])).then_inc(c_step, 1)

            def ln_stat(base, b):
                for t in range(TB * b, TB * b + TB):
                    ins = nc.vector.bn_stats(stats[:, t, :], acc[:, t, :])
                    if t < TB * b + TB - 1:
                        steps[0] += 1
                        ins.then_inc(dve_step, 1)
                    else:
                        link(ins)
                for t in range(TB * b, TB * b + TB):
                    nc.vector.bn_aggr(meanvar[:, t, :], stats[:, t, :]).then_inc(ln_stats, 1)

            def ln_normalise(base, b, dst):
                dve.wait_ge(ln_rstd, base // TB + b + 1)
                dve.wait_ge(ln_stats, base + TB * b + TB)
                if b >= 2:
                    dve.wait_ge(ln_turned, base + DC * (b - 2) + DC)
                for t in range(TB):
                    i = TB * b + t
                    nc.vector.tensor_scalar(dst[:, b % 2, t, :], acc[:, i, :], meanvar[:, i, 0:1], rstd[:, i:i + 1],
                                            ALU.subtract, ALU.mult).then_inc(ln_norm, 1)

            def columns(first, src):
                tmp = mod_tmp[:, 0, :].rearrange("p (c d) -> p c d", c=DC)
                link(nc.vector.tensor_tensor(tmp, src[:].rearrange("p (c d) -> p c d", c=DC),
                                             ident[:].unsqueeze(1).to_broadcast([P, DC, P]), ALU.mult))
                link(nc.vector.tensor_reduce(modT[:, first:first + DC], tmp, AX_X, ALU.add))

            def scale_of(first, dst):
                nc.vector.tensor_scalar(dst[:], modT[:, first:first + DC], 1.0, None, ALU.add).then_inc(mod_out, 1)

            def gate(src, dst):
                link(nc.vector.tensor_scalar(mod_tmp[:, 0, :], src, 0.0, 2.0, ALU.is_ge, ALU.mult))
                link(nc.vector.scalar_tensor_tensor(mod_tmp[:, 1, :], mod_tmp[:, 0, :], -1.0, src, ALU.add, ALU.mult))
                link(nc.vector.tensor_scalar(mod_tmp[:, 1, :], mod_tmp[:, 1, :], 0.25, None, ALU.max))
                link(nc.vector.scalar_tensor_tensor(dst[:], mod_tmp[:, 0, :], -1.0, mod_tmp[:, 1, :], ALU.add,
                                                    ALU.mult))

            def gen_out_of(kind, j, t, h):
                src = bank_of(kind, j, t)
                if kind in "qkt":
                    dve.wait_ge(gen_hi, nth_hi(kind, j, h))
                else:
                    dve.wait_ge(gen_done, nth(kind, j, t, h))
                if kind == "q":
                    ins = nc.vector.scalar_tensor_tensor(qT_lo[:], src[:], bias_now[:, 0:1], qT_hi[:].bitcast(F32),
                                                         ALU.add, ALU.subtract)
                elif kind == "k":
                    cols = slice(512 * j, 512 * j + 512)
                    ins = nc.vector.scalar_tensor_tensor(kT_lo[:, cols], src[:], bias_now[:, 1:2],
                                                         kT_hi[:, cols].bitcast(F32), ALU.add, ALU.subtract)
                elif kind == "v":
                    ins = nc.vector.tensor_scalar(vT_f[:], src[:], bias_now[:, 2:3], None, ALU.add)
                elif kind == "t":
                    rows = slice(TB * j, TB * j + TB)
                    ins = nc.vector.tensor_tensor(v_lo[:, rows, :], src[:].rearrange("p (t d) -> p t d", t=TB),
                                                  v_hi[:, rows, :].bitcast(F32), ALU.subtract)
                else:
                    i = TB * j + t
                    if t == 0:
                        dve.wait_ge(rinv_ready, h * QB + (1 if j == QB - 1 else j + 2))
                        dve.wait_ge(resid, TB if j == QB - 1 else NT)
                    ins = nc.vector.scalar_tensor_tensor(acc[:, i, :], src[:], rinv[:, i:i + 1], acc[:, i, :],
                                                         ALU.mult, ALU.add)
                ins.then_inc(gen_out, 1)

            def scores_out(j, h):
                for n, (t, ch, w) in enumerate(score_units(j)):
                    u = strips_before(j) + n
                    dve.wait_ge(strip_done, h * NSTRIP + (u + 1))
                    at = row_at[t] + 512 * ch
                    nc.vector.tensor_scalar(probs[:, at:at + w], strip[u % STRIPS][:, 0:w], SCALE, None, ALU.mult,
                                            ALU.max, accum_out=cmax[:, t, ch:ch + 1]).then_inc(strip_out, 1)
                    if ch == j:
                        dve.wait_ge(strip_out, h * NSTRIP + (STRIPS + u + 1))
                        nc.vector.tensor_reduce(nbias[:, t:t + 1], cmax[:, t, 0:j + 1], AX_X, ALU.max, negate=True
                                                ).then_inc(row_logits, 1)

            def ln2_rows(b):
                if b >= 2:
                    dve.wait_ge(n2_stored[b % 2], 16)
                ln_normalise(NT, b, n2)

            def ln2_lo(b, ch):
                dve.wait_ge(ln_mod, NT + DC * b + ch + 1)
                cols = slice(512 * b, 512 * b + 512)
                nc.vector.tensor_tensor(h2T_lo[:, ch, cols], ln2_tmp(b, ch)[:], h2T_hi[:, ch, cols].bitcast(F32),
                                        ALU.subtract).then_inc(ln_split, 1)

            def scale_chunk(c):
                dve.wait_ge(sw_landed, 48 * (c + 1))
                nc.vector.tensor_tensor(s_raw[:, DOWN, :], s_raw[:, DOWN, :], gb_bc[:], ALU.mult).then_inc(sw_scaled, 1)

            def split_chunk_lo(c):
                dve.wait_ge(sw_hi, c + 1)
                nc.vector.tensor_tensor(s_lo[c % 2][:], s_raw[:], s_hi[c % 2][:].bitcast(F32), ALU.subtract
                                        ).then_inc(sw_split, 1)

            def turned_lo(j, h, last):
                for kk in range(units(j)):
                    u = strips_before(j) + units(j) + kk
                    dve.wait_ge(pt_hi, h * NTURN + (turned_before(j) + kk + 1))
                    c0 = first_col(j, kk)
                    nc.vector.tensor_tensor(pT_lo[:, kk % PTS, c0:512], strip[u % STRIPS][:, c0:512],
                                            pT_hi[:, kk % PTS, c0:512].bitcast(F32), ALU.subtract
                                            ).then_inc(strip_out, 1)
                    if 0 <= kk - AHEAD < TB:
                        gen_out_of("o", (j - 1) % QB, kk - AHEAD, h)
                    if last and (j, kk) in LN2_STATS:
                        b = LN2_STATS[j, kk]
                        dve.wait_ge(gen_out, nth("o", b, TB - 1, h) + GENS)
                        ln_stat(NT, b)
                    if last and (j, kk) in LN2_ROWS:
                        ln2_rows(LN2_ROWS[j, kk])
                    if last and (j, kk) in LN2_CHUNKS:
                        ln2_lo(*LN2_CHUNKS[j, kk])
                    if last and (j, kk) == CHUNK_SCALED:
                        scale_chunk(0)
                    if last and (j, kk) == CHUNK_LO:
                        split_chunk_lo(0)
                for t in range(units(j) - AHEAD, TB):
                    gen_out_of("o", (j - 1) % QB, t, h)
                dve.wait_ge(attn_hi, h * QB + (j + 1))
                nc.vector.tensor_tensor(at_lo[:], pv[:], at_hi[:].bitcast(F32), ALU.subtract).then_inc(attn_split, 1)
                nc.vector.reciprocal(rinv[:, TB * j:TB * j + TB], rsum[:, TB * j:TB * j + TB]).then_inc(rinv_ready, 1)

            def head(h, last):
                for j in range(QB):
                    gen_out_of("t", j, 0, h)
                    scores_out(j, h)
                    if j < QB - 1 or not last:
                        for kind in "qkv":
                            gen_out_of(kind, (j + 1) % QB, 0, h)
                    else:
                        dve.wait_ge(gen_out, nth("t", j, 0, h) + GENS)
                        dve.sem_inc(gen_done, 3)
                        dve.sem_inc(gen_out, 3)
                        ln_stat(NT, 1)
                        ln2_rows(1)
                    turned_lo(j, h, last)

            def ln_stat_of(b):
                dve.wait_ge(x_landed[b], 16)
                ln_stat(0, b)

            dve.wait_ge(mod_mm, 1)
            nc.vector.tensor_copy(biasT[:], pv[:, 0:3 * H]).then_inc(mod_out, 1)
            ln_stat_of(0)
            ln_stat_of(1)
            ln_normalise(0, 0, n1)
            dve.wait_ge(mod_mm, 2)
            columns(0, gen[0])
            dve.wait_ge(mod_mm, 3)
            columns(DC, gen[1])
            scale_of(DC, scale_a)
            dve.wait_ge(mod_out, 2)
            dve.sem_inc(gen_out, GENS)
            ln_normalise(0, 1, n1)
            ln_stat_of(2)
            ln_stat_of(3)
            ln_normalise(0, 2, n1)
            gen_out_of("q", 0, 0, -1)
            ln_normalise(0, 3, n1)
            dve.wait_ge(mod_mm, 4)
            gate(strip[4][:], ga_bc)
            dve.sem_inc(mod_out, 1)
            dve.wait_ge(mod_mm, 5)
            columns(3 * DC, pv)
            dve.sem_inc(mod_out, 1)
            dve.wait_ge(mod_mm, 6)
            columns(4 * DC, strip[4])
            scale_of(4 * DC, scale_b)
            gen_out_of("k", 0, 0, -1)
            dve.wait_ge(ob_landed, 16)
            nc.vector.tensor_tensor(gob[:], ga_bc[:], gob[:], ALU.mult).then_inc(gob_ready, 1)
            dve.wait_ge(mod_mm, 7)
            gate(pv[:], gb_bc)
            gen_out_of("v", 0, 0, -1)
            dve.wait_ge(mod_out, 5)
            dve.wait_ge(gob_ready, 1)
            dve.wait_ge(ln_split, NT)
            dve.wait_ge(c_step, 5)
            dve.wait_ge(rinv_ready, 1)
            dve.sem_inc(strip_out, STRIPS)
            dve.sem_inc(attn_split, 1)
            dve.wait_ge(gen_out, nth("v", 0, 0, -1) + GENS)
            dve.sem_inc(gen_done, TB)
            dve.sem_inc(gen_out, TB)
            with dve.Fori(0, H - 1) as h:
                head(h, False)
            head(H - 1, True)
            dve.wait_ge(rinv_ready, QB * H + 1)
            for t in range(TB):
                dve.wait_ge(gen_done, OUTS_END + t + 1)
                i = NT - TB + t
                nc.vector.scalar_tensor_tensor(acc[:, i, :], gen[t % GENS][:], rinv[:, i:i + 1], acc[:, i, :],
                                               ALU.mult, ALU.add).then_inc(gen_out, 1)

            dve.wait_ge(gen_out, GENS + OUTS_END + TB)
            ln2_rows(2)
            ln_stat(NT, QB - 1)

            def shared_mult(n, buf, up):
                dve.wait_ge(up_done, n + 1)
                dve.wait_ge(silu_done, n + 1)
                nc.vector.tensor_tensor(sil_s[:, buf, :], up[:], sil_s[:, buf, :], ALU.mult).then_inc(hs_whole, 1)

            def shared_lo(n, buf):
                dve.wait_ge(hs_hi_ready, n + 1)
                nc.vector.tensor_tensor(hs_lo[:, buf, :], sil_s[:, buf, :], hs_hi[:, buf, :].bitcast(F32),
                                        ALU.subtract).then_inc(hs_split, 1)

            def shared_out(n, tile, t, downs):
                dve.wait_ge(down_done, n * TB + (t + 1))
                row = acc[:, bass.ds(tile, 1), :].rearrange("p o d -> p (o d)")
                nc.vector.tensor_tensor(row, downs[t % len(downs)][:], row, ALU.add).then_inc(down_out, 1)

            def shared_units(pairs, gate_up, downs, beside):
                for step, (c, b) in enumerate(pairs + [(None, None)]):
                    if step >= 1:
                        pc, pb = pairs[step - 1]
                        pn = pc * QB + pb
                        shared_outs = [(pn, pb * TB + t, t, downs if pn >= QB else DOWNS) for t in range(TB)]
                        for args in shared_outs[0:2]:
                            shared_out(*args)
                    if c is not None:
                        n = c * QB + b
                        shared_mult(n, n % 2, gate_up[n % len(gate_up)][1])
                    if step >= 1:
                        for args in shared_outs[2:4]:
                            shared_out(*args)
                    if c is not None:
                        shared_lo(n, n % 2)
                        if b == 0 and c + 1 < SC:
                            scale_chunk(c + 1)
                        if b == 1 and c + 1 < SC:
                            split_chunk_lo(c + 1)
                    beside(step)

            half = NT // 2
            mx, total, inv, inv4 = r_stat
            t0, t1, t2 = r_tmp

            def tiles_of(s):
                return slice(half * s, half * s + half)

            def wide(t, s):
                return t[:, tiles_of(s)].unsqueeze(2).to_broadcast([P, half, E])

            def in_bank(s):
                return strip[s][:].rearrange("p (t e) -> p t e", e=E)

            def route_scores(s):
                m = tiles_of(s)
                dve.wait_ge(rb_landed, 16)
                dve.wait_ge(logits_mm, 2 * s + 2)
                link(nc.vector.tensor_tensor(scores[:, m], in_bank(s), rb_bc[:].unsqueeze(1).to_broadcast([P, half, E]),
                                             ALU.add))
                link(nc.vector.tensor_reduce(mx[:, m], scores[:, m], AX_X, ALU.max))
                nc.vector.tensor_tensor(prod[:, m], scores[:, m], wide(mx, s), ALU.subtract).then_inc(r_shift, 1)

            def route_best(s):
                m = tiles_of(s)
                dve.wait_ge(r_exp, s + 1)
                link(nc.vector.tensor_reduce(total[:, m], scores[:, m], AX_X, ALU.add))
                link(nc.vector.reciprocal(inv[:, m], total[:, m]))
                link(nc.vector.tensor_tensor(scores[:, m], scores[:, m], wide(inv, s), ALU.mult))
                for t in range(half * s, half * s + half):
                    steps[0] += 1
                    nc.vector.max(vals[:, t, :], scores[:, t, :]).then_inc(dve_step, 1)
                dve.wait_ge(dve_step, steps[0])

            def route_experts(s):
                m = tiles_of(s)
                if s == 0:
                    dve.wait_ge(consts, 10)
                    link(nc.vector.tensor_copy(iota_f[:], iota_i[:]))
                for t in range(half * s, half * s + half):
                    steps[0] += 1
                    nc.vector.max_index(idx[:, t, :], vals[:, t, :], scores[:, t, :]).then_inc(dve_step, 1)
                dve.wait_ge(dve_step, steps[0])
                link(nc.vector.tensor_copy(idx_f[:, m], idx[:, m, 0:TOPK]))
                for k in range(TOPK):
                    link(nc.vector.tensor_tensor(onehot[k][:, m], iota_f[:].unsqueeze(1).to_broadcast([P, half, E]),
                                                 idx_f[:, m, k:k + 1].to_broadcast([P, half, E]), ALU.is_equal))

            def route_pick(s):
                m = tiles_of(s)
                link(nc.vector.tensor_tensor(picked[:, m], onehot[0][:, m], onehot[1][:, m], ALU.add))
                link(nc.vector.tensor_tensor(picked[:, m], picked[:, m], onehot[2][:, m], ALU.add))
                nc.vector.tensor_tensor(picked[:, m], picked[:, m], onehot[3][:, m], ALU.add).then_inc(picked_ready, 1)
                link(nc.vector.tensor_reduce(total[:, m], vals[:, m, 0:TOPK], AX_X, ALU.add))
                link(nc.vector.reciprocal(inv4[:, m], total[:, m]))
                link(nc.vector.tensor_tensor(w_top[:, m], vals[:, m, 0:TOPK],
                                             inv4[:, m].unsqueeze(2).to_broadcast([P, half, TOPK]), ALU.mult))

            def route_place(s):
                m = tiles_of(s)
                dve.wait_ge(pos_mm, s + 1)
                link(nc.vector.tensor_copy(pos[:, m], in_bank(s)))
                for k in range(TOPK):
                    link(nc.vector.tensor_tensor(prod[:, m], onehot[k][:, m], pos[:, m], ALU.mult))
                    link(nc.vector.tensor_reduce(pos_k[:, m, k], prod[:, m], AX_X, ALU.add))

            def route_rows(s):
                m = tiles_of(s)
                link(nc.vector.tensor_scalar(valid[:, m], pos_k[:, m], float(CAP), None, ALU.is_lt))
                link(nc.vector.tensor_tensor(w_top[:, m], w_top[:, m], valid[:, m], ALU.mult))
                link(nc.vector.tensor_scalar(t0[:, m], pos_k[:, m], float(CAP - 1), None, ALU.min))
                link(nc.vector.scalar_tensor_tensor(t1[:, m], idx_f[:, m], float(CAP), t0[:, m], ALU.mult, ALU.add))
                link(nc.vector.tensor_copy(slot_u[:, m], t1[:, m]))
                link(nc.vector.scalar_tensor_tensor(t0[:, m], pos_k[:, m], float(E), idx_f[:, m], ALU.mult, ALU.add))
                link(nc.vector.tensor_copy(t1[:, m], trash_i[:, m]))
                link(nc.vector.tensor_tensor(t0[:, m], t0[:, m], t1[:, m], ALU.subtract))
                link(nc.vector.tensor_tensor(t2[:, m], t0[:, m], valid[:, m], ALU.mult))
                link(nc.vector.tensor_tensor(t0[:, m], t2[:, m], t1[:, m], ALU.add))
                nc.vector.tensor_copy(scat_u[:, m], t0[:, m]).then_inc(routed, 1)

            def ffn_beside(step):
                if step == 0:
                    dve.wait_ge(wr_hi_ready, 1)
                    nc.vector.tensor_tensor(wr_lo[:], wr_sb[:], wr_hi[:].bitcast(F32), ALU.subtract
                                            ).then_inc(wr_split, 1)
                    for ch in range(DC):
                        ln2_lo(2, ch)
                    ln2_rows(3)
                if step == 1:
                    for ch in range(DC):
                        ln2_lo(3, ch)
                for part, s in ROUTING.get(step, ()):
                    {"scores": route_scores, "best": route_best, "experts": route_experts, "pick": route_pick,
                     "place": route_place, "rows": route_rows}[part](s)

            dve.sem_inc(xb_turned, EX)
            dve.sem_inc(yb_ready, EX)
            dve.sem_inc(gath_free, GATHS)
            for i in range(EX):
                dve.sem_inc(yb_stored[i], 16)
            shared_units(BEFORE, GATE_UP, DOWNS_BEFORE, ffn_beside)

            dve.wait_ge(n2_stored[0], 32)
            dve.wait_ge(n2_stored[1], 32)
            def expert_mult(e, i):
                dve.wait_ge(e_silu, e + 1)
                nc.vector.tensor_tensor(hE[:, i % 2, :], e_gateup[i % 2][:, P:2 * P], sil_e[:, i % 2, :], ALU.mult
                                        ).then_inc(e_h, 1)

            def expert_out(e, i, uses):
                dve.wait_ge(e_down, e + 1)
                dve.wait_ge(yb_stored[i % EX], uses * 16 + 16)
                nc.vector.tensor_tensor(yb[:, i % EX, :], e_out[:], gb_bc[:], ALU.mult).then_inc(yb_ready, 1)

            for m, c in enumerate(MOE_CHUNKS):
                scale_chunk(c + 1)
                split_chunk_lo(c + 1)
                with dve.Fori(0, QB) as b:
                    first = b * EU + m * QB * EU
                    use = b * (EU // EX) + m * QB * (EU // EX)
                    n = b + c * QB
                    for i in range(EU):
                        expert_mult(first + i, i)
                        if i == 0:
                            shared_mult(n, 0, GATE_UP[0][1])
                        if i == 2:
                            shared_lo(n, 0)
                        if i >= 1:
                            expert_out(first + (i - 1), i - 1, use + (i - 1) // EX)
                        if i >= EU - TB + 1:
                            t = i - (EU - TB + 1)
                            shared_out(n, b * TB + t, t, DOWNS)
                    shared_out(n, b * TB + (TB - 1), TB - 1, DOWNS)
                    expert_out(first + (EU - 1), EU - 1, use + (EU - 1) // EX)

            def combine_beside(step):
                if step not in COMBINE:
                    return
                pair = (2 * COMBINE[step], 2 * COMBINE[step] + 1)
                dve.wait_ge(down_out, TB * (UNIT_AFTER + step))
                for k in range(TOPK):
                    for t in pair:
                        if k == 0:
                            dve.wait_ge(g_landed[t % GATHS], (t // GATHS + 1) * 16 * TOPK)
                        else:
                            dve.wait_ge(dve_step, steps[0] - 1)
                        ins = nc.vector.scalar_tensor_tensor(acc[:, t, :], gath[t % GATHS][:, k, :],
                                                             w_top[:, t, k:k + 1], acc[:, t, :], ALU.mult, ALU.add)
                        steps[0] += 1
                        ins.then_inc(dve_step, 1)
                dve.wait_ge(dve_step, steps[0])
                dve.sem_inc(combined, 2)
                dve.sem_inc(gath_free, 2)

            shared_units(AFTER, GATE_UP_AFTER, DOWNS_AFTER, combine_beside)

        @block.tensor
        def _(pe):
            def matmul3(o, a_hi, a_lo, b_hi, b_lo, start, stop):
                nc.tensor.matmul(o, a_hi, b_hi, start=start, stop=False)
                nc.tensor.matmul(o, a_hi, b_lo, start=False, stop=False)
                return nc.tensor.matmul(o, a_lo, b_hi, start=False, stop=stop)

            def mod_rows(o, part):
                for ch in range(DC):
                    last = nc.tensor.matmul(o[:], sc_bc[:, ch, :], wmod_sb[:, ch, part * D:part * D + D],
                                            start=ch == 0, stop=ch == DC - 1)
                last.then_inc(mod_mm, 1)

            def ln_turn(b):
                for ch in range(DC):
                    if b >= 1:
                        pe.wait_ge(ln_mod, DC * (b - 1) + ch + 1)
                    for t in range(TB):
                        if ch == 0:
                            pe.wait_ge(ln_norm, TB * b + t + 1)
                        last = nc.tensor.transpose(strip[ch][:, P * t:P * t + P], n1[:, b % 2, t, P * ch:P * ch + P],
                                                   ident[:])
                    last.then_inc(ln_turned, 1)

            def project(n, kind, j, h):
                pe.wait_ge(gen_out, nth(kind, j, 0, h))
                o = bank_of(kind, j, 0)
                if kind == "q":
                    pe.wait_ge(ln_split, DC * (j + 1))
                if j == 0:
                    pe.wait_ge(w_split, h * 4 + (n + 5))
                for ch in range(DC):
                    cols = slice(512 * j, 512 * j + 512)
                    last = matmul3(o[:], w_hi_t[n][:, ch, :], w_lo_t[n][:, ch, :],
                                   hT_hi[:, ch, cols], hT_lo[:, ch, cols], ch == 0, ch == DC - 1)
                last.then_inc(gen_done, 1)

            def out_project(t, o):
                last = matmul3(o[:], at_hi[:, P * t:P * t + P], at_lo[:, P * t:P * t + P],
                               w_hi_t[3][:].rearrange("p c d -> p (c d)"), w_lo_t[3][:].rearrange("p c d -> p (c d)"),
                               True, True)
                last.then_inc(gen_done, 1)

            def outs_of(j, t, h):
                if t == 0:
                    pe.wait_ge(attn_split, h * QB + (1 if j == QB - 1 else j + 2))
                    if j < QB - 1:
                        pe.wait_ge(w_split, h * 4 + 4)
                pe.wait_ge(gen_out, nth("o", j, t, h))
                out_project(t, bank_of("o", j, t))

            def turn_values(j, h):
                pe.wait_ge(gen_out, nth("t", j, 0, h))
                pe.wait_ge(gen_out, nth("v", j, 0, h - 1 if j == 0 else h) + GENS)
                o = bank_of("t", j, 0)
                for t in range(TB):
                    last = nc.tensor.transpose(o[:, P * t:P * t + P], vT_f[:, P * t:P * t + P], ident[:])
                last.then_inc(gen_done, 1)

            def score(j, h):
                pe.wait_ge(gen_out, nth("k", j, 0, h - 1 if j == 0 else h) + GENS)
                for n, (t, ch, w) in enumerate(score_units(j)):
                    u = strips_before(j) + n
                    pe.wait_ge(strip_out, h * NSTRIP + (u + 1))
                    o = strip[u % STRIPS]
                    rows, cols = slice(P * t, P * t + P), slice(512 * ch, 512 * ch + w)
                    last = matmul3(o[:, 0:w], qT_hi[:, rows], qT_lo[:, rows], kT_hi[:, cols], kT_lo[:, cols],
                                   True, True)
                    if ch == j:
                        last = nc.tensor.matmul(o[:, w - P:w], ident_bf[:], mask_bf[:], start=False, stop=True,
                                                skip_group_check=True)
                    last.then_inc(strip_done, 1)

            def turn_and_sum(j, h, last):
                n = units(j)
                pe.wait_ge(row_probs, h * NT + TB * (j + 1))

                def turn(kk):
                    u = strips_before(j) + n + kk
                    pe.wait_ge(strip_out, h * NSTRIP + (u + 1))
                    for t in range(first_col(j, kk) // P, TB):
                        at = row_at[t] + P * kk
                        last = nc.tensor.transpose(strip[u % STRIPS][:, P * t:P * t + P], probs[:, at:at + P], ident[:])
                    last.then_inc(strip_done, 1)

                def sum_values(kk):
                    u = strips_before(j) + n + kk
                    pe.wait_ge(strip_out, h * NSTRIP + (STRIPS + u + 1))
                    if kk == 0 or kk == TB * j:
                        pe.wait_ge(gen_out, nth("t", kk // TB, 0, h) + GENS)
                    c0 = first_col(j, kk)
                    last = matmul3(pv[:, c0:512], v_hi[:, kk, :], v_lo[:, kk, :], pT_hi[:, kk % PTS, c0:512],
                                   pT_lo[:, kk % PTS, c0:512], kk == 0, kk == n - 1)
                    last.then_inc(pv_done, 1)

                for kk in range(n + AHEAD):
                    if kk < n:
                        turn(kk)
                    if kk >= AHEAD:
                        if kk - AHEAD < TB:
                            outs_of((j - 1) % QB, kk - AHEAD, h)
                        sum_values(kk - AHEAD)
                    if last and (j, kk) in LN2_CHUNKS:
                        ln2_turn(*LN2_CHUNKS[j, kk], nth("o", j - 1, TB - 1, h) + GENS)

            def ln2_turn(b, ch, bank_free=None):
                n = NT + DC * b + ch
                if ch == 0:
                    pe.wait_ge(ln_norm, NT + TB * b + TB)
                if bank_free is not None and ch < 2:
                    pe.wait_ge(gen_out, bank_free)
                if ch >= 2 or b == 3:
                    pe.wait_ge(ln_mod, n - 1)
                for t in range(TB):
                    last = nc.tensor.transpose(ln2_bank(b, ch)[:, P * t:P * t + P], n2[:, b % 2, t, P * ch:P * ch + P],
                                               ident[:])
                last.then_inc(ln_turned, 1)

            def head(h, last):
                for j in range(QB):
                    if last and j == QB - 1:
                        pe.wait_ge(ln_mod, NT + DC)
                    turn_values(j, h)
                    score(j, h)
                    if j < QB - 1 or not last:
                        for n, kind in enumerate("qkv"):
                            project(n, kind, (j + 1) % QB, h)
                    turn_and_sum(j, h, last)

            pe.wait_ge(consts, 4)
            pe.wait_ge(rows_landed, 48)
            nc.tensor.transpose(pv[:, 0:3 * H], bias_rows[:], ident[0:3 * H, 0:3 * H]).then_inc(mod_mm, 1)
            pe.wait_ge(c_step, 5)
            pe.wait_ge(mod_landed[0], 16)
            mod_rows(gen[0], 0)
            mod_rows(gen[1], 1)
            ln_turn(0)
            ln_turn(1)
            project(0, "q", 0, -1)
            pe.wait_ge(mod_landed[1], 16)
            mod_rows(strip[4], 2)
            ln_turn(2)
            project(1, "k", 0, -1)
            pe.wait_ge(mod_landed[2], 16)
            pe.wait_ge(mod_out, 1)
            mod_rows(pv, 0)
            pe.wait_ge(mod_out, 3)
            mod_rows(strip[4], 1)
            ln_turn(3)
            project(2, "v", 0, -1)
            pe.wait_ge(mod_landed[3], 16)
            pe.wait_ge(mod_out, 4)
            mod_rows(pv, 2)
            with pe.Fori(0, H - 1) as h:
                head(h, False)
            head(H - 1, True)
            pe.wait_ge(strip_out, NSTRIP * H + STRIPS)
            pe.wait_ge(attn_split, QB * H + 1)
            pe.wait_ge(ln_mod, NT + 2 * DC)
            for t in range(TB):
                pe.wait_ge(gen_out, OUTS_END + t + 1)
                out_project(t, gen[t % GENS])

            half = NT // 2

            def logits(b):
                if b == 0:
                    pe.wait_ge(wr_split, 1)
                if b >= 2:
                    pe.wait_ge(logitsT_out, b - 1)
                pe.wait_ge(ln_split, NT + DC * (b + 1))
                cols = slice(512 * b, 512 * b + 512)
                for ch in range(DC):
                    last = matmul3(r_logitsT[b % 2][0:E, :], wr_hi[:, ch, :], wr_lo[:, ch, :],
                                   h2T_hi[:, ch, cols], h2T_lo[:, ch, cols], ch == 0, ch == DC - 1)
                last.then_inc(logitsT_mm, 1)

            def turn_logits(b):
                if b == 0:
                    pe.wait_ge(ln_mod, 2 * NT)
                pe.wait_ge(logitsT_out, b + 1)
                for t in range(TB):
                    at = E * (TB * (b % 2) + t)
                    last = nc.tensor.transpose(strip[b // 2][:, at:at + E], logitsT[:, b % 2, P * t:P * t + P],
                                               ident[0:E, 0:E])
                last.then_inc(logits_mm, 1)

            def places(s):
                pe.wait_ge(picked_ready, s + 1)
                mine = slice(half * s, half * s + half)
                last = nc.tensor.matmul(strip[s][:], tri_bf[:], picked[:, mine, :].rearrange("p t e -> p (t e)"),
                                        start=True, stop=True)
                for j in range(half * s + half - 1):
                    first = max(j + 1, half * s)
                    n = half * s + half - first
                    last = nc.tensor.matmul(strip[s][:, E * (first - half * s):512]
                                            .rearrange("p (t e) -> p t e", e=E), ones_bf[:],
                                            picked[:, j:j + 1, :].to_broadcast([P, n, E]), start=False,
                                            stop=True, skip_group_check=True)
                last.then_inc(pos_mm, 1)

            def gate_or_up(o, part, c, b):
                cols = bass.ds(b * 512, 512)
                for ch in range(DC):
                    w = slice(P * ch, P * ch + P)
                    last = matmul3(o[:], s_hi[c % 2][:, part, w], s_lo[c % 2][:, part, w],
                                   h2T_hi[:, ch, cols], h2T_lo[:, ch, cols], ch == 0, ch == DC - 1)
                return last

            def shared_down(n, c, t, buf, downs):
                if t == 0:
                    pe.wait_ge(hs_split, n + 1)
                tok = slice(P * t, P * t + P)
                matmul3(downs[t % len(downs)][:], hs_hi[:, buf, tok], hs_lo[:, buf, tok], s_hi[c % 2][:, DOWN, :],
                        s_lo[c % 2][:, DOWN, :], True, True).then_inc(down_done, 1)

            def shared_units(pairs, gate_up, downs, beside):
                first = pairs[0][0] * QB

                def down(n, c, t):
                    banks = downs if n >= QB else DOWNS
                    uses = n * TB + t
                    if uses >= len(DOWNS):
                        lag = len(banks) if n > max(first, QB) else len(DOWNS)
                        pe.wait_ge(down_out, uses - lag + 1)
                    shared_down(n, c, t, n % 2, banks)

                for step, (c, b) in enumerate(pairs + [(None, None)]):
                    if c is not None:
                        n = c * QB + b
                        gate, up = gate_up[n % len(gate_up)]
                        if b == 0:
                            pe.wait_ge(sw_split, c + 1)
                        if c == 0:
                            pe.wait_ge(ln_split, NT + DC * (b + 1))
                        if n >= len(gate_up):
                            pe.wait_ge(silu_done, n - len(gate_up) + 1)
                        gate_or_up(gate, GATE, c, b).then_inc(gate_done, 1)
                    if step >= 1:
                        last_c, last_b = pairs[step - 1]
                        for t in range(2):
                            down(last_c * QB + last_b, last_c, t)
                    if c is not None:
                        if n >= len(gate_up):
                            pe.wait_ge(hs_whole, n - len(gate_up) + 1)
                        gate_or_up(up, UP, c, b).then_inc(up_done, 1)
                    if step >= 1:
                        for t in range(2, TB):
                            down(last_c * QB + last_b, last_c, t)
                    beside(step)

            def router_beside(step):
                if step in (0, 1):
                    for ch in range(DC):
                        ln2_turn(2 + step, ch)
                if step == 1:
                    logits(0)
                    logits(1)
                if step == 2:
                    turn_logits(0)
                    turn_logits(1)
                    logits(2)
                    logits(3)
                if step == 3:
                    turn_logits(2)
                    turn_logits(3)
                if step in PLACES:
                    places(PLACES[step])

            pe.wait_ge(gen_out, GENS + OUTS_END + TB)
            shared_units(BEFORE, GATE_UP, DOWNS_BEFORE, router_beside)

            def expert_turn(e, i, uses):
                pe.wait_ge(xb_landed[i % EX], uses * 16 + 16)
                pe.wait_ge(xbT_ready, e + 1)
                for ch in range(DC):
                    last = nc.tensor.transpose(e_turn[:, P * ch:P * ch + P], xb[:, i % EX, P * ch:P * ch + P], ident[:])
                last.then_inc(xb_turned, 1)

            def expert_gate_up(e, i, uses):
                pe.wait_ge(xbT_ready, e + 2)
                pe.wait_ge(e_landed[i % EX], uses * 48 + 48)
                for n, w in enumerate((wg_sb, wu_sb)):
                    for c in range(DC):
                        last = nc.tensor.matmul(e_gateup[i % 2][:, P * n:P * n + P], w[:, i % EX, c, :],
                                                xbT[:, i % 2, P * c:P * c + P], start=c == 0, stop=c == DC - 1)
                last.then_inc(e_gu, 1)

            def expert_down(e, i):
                pe.wait_ge(e_h, e + 1)
                pe.wait_ge(yb_ready, e + EX)
                nc.tensor.matmul(e_out[:], hE[:, i % 2, :], wd_sb[:, i % EX, :], start=True, stop=True
                                 ).then_inc(e_down, 1)

            pe.wait_ge(routed, 2)
            pe.wait_ge(down_out, TB * QB * MOE_CHUNKS[0] - 1)
            for m, c in enumerate(MOE_CHUNKS):
                pe.wait_ge(sw_split, c + 1)
                with pe.Fori(0, QB) as b:
                    first = b * EU + m * QB * EU
                    use = b * (EU // EX) + m * QB * (EU // EX)
                    n = b + c * QB
                    expert_turn(first, 0, use)
                    pe.wait_ge(silu_done, n)
                    gate_or_up(GATE_UP[0][0], GATE, c, b).then_inc(gate_done, 1)
                    for i in range(EU):
                        if i + 1 < EU:
                            expert_turn(first + (i + 1), i + 1, use + (i + 1) // EX)
                        expert_gate_up(first + i, i, use + i // EX)
                        if i == 0:
                            pe.wait_ge(hs_whole, n)
                            gate_or_up(GATE_UP[0][1], UP, c, b).then_inc(up_done, 1)
                        if i >= 1:
                            expert_down(first + (i - 1), i - 1)
                        if i >= EU - TB:
                            t = i - (EU - TB)
                            pe.wait_ge(down_out, n * TB + (t + 1 - len(DOWNS)))
                            shared_down(n, c, t, 0, DOWNS)
                    expert_down(first + (EU - 1), EU - 1)
            pe.wait_ge(yb_ready, EX + E)
            shared_units(AFTER, GATE_UP_AFTER, DOWNS_AFTER, lambda step: None)


_INS = ["L0_attn_x", "L0_attn_Q_w", "L0_attn_Q_b", "L0_attn_K_w", "L0_attn_K_b", "L0_attn_V_w", "L0_attn_V_b",
        "L0_attn_O_w", "L0_attn_O_b", "L0_ffn_Wr", "L0_ffn_router_bias", "L0_ffn_Wg", "L0_ffn_Wu", "L0_ffn_Wd",
        "L0_ffn_Sg", "L0_ffn_Su", "L0_ffn_Sd", "L0_c", "L0_wmod"]


def kernel(**inputs):
    import concourse.bacc as bacc
    from concourse.bass_utils import run_bass_kernel_spmd

    nc = bacc.Bacc("TRN2", target_bir_lowering=False, num_devices=1)
    arrays, args = {}, []
    for name in _INS:
        arr = np.ascontiguousarray(inputs[name])
        arrays[f"in_{name}"] = arr
        args.append(nc.dram_tensor(f"in_{name}", arr.shape, mybir.dt.from_np(arr.dtype), kind="ExternalInput").ap())
    shape = inputs["L0_attn_x"].shape
    args.append(nc.dram_tensor("out_y", shape, F32, kind="ExternalOutput").ap())
    adaln_block(nc, *args)
    r = run_bass_kernel_spmd(nc, [arrays], core_ids=[0])
    return r.results[0]["out_y"]
```
